# Optimizing a Trainium2 kernel written in Bass

```python
import numpy as np
import jax
import jax.numpy as jnp

def _softmax(x, axis=-1):
    return jax.nn.softmax(x, axis=axis)

def _gelu(x):
    return jax.nn.gelu(x, approximate=True)

def _silu(x):
    return jax.nn.silu(x)

def _sigmoid(x):
    return jax.nn.sigmoid(x)

def _layernorm(x, axis=-1, eps=1e-05):
    m = jnp.mean(x, axis=axis, keepdims=True)
    v = jnp.var(x, axis=axis, keepdims=True)
    return (x - m) / jnp.sqrt(v + eps)

def _scatter_add(tgt, idx, src, axis=0):
    return tgt.at[idx].add(src)

def _segment_sum(src, seg, n):
    return jax.ops.segment_sum(src, seg, n)
kernel_name = 'mk_gps_d1_gnn_r32_751fc2'

def setup_inputs(seed: int=0):
    np.random.seed(seed)
    _w = jnp.asarray

    def _rec_inputs():
        import jax
        import jax.numpy as jnp
        _gk = jax.random.key(seed)
        x = -0.0002117 + 1 * jax.random.normal(jax.random.fold_in(_gk, 1), (3125, 256), jnp.float32)
        src = jax.random.randint(jax.random.fold_in(_gk, 2), (50000,), 0, 3125, jnp.int32)
        dst = jax.random.randint(jax.random.fold_in(_gk, 3), (50000,), 0, 3125, jnp.int32)
        _o = jnp.argsort(dst, stable=True)
        src = src[_o]
        dst = dst[_o]
        edge_weight = jax.random.uniform(jax.random.fold_in(_gk, 12), (50000,), jnp.float32, 0.0, 1)
        return (x, src, dst, edge_weight)
    x, src, dst, edge_weight = _rec_inputs()

    def _L0_gnn_setup():
        import jax, jax.numpy as jnp
        import numpy as np
        N = 3125
        E = 100000
        IN = 256
        OUT = 256
        BN_EPS = 1e-05

        def _hamilton(w):
            r, i, j, k = jnp.split(w, 4, axis=1)
            h0 = jnp.concatenate([r, -i, -j, -k], axis=0)
            h1 = jnp.concatenate([i, r, -k, j], axis=0)
            h2 = jnp.concatenate([j, k, r, -i], axis=0)
            h3 = jnp.concatenate([k, -j, i, r], axis=0)
            return jnp.concatenate([h0, h1, h2, h3], axis=1)
        key = jax.random.key(seed)
        k0, k1, k2, k3, k4 = jax.random.split(key, 5)
        x = jax.random.normal(k0, (N, IN), dtype=jnp.float32)
        edge_row = jax.random.randint(k1, (E,), 0, N)
        edge_col = jax.random.randint(k2, (E,), 0, N)
        edge_weight = jax.random.uniform(k3, (E,), dtype=jnp.float32)
        stdv = float(np.sqrt(6.0 / (IN // 4 + OUT)))
        weight = jax.random.uniform(k4, (IN // 4, OUT), dtype=jnp.float32, minval=-stdv, maxval=stdv)
        gamma = jnp.ones((OUT,), dtype=jnp.float32)
        beta = jnp.zeros((OUT,), dtype=jnp.float32)
        return {'x': x, 'edge_row': edge_row, 'edge_col': edge_col, 'edge_weight': edge_weight, 'weight': weight, 'gamma': gamma, 'beta': beta}
    _L0_gnn_all = _L0_gnn_setup()
    _L0_gnn_in = {k: v for k, v in _L0_gnn_all.items() if k in ('weight', 'gamma', 'beta')}
    del _L0_gnn_all

    def _L0_mix_setup():
        import jax, jax.numpy as jnp
        import numpy as np
        B, N, C = (8, 256, 256)
        HEADS, DH, KR = (8, 32, 4)
        INNER = HEADS * DH
        FF = 4 * C
        EPS = 1e-05

        def layernorm(x, g, b):
            mu = jnp.mean(x, axis=-1, keepdims=True)
            var = jnp.mean((x - mu) ** 2, axis=-1, keepdims=True)
            return (x - mu) * jax.lax.rsqrt(var + EPS) * g + b
        key = jax.random.key(seed)
        ks = jax.random.split(key, 16)
        s = 0.02
        return {'x': jax.random.normal(ks[0], (B, N, C), jnp.float32), 'ln1_g': jnp.ones((C,), jnp.float32), 'ln1_b': jnp.zeros((C,), jnp.float32), 'Wx': jax.random.normal(ks[1], (C, INNER), jnp.float32) * s, 'bx': jnp.zeros((INNER,), jnp.float32), 'Wq': jax.random.normal(ks[2], (DH, KR), jnp.float32) * s, 'Wk': jax.random.normal(ks[3], (DH, KR), jnp.float32) * s, 'Wv': jax.random.normal(ks[4], (DH, DH), jnp.float32) * s, 'Wo': jax.random.normal(ks[5], (INNER, C), jnp.float32) * s, 'bo': jnp.zeros((C,), jnp.float32), 'ln2_g': jnp.ones((C,), jnp.float32), 'ln2_b': jnp.zeros((C,), jnp.float32), 'W1': jax.random.normal(ks[6], (C, FF), jnp.float32) * s, 'b1': jnp.zeros((FF,), jnp.float32), 'W2': jax.random.normal(ks[7], (FF, C), jnp.float32) * s, 'b2': jnp.zeros((C,), jnp.float32)}
    _L0_mix_all = _L0_mix_setup()
    _L0_mix_in = {k: v for k, v in _L0_mix_all.items() if k in ('ln1_g', 'ln1_b', 'Wx', 'bx', 'Wq', 'Wk', 'Wv', 'Wo', 'bo', 'ln2_g', 'ln2_b', 'W1', 'b1', 'W2', 'b2')}
    del _L0_mix_all

    def _L0_ffn_setup():
        import jax, jax.numpy as jnp
        import numpy as np
        B, N, D = (16, 128, 256)
        NUM_EXPERTS, TOP_K, HEADS = (4, 2, 4)
        N_EDGES = 32768
        LN_EPS = 1e-05

        def _layernorm(x, g, b):
            mu = x.mean(-1, keepdims=True)
            var = ((x - mu) ** 2).mean(-1, keepdims=True)
            return (x - mu) * jax.lax.rsqrt(var + LN_EPS) * g + b

        def _forward(x, edge_index, W_gat, att_src, att_dst, b_gat, ln_gamma, ln_beta, W1, b1, W2, b2):
            Bc, Nc, Dc = x.shape
            M = Bc * Nc
            x_flat = x.reshape(M, Dc)
            h = (x_flat @ W_gat).reshape(M, HEADS, NUM_EXPERTS)
            loops = jnp.arange(M, dtype=edge_index.dtype)
            src = jnp.concatenate([edge_index[0], loops])
            dst = jnp.concatenate([edge_index[1], loops])
            a_src = (h * att_src).sum(-1)
            a_dst = (h * att_dst).sum(-1)
            e = jax.nn.leaky_relu(a_src[src] + a_dst[dst], negative_slope=0.2)
            e_max = jax.ops.segment_max(e, dst, num_segments=M)
            ee = jnp.exp(e - e_max[dst])
            denom = jax.ops.segment_sum(ee, dst, num_segments=M)
            alpha = ee / (denom[dst] + 1e-16)
            msg = h[src] * alpha[:, :, None]
            agg = jax.ops.segment_sum(msg, dst, num_segments=M).reshape(M, HEADS * NUM_EXPERTS) + b_gat
            scores = _layernorm(agg, ln_gamma, ln_beta).reshape(M, HEADS, NUM_EXPERTS).mean(1)
            scores = scores.reshape(Bc, Nc, NUM_EXPERTS)
            topk_s, topk_i = jax.lax.top_k(scores, TOP_K)
            w = jax.nn.softmax(topk_s, axis=-1)
            out = jnp.zeros_like(x)
            for ei in range(NUM_EXPERTS):
                g = jnp.where(topk_i == ei, w, 0.0).sum(-1)
                hh = jax.nn.gelu(x @ W1[ei] + b1[ei], approximate=False)
                out = out + g[..., None] * (hh @ W2[ei] + b2[ei])
            return out
        key = jax.random.key(seed)
        ks = jax.random.split(key, 8)
        s = 0.05
        return {'x': jax.random.normal(ks[0], (B, N, D), jnp.float32), 'W_gat': jax.random.normal(ks[1], (D, HEADS * NUM_EXPERTS), jnp.float32) * s, 'att_src': jax.random.normal(ks[2], (HEADS, NUM_EXPERTS), jnp.float32) * s, 'att_dst': jax.random.normal(ks[3], (HEADS, NUM_EXPERTS), jnp.float32) * s, 'b_gat': jnp.zeros((HEADS * NUM_EXPERTS,), jnp.float32), 'ln_gamma': jnp.ones((HEADS * NUM_EXPERTS,), jnp.float32), 'ln_beta': jnp.zeros((HEADS * NUM_EXPERTS,), jnp.float32), 'W1': jax.random.normal(ks[4], (NUM_EXPERTS, D, 2 * D), jnp.float32) * s, 'b1': jnp.zeros((NUM_EXPERTS, 2 * D), jnp.float32), 'W2': jax.random.normal(ks[5], (NUM_EXPERTS, 2 * D, D), jnp.float32) * s, 'b2': jnp.zeros((NUM_EXPERTS, D), jnp.float32), 'edge_index': jax.random.randint(ks[6], (2, N_EDGES), 0, B * N, jnp.int32)}
    _L0_ffn_all = _L0_ffn_setup()
    _L0_ffn_in = {k: v for k, v in _L0_ffn_all.items() if k in ('W_gat', 'att_src', 'att_dst', 'b_gat', 'ln_gamma', 'ln_beta', 'W1', 'b1', 'W2', 'b2', 'edge_index')}
    del _L0_ffn_all
    return {'x': x, 'src': src, 'dst': dst, 'edge_weight': edge_weight, 'L0_gnn_weight': _L0_gnn_in['weight'], 'L0_gnn_gamma': _L0_gnn_in['gamma'], 'L0_gnn_beta': _L0_gnn_in['beta'], 'L0_mix_ln1_g': _L0_mix_in['ln1_g'], 'L0_mix_ln1_b': _L0_mix_in['ln1_b'], 'L0_mix_Wx': _L0_mix_in['Wx'], 'L0_mix_bx': _L0_mix_in['bx'], 'L0_mix_Wq': _L0_mix_in['Wq'], 'L0_mix_Wk': _L0_mix_in['Wk'], 'L0_mix_Wv': _L0_mix_in['Wv'], 'L0_mix_Wo': _L0_mix_in['Wo'], 'L0_mix_bo': _L0_mix_in['bo'], 'L0_mix_ln2_g': _L0_mix_in['ln2_g'], 'L0_mix_ln2_b': _L0_mix_in['ln2_b'], 'L0_mix_W1': _L0_mix_in['W1'], 'L0_mix_b1': _L0_mix_in['b1'], 'L0_mix_W2': _L0_mix_in['W2'], 'L0_mix_b2': _L0_mix_in['b2'], 'L0_ffn_W_gat': _L0_ffn_in['W_gat'], 'L0_ffn_att_src': _L0_ffn_in['att_src'], 'L0_ffn_att_dst': _L0_ffn_in['att_dst'], 'L0_ffn_b_gat': _L0_ffn_in['b_gat'], 'L0_ffn_ln_gamma': _L0_ffn_in['ln_gamma'], 'L0_ffn_ln_beta': _L0_ffn_in['ln_beta'], 'L0_ffn_W1': _L0_ffn_in['W1'], 'L0_ffn_b1': _L0_ffn_in['b1'], 'L0_ffn_W2': _L0_ffn_in['W2'], 'L0_ffn_b2': _L0_ffn_in['b2'], 'L0_ffn_edge_index': _L0_ffn_in['edge_index']}

def reference(x, src, dst, edge_weight, L0_gnn_weight, L0_gnn_gamma, L0_gnn_beta, L0_mix_ln1_g, L0_mix_ln1_b, L0_mix_Wx, L0_mix_bx, L0_mix_Wq, L0_mix_Wk, L0_mix_Wv, L0_mix_Wo, L0_mix_bo, L0_mix_ln2_g, L0_mix_ln2_b, L0_mix_W1, L0_mix_b1, L0_mix_W2, L0_mix_b2, L0_ffn_W_gat, L0_ffn_att_src, L0_ffn_att_dst, L0_ffn_b_gat, L0_ffn_ln_gamma, L0_ffn_ln_beta, L0_ffn_W1, L0_ffn_b1, L0_ffn_W2, L0_ffn_b2, L0_ffn_edge_index):
    import jax
    import jax.numpy as jnp

    def _L0_gnn_ref(x, edge_row, edge_col, edge_weight, weight, gamma, beta):
        import jax, jax.numpy as jnp
        import numpy as np
        N = 3125
        E = 100000
        IN = 256
        OUT = 256
        BN_EPS = 1e-05

        def _hamilton(w):
            r, i, j, k = jnp.split(w, 4, axis=1)
            h0 = jnp.concatenate([r, -i, -j, -k], axis=0)
            h1 = jnp.concatenate([i, r, -k, j], axis=0)
            h2 = jnp.concatenate([j, k, r, -i], axis=0)
            h3 = jnp.concatenate([k, -j, i, r], axis=0)
            return jnp.concatenate([h0, h1, h2, h3], axis=1)
        n = x.shape[0]
        support = x @ _hamilton(weight)
        msgs = edge_weight[:, None] * support[edge_col]
        agg = jax.ops.segment_sum(msgs, edge_row, num_segments=n)
        mean = jnp.mean(agg, axis=0)
        var = jnp.mean(jnp.square(agg - mean), axis=0)
        y = (agg - mean) * jax.lax.rsqrt(var + BN_EPS) * gamma + beta
        return jnp.tanh(y)

    def _L0_mix_ref(x, ln1_g, ln1_b, Wx, bx, Wq, Wk, Wv, Wo, bo, ln2_g, ln2_b, W1, b1, W2, b2):
        import jax, jax.numpy as jnp
        import numpy as np
        B, N, C = (8, 256, 256)
        HEADS, DH, KR = (8, 32, 4)
        INNER = HEADS * DH
        FF = 4 * C
        EPS = 1e-05

        def layernorm(x, g, b):
            mu = jnp.mean(x, axis=-1, keepdims=True)
            var = jnp.mean((x - mu) ** 2, axis=-1, keepdims=True)
            return (x - mu) * jax.lax.rsqrt(var + EPS) * g + b
        b, n, c = x.shape
        h = layernorm(x, ln1_g, ln1_b)
        xm = h @ Wx + bx
        xm = xm.reshape(b, n, HEADS, DH).transpose(0, 2, 1, 3)
        q = jax.nn.softmax(xm @ Wq, axis=-1)
        k = jax.nn.softmax(xm @ Wk, axis=-2)
        v = xm @ Wv
        kv = jnp.einsum('bhnr,bhnd->bhrd', k, v)
        qkv = jnp.einsum('bhnr,bhrd->bhnd', q, kv)
        attn = qkv.transpose(0, 2, 1, 3).reshape(b, n, INNER) @ Wo + bo
        fx = attn + x
        h2 = layernorm(fx, ln2_g, ln2_b)
        m = jax.nn.gelu(h2 @ W1 + b1, approximate=False) @ W2 + b2
        return m + fx

    def _L0_ffn_ref(x, W_gat, att_src, att_dst, b_gat, ln_gamma, ln_beta, W1, b1, W2, b2, edge_index):
        import jax, jax.numpy as jnp
        import numpy as np
        B, N, D = (16, 128, 256)
        NUM_EXPERTS, TOP_K, HEADS = (4, 2, 4)
        N_EDGES = 32768
        LN_EPS = 1e-05

        def _layernorm(x, g, b):
            mu = x.mean(-1, keepdims=True)
            var = ((x - mu) ** 2).mean(-1, keepdims=True)
            return (x - mu) * jax.lax.rsqrt(var + LN_EPS) * g + b

        def _forward(x, edge_index, W_gat, att_src, att_dst, b_gat, ln_gamma, ln_beta, W1, b1, W2, b2):
            Bc, Nc, Dc = x.shape
            M = Bc * Nc
            x_flat = x.reshape(M, Dc)
            h = (x_flat @ W_gat).reshape(M, HEADS, NUM_EXPERTS)
            loops = jnp.arange(M, dtype=edge_index.dtype)
            src = jnp.concatenate([edge_index[0], loops])
            dst = jnp.concatenate([edge_index[1], loops])
            a_src = (h * att_src).sum(-1)
            a_dst = (h * att_dst).sum(-1)
            e = jax.nn.leaky_relu(a_src[src] + a_dst[dst], negative_slope=0.2)
            e_max = jax.ops.segment_max(e, dst, num_segments=M)
            ee = jnp.exp(e - e_max[dst])
            denom = jax.ops.segment_sum(ee, dst, num_segments=M)
            alpha = ee / (denom[dst] + 1e-16)
            msg = h[src] * alpha[:, :, None]
            agg = jax.ops.segment_sum(msg, dst, num_segments=M).reshape(M, HEADS * NUM_EXPERTS) + b_gat
            scores = _layernorm(agg, ln_gamma, ln_beta).reshape(M, HEADS, NUM_EXPERTS).mean(1)
            scores = scores.reshape(Bc, Nc, NUM_EXPERTS)
            topk_s, topk_i = jax.lax.top_k(scores, TOP_K)
            w = jax.nn.softmax(topk_s, axis=-1)
            out = jnp.zeros_like(x)
            for ei in range(NUM_EXPERTS):
                g = jnp.where(topk_i == ei, w, 0.0).sum(-1)
                hh = jax.nn.gelu(x @ W1[ei] + b1[ei], approximate=False)
                out = out + g[..., None] * (hh @ W2[ei] + b2[ei])
            return out
        return _forward(x, edge_index, W_gat, att_src, att_dst, b_gat, ln_gamma, ln_beta, W1, b1, W2, b2)
    xn = _layernorm(x, axis=-1)
    x = x + _L0_gnn_ref(xn, src, dst, edge_weight, L0_gnn_weight, L0_gnn_gamma, L0_gnn_beta) + _L0_mix_ref(xn[None], L0_mix_ln1_g, L0_mix_ln1_b, L0_mix_Wx, L0_mix_bx, L0_mix_Wq, L0_mix_Wk, L0_mix_Wv, L0_mix_Wo, L0_mix_bo, L0_mix_ln2_g, L0_mix_ln2_b, L0_mix_W1, L0_mix_b1, L0_mix_W2, L0_mix_b2)[0]
    x = x + _L0_ffn_ref(_layernorm(x, axis=-1)[None], L0_ffn_W_gat, L0_ffn_att_src, L0_ffn_att_dst, L0_ffn_b_gat, L0_ffn_ln_gamma, L0_ffn_ln_beta, L0_ffn_W1, L0_ffn_b1, L0_ffn_W2, L0_ffn_b2, L0_ffn_edge_index)[0]
    return x

_drawn_inputs = setup_inputs


def setup_inputs(seed=0):
    import zlib

    import numpy as np

    out = dict(_drawn_inputs(seed))
    spreads = {'L0_gnn_gamma': (1.0, 0.6),
     'L0_gnn_beta': (0.0, 0.383),
     'L0_mix_ln1_g': (1.0, 0.6),
     'L0_mix_ln1_b': (0.0, 0.8),
     'L0_mix_bx': (0.0, 0.729),
     'L0_mix_bo': (0.0, 0.381),
     'L0_mix_ln2_g': (1.0, 0.6),
     'L0_mix_ln2_b': (0.0, 2.0),
     'L0_mix_b1': (0.0, 0.656),
     'L0_mix_b2': (0.0, 0.418),
     'L0_ffn_b_gat': (0.0, 0.1),
     'L0_ffn_ln_gamma': (1.0, 0.2),
     'L0_ffn_ln_beta': (0.0, 0.281),
     'L0_ffn_b1': (0.0, 0.869),
     'L0_ffn_b2': (0.0, 0.643)}
    factors = {'L0_mix_Wx': 8.0,
     'L0_mix_Wq': 8.0,
     'L0_mix_Wk': 8.0,
     'L0_mix_Wv': 6.391,
     'L0_mix_Wo': 7.219,
     'L0_ffn_att_dst': 27.184,
     'L0_ffn_att_src': 6.197}
    for name, (base, spread) in spreads.items():
        noise = np.random.default_rng([zlib.crc32(name.encode()), seed]).standard_normal(out[name].shape)
        drawn = base * np.exp(spread * noise) if base else spread * noise
        out[name] = jnp.asarray(drawn.astype(out[name].dtype))
    for name, factor in factors.items():
        out[name] = (out[name] * factor).astype(out[name].dtype)
    return out
```

```python
from contextlib import ExitStack

import concourse.bass as bass
from concourse import mybir
from concourse.alu_op_type import AluOpType as ALU

ACT = mybir.ActivationFunctionType
AX = mybir.AxisListType
F32, F16, I32, U32 = mybir.dt.float32, mybir.dt.float16, mybir.dt.int32, mybir.dt.uint32
ds = bass.ds

P = 128
N, D = 3125, 256
T = 25
LAST = N - (T - 1) * P
NP = T * P
KT = D // P
EPS = 1e-5
E1, C1 = 50000, 392
FULL1, REST1 = E1 // C1, E1 % C1
CH = 416
LC = 14
E2, C2 = 32768, 288
KEYS2 = 57
HEADS, DH, KR = 8, 32, 4
QN = HEADS * KR
QKVN = 2 * QN + D
FF = 1024
FM = FF // P
NE, FE = 4, 512
EM = FE // P
GH = 4
ROW2 = 2 * GH + GH * NE
SUMS = GH + GH * NE
GROUPS = T // 4
BIG = 1.0e30
ROUND = 12582912.0

LOADS = ["x", "src", "dst", "edge_weight", "L0_gnn_weight", "L0_gnn_gamma", "L0_gnn_beta", "L0_mix_ln1_g",
         "L0_mix_ln1_b", "L0_mix_Wx", "L0_mix_bx", "L0_mix_Wq", "L0_mix_Wk", "L0_mix_Wv", "L0_mix_Wo",
         "L0_mix_bo", "L0_mix_ln2_g", "L0_mix_ln2_b", "L0_mix_W1", "L0_mix_b1", "L0_mix_W2", "L0_mix_b2",
         "L0_ffn_W_gat", "L0_ffn_att_src", "L0_ffn_att_dst", "L0_ffn_b_gat", "L0_ffn_ln_gamma",
         "L0_ffn_ln_beta", "L0_ffn_W1", "L0_ffn_b1", "L0_ffn_W2", "L0_ffn_b2", "L0_ffn_edge_index"]


class Chain:

    def __init__(self, eng, sem):
        self.eng, self.sem, self.n = eng, sem, 0

    def __call__(self, ins):
        ins.then_inc(self.sem, 1)
        self.n = self.n + 1
        self.eng.wait_ge(self.sem, self.n)

    def loop(self, count, per, body):
        base = self.n
        with self.eng.Fori(0, count) as i:
            self.n = base + i * per
            body(i)
        self.n = base + count * per


def tiles_in_pairs(eng, work):
    with eng.Fori(0, T // 2) as i:
        work(2 * i, 0)
        work(2 * i + 1, 1)
    work(T - 1, 0)


def tiles_ahead(eng, ahead, work):
    ahead(0, 0)
    with eng.Fori(0, T // 2) as i:
        ahead(2 * i + 1, 1)
        work(2 * i, 0)
        ahead(2 * i + 2, 0)
        work(2 * i + 1, 1)
    work(T - 1, 0)


def groups_ahead(eng, ahead, work):
    ahead(0, 0, 4)

    def turn(g, b, tiles):
        work(g, b, tiles, lambda: ahead(g + 1, 1 - b, 4))
    with eng.Fori(0, 2) as i:
        turn(2 * i, 0, 4)
        turn(2 * i + 1, 1, 4)
    turn(4, 0, 4)
    work(5, 1, 4, lambda: ahead(6, 0, 1))
    work(6, 0, 1, lambda: None)


def build(nc, A, out):
    with ExitStack() as ctx:
        def sb(name, shape, dt=F32):
            return ctx.enter_context(nc.sbuf_tensor(name, shape, dt))

        def sem(name):
            return ctx.enter_context(nc.semaphore(name))

        X = sb("X", [P, T, D])
        XN = sb("XN", [P, T, D])
        RQ = sb("RQ", [P, KEYS2 * C2 // 2])
        RR = sb("RR", [P, 11232])
        RT = sb("RT", [P, 6400])

        def cut(region, start, *shape):
            size = 1
            for s in shape:
                size *= s
            v = region[:, start:start + size]
            if len(shape) == 2:
                return v.rearrange("p (a b) -> p a b", a=shape[0])
            if len(shape) == 3:
                return v.rearrange("p (a b c) -> p a b c", a=shape[0], b=shape[1])
            return v

        onehot = RQ[:, :].bitcast(F16)
        at = C1 * T // 2
        Wx = cut(RQ, at, KT, D); at += KT * D
        WxT = cut(RQ, at, KT, D); at += KT * D
        BD = cut(RQ, at, KT, QKVN); at += KT * QKVN
        bxb = cut(RQ, at, KT, P); at += KT * P
        SRC = cut(RQ, at, C1).bitcast(I32); at += C1
        DST = cut(RQ, at, C1).bitcast(I32); at += C1
        WT = cut(RQ, at, C1)
        QKV = cut(RQ, 0, T, QKVN)
        AG = cut(RQ, 0, T, D)
        X2T = cut(RQ, 0, KT, NP)
        M2 = cut(RQ, KT * NP, P)
        MADD = [cut(RQ, KT * NP + P * (1 + i), P) for i in range(2)]
        DG = cut(RQ, KT * NP + 3 * P, GH, P)
        HT = cut(RQ, KT * NP + 7 * P, T, ROW2)
        counts = RR[:, 0:KEYS2 * C2 // 2].bitcast(F16)
        SRC2I = cut(RR, 5000, C2).bitcast(I32)
        DST2I = cut(RR, 5300, C2).bitcast(I32)
        jrow = cut(RR, 5600, CH)
        W1s = cut(RR, 0, KT, FF)
        HID = [cut(RR, 2048 + 4096 * b, FM, 512) for b in range(2)]
        SQ = cut(RR, 0, T, D)
        G = cut(RR, 0, C2, ROW2)
        MF, MB, AD = (cut(RR, C2 * (ROW2 + GH * i), C2, GH) for i in range(3))
        FLG = cut(RR, C2 * (ROW2 + 3 * GH), 3, C2)
        nodes = cut(RR, 0, T, SUMS)
        nodes2 = cut(RR, 500, T, GH * NE)
        nodes3 = cut(RR, 900, T, GH * NE)
        EHID = [cut(RR, 2048 * (1 + b), EM, 512) for b in range(2)]
        tmp_s, part_s = RT[:, 0:5 * C1], RT[:, 5 * C1:10 * C1]
        tmp_2, part_2 = RT[:, 0:3 * C2], RT[:, 3 * C2:22 * C2]
        stat = cut(RT, 0, 3, D)
        ring_s = [cut(RT, 768 + D * b, D) for b in range(2)]
        lhs = [cut(RT, P * s, P) for s in range(4)]
        rhs = [cut(RT, 512 + C2 * s, C2) for s in range(4)]
        ROWS = [cut(RT, D * s, D) for s in range(16)]
        SW = [cut(RT, 4096 + P * r, P) for r in range(4)]
        H2T = [cut(RT, 1280 + 1024 * b, KT, 512) for b in range(2)]
        W2s = cut(RT, 3328, FM, D)
        ROWS2 = [cut(RT, 8 * ROW2 * h, 8 * ROW2) for h in range(2)]
        SC = cut(RT, 0, C2, SUMS)
        crows = cut(RT, C2 * SUMS, GH, P)
        EW2b = cut(RT, 0, 2, EM * D).rearrange("p e (k n) -> p e k n", k=EM)
        EW1 = XN[:, 0:16, :].rearrange("p t d -> p (t d)").rearrange("p (e k n) -> p e k n", e=NE, k=KT)
        EW2a = XN[:, 16:24, :].rearrange("p t d -> p (t d)").rearrange("p (e k n) -> p e k n", e=2, k=EM)

        iota = sb("iota", [P, 512], F16)
        iota_f = sb("iota_f", [P, P])
        flat_i = sb("flat_i", [P, C2], I32)
        rowid = sb("rowid", [P, 1])
        ident = sb("ident", [P, P])
        tri = sb("tri", [P, P])
        low = sb("low", [P, P])
        ones = sb("ones", [P, P])
        epsc = sb("epsc", [P, 1])
        hmask = sb("hmask", [QN, D])
        st6 = sb("st6", [P, T, 6])
        mv = sb("mv", [P, T, 2])
        rstd = sb("rstd", [P, T])
        mv2 = sb("mv2", [P, T, 2])
        rstd2 = sb("rstd2", [P, T])
        ring_n = [sb(f"ring_n{b}", [P, 2 * D]) for b in range(2)]
        ring_t = [sb(f"ring_t{b}", [P, 4, P]) for b in range(2)]
        g1, b1, g2, b2, bxc = (sb(n, [P, KT]) for n in ("g1", "b1", "g2", "b2", "bxc"))
        fb1 = sb("fb1", [P, FM])
        eb1 = sb("eb1", [P, NE, EM])
        rowv = sb("rowv", [P, 4, D])
        eb2 = sb("eb2", [P, NE, D])
        Wo, WH = sb("Wo", [P, KT, D]), sb("WH", [P, KT, D])
        Wc, bc = sb("Wc", [P, KT, QKVN]), sb("bc", [P, QKVN])
        Wg = sb("Wg", [P, KT, GH * NE])
        attn_w = sb("attn_w", [P, 5, GH * NE])
        REC = sb("REC", [P, CH + 16, 4])
        K0, K1, K2 = sb("K0", [P, CH]), sb("K1", [P, CH]), sb("K2", [P, CH])
        K16 = sb("K16", [P, C1], F16)
        KI = sb("KI", [P, C2], I32)
        POSI = sb("POSI", [P, CH], I32)
        VAL = sb("VAL", [P, C2])
        cnts = sb("cnts", [P, 6, 64])
        blk_i = sb("blk_i", [P, CH], I32)
        st_idx = [sb(f"st_idx{h}", [P, 8], I32) for h in range(2)]
        st_rec = [sb(f"st_rec{h}", [P, 8 * 4]) for h in range(2)]
        turnstile = sb("turnstile", [P, 1])
        DSTS = sb("DSTS", [P, C2])
        SRCSI = sb("SRCSI", [P, C2], I32)
        dedge = sb("dedge", [P, 2])
        endi = sb("endi", [P, T], I32)
        small = sb("small", [P, 256])
        gates = sb("gates", [P, T, NE])
        rank = sb("rank", [P, T, NE])
        gstat = sb("gstat", [P, T, 2])

        B = [ctx.enter_context(nc.psum_tensor(f"bank{i}", [P, 512], F32)) for i in range(8)]

        table1 = nc.dram_tensor("table1", [NP, D], F32, kind="Internal").ap()
        recs = nc.dram_tensor("recs", [P * CH, 4], F32, kind="Internal").ap()
        table2 = nc.dram_tensor("table2", [NP, ROW2], F32, kind="Internal").ap()
        sums2 = nc.dram_tensor("sums2", [P * C2, SUMS], F32, kind="Internal").ap()

        (consts, padded, padded2, x_in, edges1_in, edges2_in, recs_zeroed, bd_zeroed, weights_in, signs,
         vec_step, tile_stats, stats_ready, root_ready, cnt_ready, pre_ready, pos1_ready, wxt_ready, wxt_out, wc_ready,
         wc_out, hh_ready, xr_ready, tp_done, t_out, proj_done, proj_out, sup_ready, mlp_in, recs_back,
         kmax_in, kmax_out, exp_go, exp_done, kv_done, kv_out, qc_ready, qt_done, qt_out, at_done, at_out,
         n2_ready, tp2_done, t2_out, hp_done, hid_out, op_done, op_added, perm_ready, perm_used, perm_done,
         perm_read, sorted2_ready, edge_in, idx2_ready, ends_ready, chunks_ready, staged, sw_ready, seg_done,
         seg_added, bn_go, bn_done, act_bn, x1_ready, experts_in, n3_ready, tp3_done, t3_out, h_done, h_out,
         tab2_ready, tab2_out, g_copied, carry_go, carry_done, esc_go, esc_done, sums_ready, sums_out,
         nodes_in, gate_go, gate_done, moe_go, ep_done, ehid_out, eo_done, eo_added, out_done) = (
            sem(n) for n in (
                "consts padded padded2 x_in edges1_in edges2_in recs_zeroed bd_zeroed weights_in signs "
                "vec_step tile_stats stats_ready root_ready cnt_ready pre_ready pos1_ready wxt_ready wxt_out wc_ready "
                "wc_out hh_ready xr_ready tp_done t_out proj_done proj_out sup_ready mlp_in recs_back "
                "kmax_in kmax_out exp_go exp_done kv_done kv_out qc_ready qt_done qt_out at_done at_out "
                "n2_ready tp2_done t2_out hp_done hid_out op_done op_added perm_ready perm_used perm_done "
                "perm_read sorted2_ready edge_in idx2_ready ends_ready chunks_ready staged sw_ready seg_done "
                "seg_added bn_go bn_done act_bn x1_ready experts_in n3_ready tp3_done t3_out h_done h_out "
                "tab2_ready tab2_out g_copied carry_go carry_done esc_go esc_done sums_ready sums_out "
                "nodes_in gate_go gate_done moe_go ep_done ehid_out eo_done eo_added out_done").split())
        sup_out = [sem(f"sup_out{b}") for b in range(2)]
        slot = [sem(f"slot{i}") for i in range(16)]
        slot1 = [16 * (C1 // LC) if s < LC else 0 for s in range(16)]
        slot2 = [n + 16 * (CH // 16) for n in slot1]
        N_CONSTS = 10

        col = lambda v, k: v.rearrange("(k p) -> p k", k=k)
        weights = [(g1[:, :], col(A["L0_mix_ln1_g"], KT)), (b1[:, :], col(A["L0_mix_ln1_b"], KT)),
                   (g2[:, :], col(A["L0_mix_ln2_g"], KT)), (b2[:, :], col(A["L0_mix_ln2_b"], KT)),
                   (bxc[:, :], col(A["L0_mix_bx"], KT)), (fb1[:, :], col(A["L0_mix_b1"], FM)),
                   (Wx, A["L0_mix_Wx"].rearrange("(k p) n -> p k n", p=P)),
                   (Wo[:, :, :], A["L0_mix_Wo"].rearrange("(k p) n -> p k n", p=P)),
                   (Wg[:, :, :], A["L0_ffn_W_gat"].rearrange("(k p) n -> p k n", p=P))]
        weights += [(rowv[:, i, :], A[n].partition_broadcast(P))
                    for i, n in enumerate(("L0_mix_bo", "L0_mix_b2", "L0_gnn_gamma", "L0_gnn_beta"))]
        for e in range(NE):
            weights.append((eb2[:, e, :], A["L0_ffn_b2"][e, :].partition_broadcast(P)))
            weights.append((eb1[:, e, :], col(A["L0_ffn_b1"][e, :], EM)))
        weights += [(attn_w[:, i, :], A[n].rearrange("h e -> (h e)").partition_broadcast(P))
                    for i, n in enumerate(("L0_ffn_att_src", "L0_ffn_att_dst"))]
        weights += [(attn_w[:, 2 + i, :], A[n].partition_broadcast(P))
                    for i, n in enumerate(("L0_ffn_b_gat", "L0_ffn_ln_gamma", "L0_ffn_ln_beta"))]
        for h in range(HEADS):
            k, q = h // 4, DH * (h % 4)
            weights.append((BD[q:q + DH, k, KR * h:KR * h + KR], A["L0_mix_Wq"]))
            weights.append((BD[q:q + DH, k, QN + KR * h:QN + KR * h + KR], A["L0_mix_Wk"]))
            weights.append((BD[q:q + DH, k, 2 * QN + DH * h:2 * QN + DH * h + DH], A["L0_mix_Wv"]))
        PARTS = ((0, 1, 2, 3), (1, 0, 3, 2), (2, 3, 0, 1), (3, 2, 1, 0))
        MINUS = ((1, 0), (2, 0), (3, 0), (1, 3), (2, 1), (3, 2))
        for r in range(4):
            for c in range(4):
                weights.append((WH[64 * (r % 2):64 * (r % 2) + 64, r // 2, 64 * c:64 * c + 64],
                                A["L0_gnn_weight"][:, 64 * PARTS[r][c]:64 * PARTS[r][c] + 64]))

        block = ctx.enter_context(nc.Block())

        @block.sync
        def _(sp):
            for b in range(2):
                sp.sem_inc(sup_out[b], 16)
            sp.wait_ge(padded, 7)
            sp.dma_start(recs.rearrange("(p c) f -> p (c f)", p=P), RT[:, 0:CH * 4]).then_inc(recs_zeroed, 16)
            for name, tile in (("src", SRC), ("dst", DST), ("edge_weight", WT)):
                a = A[name]
                sp.dma_start(tile[0:FULL1, :], a[0:FULL1 * C1].rearrange("(p c) -> p c", c=C1)).then_inc(edges1_in, 16)
                sp.dma_start(tile[FULL1:FULL1 + 1, 0:REST1],
                             a[FULL1 * C1:E1].rearrange("(p c) -> p c", p=1)).then_inc(edges1_in, 16)
            x = A["x"]
            sp.dma_start(X[:, 0:T - 1, :], x[0:(T - 1) * P, :].rearrange("(t p) d -> p t d", p=P)).then_inc(x_in, 16)
            sp.dma_start(X[0:LAST, T - 1, :], x[(T - 1) * P:N, :]).then_inc(x_in, 16)
            sp.wait_ge(padded2, 2)
            p0, c0 = NP // C2, NP % C2
            head = C2 - c0
            full = (E2 - head) // C2
            rest = E2 - head - full * C2
            for r, tile in ((0, SRC2I), (1, DST2I)):
                e = A["L0_ffn_edge_index"][r:r + 1, :]
                sp.dma_start(tile[p0:p0 + 1, c0:C2], e[:, 0:head]).then_inc(edges2_in, 16)
                sp.dma_start(tile[p0 + 1:p0 + 1 + full, :],
                             e[:, head:head + full * C2].rearrange("a (p c) -> (a p) c", c=C2)).then_inc(edges2_in, 16)
                sp.dma_start(tile[p0 + 1 + full:p0 + 2 + full, 0:rest], e[:, E2 - rest:E2]).then_inc(edges2_in, 16)

            def store(t, b):
                sp.wait_ge(sup_ready, t + 1)
                sp.dma_start(table1[ds(t * P, P), :], ring_s[b]).then_inc(sup_out[b], 16)
            tiles_in_pairs(sp, store)
            sp.dma_start(W1s, A["L0_mix_W1"].rearrange("(k p) n -> p k n", p=P)).then_inc(mlp_in, 16)
            sp.dma_start(W2s, A["L0_mix_W2"].rearrange("(k p) n -> p k n", p=P)).then_inc(mlp_in, 16)
            for s in range(LC):
                sp.wait_ge(slot[s], slot1[s])
            sp.dma_start(REC[:, 0:CH, :], recs.rearrange("(p c) f -> p c f", p=P)).then_inc(recs_back, 16)
            sp.wait_ge(sorted2_ready, 1)
            sp.dma_start(dedge[1:P, 0:1], DSTS[0:P - 1, C2 - 1:C2]).then_inc(edge_in, 16)
            sp.dma_start(dedge[0:P - 1, 1:2], DSTS[1:P, 0:1]).then_inc(edge_in, 16)
            sp.wait_ge(x1_ready, 1)
            sp.dma_start(EW1, A["L0_ffn_W1"].rearrange("e (k p) n -> p e k n", p=P)).then_inc(experts_in, 16)
            sp.dma_start(EW2a, A["L0_ffn_W2"][0:2].rearrange("e (k p) n -> p e k n", p=P)).then_inc(experts_in, 16)
            sp.wait_ge(tab2_ready, 1)
            sp.dma_start(table2.rearrange("(t p) f -> p t f", p=P), HT).then_inc(tab2_out, 16)
            sp.wait_ge(sums_ready, 1)
            sp.dma_start(sums2.rearrange("(p c) f -> p c f", p=P), SC).then_inc(sums_out, 16)
            sp.wait_ge(sums_out, 16)
            sp.dma_start(EW2b, A["L0_ffn_W2"][2:4].rearrange("e (k p) n -> p e k n", p=P)).then_inc(experts_in, 16)
            for g in range(GROUPS):
                sp.wait_ge(eo_added, 2 + 16 * g + 16)
                sp.dma_start(out[g * 512:(g + 1) * 512, :].rearrange("(t p) d -> p t d", p=P),
                             X[:, 4 * g:4 * g + 4, :]).then_inc(out_done, 16)
            sp.wait_ge(eo_added, 2 + 16 * GROUPS + NE)
            sp.dma_start(out[(T - 1) * P:N, :], X[0:LAST, T - 1, :]).then_inc(out_done, 16)
            sp.wait_ge(out_done, 16 * (GROUPS + 1))

        @block.gpsimd
        def _(gp):
            gp.memset(RT[:, 0:CH * 4], 0.0).then_inc(padded, 1)
            gp.memset(SRC, 0).then_inc(padded, 1)
            gp.memset(DST, 0).then_inc(padded, 1)
            gp.memset(WT, 0.0).then_inc(padded, 1)
            gp.memset(X[:, T - 1, :], 0.0).then_inc(padded, 1)
            gp.memset(REC[:, :, :], 0.0).then_inc(padded, 1)
            gp.iota(flat_i[:, :], pattern=[[1, C2]], base=0, channel_multiplier=C2).then_inc(padded, 1)
            gp.iota(iota[:, :], pattern=[[1, 512]], base=0, channel_multiplier=0,
                    allow_small_or_imprecise_dtypes=True).then_inc(consts, 1)
            gp.iota(iota_f[:, :], pattern=[[1, P]], base=0, channel_multiplier=0,
                    allow_small_or_imprecise_dtypes=True).then_inc(consts, 1)
            gp.iota(rowid[:, :], pattern=[[0, 1]], base=0, channel_multiplier=1,
                    allow_small_or_imprecise_dtypes=True).then_inc(consts, 1)
            gp.iota(jrow, pattern=[[P, CH]], base=0, channel_multiplier=0,
                    allow_small_or_imprecise_dtypes=True).then_inc(consts, 1)
            gp.memset(ones[:, :], 1.0).then_inc(consts, 1)
            gp.memset(epsc[:, :], EPS).then_inc(consts, 1)
            gp.memset(dedge[:, :], -1.0).then_inc(consts, 1)
            gp.memset(BD, 0.0).then_inc(bd_zeroed, 1)
            gp.memset(hmask[:, :], 1.0).then_inc(consts, 1)
            gp.wait_ge(consts, 8)
            hm = hmask[:, :].rearrange("p (h d) -> p h d", h=HEADS)
            gp.affine_select(out=hm, in_=hm, compare_op=ALU.is_ge, fill=0.0, base=0,
                             pattern=[[-KR, HEADS], [0, DH]], channel_multiplier=1).then_inc(consts, 1)
            gp.wait_ge(consts, 9)
            gp.affine_select(out=hm, in_=hm, compare_op=ALU.is_ge, fill=0.0, base=KR - 1,
                             pattern=[[KR, HEADS], [0, DH]], channel_multiplier=-1).then_inc(consts, 1)

            def pass_through():
                gp.tensor_tensor(turnstile[:, :], rowid[:, :], rowid[:, :], ALU.add)

            gp.wait_ge(pos1_ready, 1)
            gp.wait_ge(recs_zeroed, 16)
            half = LC // 2
            flat_rec = REC[:, :, :].rearrange("p c f -> p (c f)")

            def scatter(i, first=False):
                for h in range(2):
                    if not first:
                        for s in range(half):
                            gp.wait_ge(slot[half * h + s], i * 16)
                    c = i * LC + half * h
                    gp.tensor_copy(st_idx[h][:, 0:half], POSI[:, ds(c, half)]).then_inc(staged, 1)
                    gp.tensor_copy(st_rec[h][:, 0:4 * half], flat_rec[:, ds(c * 4, 4 * half)]).then_inc(staged, 1)
                    gp.wait_ge(staged, i * 4 + 2 * h + 2)
                    pass_through()
                    for s in range(half):
                        gp.indirect_dma_start(
                            recs, bass.IndirectOffsetOnAxis(ap=st_idx[h][:, s:s + 1].bitcast(U32), axis=0),
                            st_rec[h][:, 4 * s:4 * s + 4], None).then_inc(slot[half * h + s], 16)
            scatter(0, first=True)
            with gp.Fori(1, C1 // LC) as i:
                scatter(i)
            n = 4 * (C1 // LC)

            def gather(i, h, rows, table, first, used):
                if used is not None:
                    gp.wait_ge(*used)
                gp.tensor_copy(st_idx[h][:, :], (POSI if table is table1 else SRCSI)[:, ds(i * 16 + 8 * h, 8)]).then_inc(staged, 1)
                gp.wait_ge(staged, i * 2 + first + h + 1)
                pass_through()
                for s in range(8):
                    gp.indirect_dma_start(
                        rows(h, s), None, table,
                        bass.IndirectOffsetOnAxis(ap=st_idx[h][:, s:s + 1].bitcast(U32), axis=0)
                    ).then_inc(slot[8 * h + s], 16)

            gp.wait_ge(chunks_ready, 1)
            for b in range(2):
                gp.wait_ge(sup_out[b], 16 + 16 * ((T + 1 - b) // 2))
            rows1 = lambda h, s: ROWS[8 * h + s]
            for h in range(2):
                gather(0, h, rows1, table1, n, None)
            with gp.Fori(1, CH // 16) as i:
                for h in range(2):
                    gather(i, h, rows1, table1, n, (seg_done, i * 16 + 8 * h - 8))
            n += 2 * (CH // 16)

            gp.wait_ge(tab2_out, 16)
            gp.wait_ge(idx2_ready, 1)
            rows2 = lambda h, s: ROWS2[h][:, ROW2 * s:ROW2 * s + ROW2]
            for h in range(2):
                gather(0, h, rows2, table2, n, None)
            with gp.Fori(1, C2 // 16) as i:
                for h in range(2):
                    gather(i, h, rows2, table2, n, (g_copied, i * 2 + h - 1))

            gp.wait_ge(sums_out, 16)
            gp.wait_ge(ends_ready, 1)
            for t in range(T):
                gp.indirect_dma_start(
                    nodes[:, t, :], None, sums2,
                    bass.IndirectOffsetOnAxis(ap=endi[:, t:t + 1].bitcast(U32), axis=0)).then_inc(nodes_in, 16)

        @block.scalar
        def _(act):
            act.sem_inc(t_out, 6)
            act.sem_inc(qt_out, 2)
            act.sem_inc(t2_out, 4)
            act.sem_inc(hid_out, 2)
            act.sem_inc(t3_out, 4)
            act.sem_inc(ehid_out, 2)
            act.wait_ge(bd_zeroed, 1)
            for dst, src in weights:
                act.dma_start(dst, src, allow_slow_non_contiguous=True).then_inc(weights_in, 16)

            def root(k, tile, var):
                act.wait_ge(stats_ready, k)
                act.activation(tile, var, ACT.Sqrt, bias=epsc[:, 0:1], scale=1.0).then_inc(root_ready, 1)
            act.wait_ge(consts, N_CONSTS)
            root(1, rstd[:, :], mv[:, :, 1])
            root(2, rstd2[:, :], mv2[:, :, 1])

            act.wait_ge(wxt_ready, 1)
            for k in range(KT):
                act.activation(WxT[:, k, :], B[k][:, 0:D], ACT.Copy).then_inc(wxt_out, 1)

            act.wait_ge(weights_in, 16 * len(weights))

            def place(t, b):
                act.wait_ge(tp_done, t + 1)
                act.activation(ring_n[b][:, 0:D], XN[:, t, :], ACT.Copy).then_inc(xr_ready, 1)

            def turned(t, b):
                act.wait_ge(tp_done, 2 + t + 1)
                act.wait_ge(proj_done, t + 1)
                act.activation(ring_t[b][:, 0:2, :].rearrange("p k n -> p (k n)"), B[b][:, 0:D], ACT.Copy).then_inc(t_out, 1)
                for k in range(KT):
                    act.activation(ring_t[b][:, 2 + k, :], B[b][:, D + P * k:D + P * k + P], ACT.Identity,
                                   bias=b1[:, k:k + 1], scale=g1[:, k:k + 1]).then_inc(t_out, 1)
            tiles_ahead(act, place, turned)

            act.wait_ge(exp_go, 1)
            act.activation(QKV[:, :, QN:2 * QN], QKV[:, :, QN:2 * QN], ACT.Exp).then_inc(exp_done, 1)
            act.wait_ge(exp_go, 2)
            act.activation(QKV[:, :, 0:QN], QKV[:, :, 0:QN], ACT.Exp).then_inc(exp_done, 1)

            act.wait_ge(exp_go, 3)

            def place_q(t, b):
                act.wait_ge(qt_done, t + 1)
                act.activation(ring_n[b][:, 0:QN], QKV[:, t, 0:QN], ACT.Copy).then_inc(qc_ready, 1)

            def turned_q(t, b):
                act.wait_ge(qt_done, 2 + t + 1)
                act.wait_ge(at_done, t + 1)
                act.activation(ring_t[b][0:QN, 0, :], B[b][0:QN, 0:P], ACT.Copy).then_inc(qt_out, 1)
            tiles_ahead(act, place_q, turned_q)

            root(3, rstd[:, :], mv[:, :, 1])

            def turned2(g, b, tiles):
                act.wait_ge(hp_done, 8 * g + 8)
                for j in range(tiles):
                    act.wait_ge(tp2_done, 2 + 4 * g + j + 1)
                    for k in range(KT):
                        act.activation(H2T[b][:, k, P * j:P * j + P], B[j % 2][:, P * k:P * k + P], ACT.Identity,
                                       bias=b2[:, k:k + 1], scale=g2[:, k:k + 1]).then_inc(t2_out, 1)

            def gelu(g, b, tiles, ahead):
                act.wait_ge(op_done, 4 * g + 4)
                for m in range(FM):
                    act.wait_ge(hp_done, 16 + FM * g + m + 1)
                    act.activation(HID[b][:, m, 0:P * tiles], B[2 + m % 2][:, 0:P * tiles], ACT.Gelu,
                                   bias=fb1[:, m:m + 1], scale=1.0).then_inc(hid_out, 1)
                ahead()
            groups_ahead(act, turned2, gelu)

            act.wait_ge(bn_go, 2)
            act.activation(SQ, AG, ACT.Square).then_inc(act_bn, 1)
            act.wait_ge(bn_done, 2)
            act.activation(stat[:, 1, :], B[5][:, 0:D], ACT.Sqrt, bias=epsc[:, 0:1], scale=1.0 / N).then_inc(act_bn, 1)
            act.wait_ge(bn_go, 3)
            act.activation(AG, AG, ACT.Tanh).then_inc(act_bn, 1)

            root(4, rstd[:, :], mv[:, :, 1])

            def turned3(t, b):
                act.wait_ge(tp3_done, 2 + t + 1)
                act.wait_ge(h_done, t + 1)
                act.activation(ring_t[b][:, 0:2, :].rearrange("p k n -> p (k n)"), B[b][:, 0:D], ACT.Copy).then_inc(t3_out, 1)
                act.activation(X2T[:, :, ds(t * P, P)], B[b][:, 0:D].rearrange("p (k n) -> p k n", k=KT), ACT.Copy).then_inc(t3_out, 1)
            tiles_in_pairs(act, turned3)

            act.wait_ge(esc_go, 1)
            act.activation(G[:, :, GH:2 * GH], MF, ACT.Exp).then_inc(esc_done, 1)
            root(5, gstat[:, :, 1], gstat[:, :, 1])
            act.wait_ge(gate_go, 1)
            act.activation(rank[:, :, :], gates[:, :, :], ACT.Exp).then_inc(gate_done, 1)

            def moe(g, tiles):
                for e in range(NE):
                    act.wait_ge(eo_done, (16 * g + 4 * e + 4) if tiles == 4 or e < 2 else 16 * g + 7 + e)
                    for m in range(EM):
                        act.wait_ge(ep_done, 2 + 16 * g + 4 * e + m + 1)
                        act.activation(EHID[e % 2][:, m, 0:P * tiles], B[2 + m % 2][:, 0:P * tiles], ACT.Gelu,
                                       bias=eb1[:, e, m:m + 1], scale=1.0).then_inc(ehid_out, 1)
            with act.Fori(0, GROUPS) as g:
                moe(g, 4)
            moe(GROUPS, 1)

        @block.tensor
        def _(pe):
            mm, tr = nc.tensor.matmul, nc.tensor.transpose
            pe.sem_inc(tp_done, 2)
            pe.sem_inc(proj_done, 2)
            pe.sem_inc(qt_done, 2)
            pe.sem_inc(at_done, 2)
            pe.sem_inc(tp2_done, 2)
            pe.sem_inc(hp_done, 16)
            pe.sem_inc(op_done, 8)
            pe.sem_inc(perm_used, 4)
            pe.sem_inc(tp3_done, 2)
            pe.sem_inc(h_done, 2)
            pe.sem_inc(ep_done, 2)
            pe.sem_inc(eo_done, 8)
            pe.wait_ge(consts, N_CONSTS)

            def prefix(k, keys):
                pe.wait_ge(cnt_ready, k)
                mm(B[7][:, 0:keys], tri[:, :], cnts[:, 0, 0:keys], start=True, stop=True)
                mm(B[7][:, 64:64 + keys], ones[:, :], cnts[:, 0, 0:keys], start=True, stop=True).then_inc(pre_ready, 1)
            prefix(1, T)

            pe.wait_ge(weights_in, 16 * len(weights))
            for k in range(KT):
                for m in range(KT):
                    last = tr(B[k][:, P * m:P * m + P], Wx[:, m, P * k:P * k + P], ident[:, :])
            last.then_inc(wxt_ready, 1)
            pe.wait_ge(wxt_out, 2)
            for m in range(KT):
                for k in range(KT):
                    mm(B[2 + m][:, 0:QKVN], WxT[:, k, P * m:P * m + P], BD[:, k, :], start=(k == 0), stop=(k == KT - 1))
            pe.wait_ge(signs, 1)
            for k in range(KT):
                last = mm(B[4][:, 0:QKVN], bxb[:, k, :], BD[:, k, :], start=(k == 0), stop=(k == KT - 1))
            last.then_inc(wc_ready, 1)
            pe.wait_ge(wc_out, 3)

            def turn(t, b):
                pe.wait_ge(hh_ready, t + 1)
                pe.wait_ge(xr_ready, t + 1)
                pe.wait_ge(t_out, 3 * t + 3)
                for k in range(4):
                    last = tr(B[b][:, P * k:P * k + P], ring_n[b][:, P * k:P * k + P], ident[:, :])
                last.then_inc(tp_done, 1)

            def project(t, b):
                pe.wait_ge(t_out, 6 + 3 * t + 3)
                pe.wait_ge(proj_out, t + 1)
                for k in range(KT):
                    mm(B[2 + b][:, 0:D], ring_t[b][:, k, :], WH[:, k, :], start=(k == 0), stop=(k == KT - 1))
                for k in range(KT):
                    last = mm(B[4 + b][:, 0:QKVN], ring_t[b][:, 2 + k, :], Wc[:, k, :], start=(k == 0), stop=(k == KT - 1))
                last.then_inc(proj_done, 1)
            tiles_ahead(pe, turn, project)

            pe.wait_ge(kmax_in, 1)
            tr(B[6][0:QN, 0:P], small[:, 0:QN], ident[:, :]).then_inc(kmax_out, 1)
            pe.wait_ge(kmax_in, 2)
            mm(B[7][:, 128:128 + QN], ones[0:QN, :], small[0:QN, 64:64 + QN], start=True, stop=True).then_inc(kmax_out, 1)
            pe.wait_ge(exp_done, 1)
            for t in range(T):
                n = P if t < T - 1 else LAST
                mm(B[6][0:QN, 0:D], QKV[0:n, t, QN:2 * QN], QKV[0:n, t, 2 * QN:QKVN], start=(t == 0), stop=(t == T - 1))
                last = mm(B[0][0:QN, 0:1], QKV[0:n, t, QN:2 * QN], ones[0:n, 0:1], start=(t == 0), stop=(t == T - 1))
            last.then_inc(kv_done, 1)
            pe.wait_ge(kv_out, 1)
            for k in range(KT):
                last = tr(B[4][:, QN * k:QN * k + QN], stat[0:QN, 0, P * k:P * k + P], ident[0:QN, 0:QN])
            last.then_inc(kv_done, 1)
            pe.wait_ge(kv_out, 2)
            for k in range(KT):
                last = mm(B[5][0:QN, 0:D], small[:, 96 + QN * k:96 + QN * k + QN], Wo[:, k, :], start=(k == 0), stop=(k == KT - 1))
            last.then_inc(kv_done, 1)
            pe.wait_ge(kv_out, 3)

            def turn_q(t, b):
                pe.wait_ge(qc_ready, t + 1)
                pe.wait_ge(qt_out, t + 1)
                tr(B[b][0:QN, 0:P], ring_n[b][:, 0:QN], ident[:, :]).then_inc(qt_done, 1)

            def attend(t, b):
                pe.wait_ge(qt_out, 2 + t + 1)
                pe.wait_ge(at_out, t + 1)
                mm(B[2 + b][:, 0:D], ring_t[b][0:QN, 0, :], stat[0:QN, 1, :], start=True, stop=True).then_inc(at_done, 1)
            tiles_ahead(pe, turn_q, attend)

            pe.wait_ge(mlp_in, 32)

            def turn2(g, b, tiles):
                for j in range(tiles):
                    pe.wait_ge(n2_ready, 4 * g + j + 1)
                    pe.wait_ge(t2_out, 8 * g + 2 * j + 2)
                    for k in range(KT):
                        last = tr(B[j % 2][:, P * k:P * k + P], ring_n[j % 2][:, P * k:P * k + P], ident[:, :])
                    last.then_inc(tp2_done, 1)

            def mlp(g, b, tiles, ahead):
                n = P * tiles
                pe.wait_ge(t2_out, 4 + 8 * g + 2 * tiles)
                for m in range(FM):
                    pe.wait_ge(hid_out, FM * g + m + 1)
                    for k in range(KT):
                        last = mm(B[2 + m % 2][:, 0:n], W1s[:, k, P * m:P * m + P], H2T[b][:, k, 0:n], start=(k == 0), stop=(k == KT - 1))
                    last.then_inc(hp_done, 1)
                ahead()
                pe.wait_ge(hid_out, 2 + FM * g + FM)
                for j in range(tiles):
                    pe.wait_ge(op_added, 4 * g + j + 1)
                    for k in range(FM):
                        last = mm(B[4 + j % 2][:, 0:D], HID[b][:, k, P * j:P * j + P], W2s[:, k, :], start=(k == 0), stop=(k == FM - 1))
                    last.then_inc(op_done, 1)
            groups_ahead(pe, turn2, mlp)

            def permute(k, width):
                def columns(c, first=False, final=False):
                    for s in range(4):
                        pe.wait_ge(perm_ready, c + (k * C2 + s + 1))
                        mm(B[6][:, 0:width], lhs[s], rhs[s][:, 0:width], start=(first and s == 0),
                           stop=(final and s == 3), skip_group_check=True).then_inc(perm_used, 1)
                columns(0, first=True)
                with pe.Fori(1, C2 // 4 - 1) as i:
                    columns(i * 4)
                columns(C2 - 4, final=True)
            prefix(2, KEYS2)
            permute(0, C2)
            prefix(3, KEYS2)
            permute(1, C2)
            pe.wait_ge(perm_read, 2)
            permute(2, T)

            with pe.Fori(0, CH // 16) as i:
                for s in range(16):
                    pe.wait_ge(sw_ready, i * 16 + s + 1)
                    pe.wait_ge(slot[s], i * 16 + slot1[s] + 16)
                    pe.wait_ge(seg_added, i * 16 + s + 1)
                    mm(B[s % 4][:, 0:D], SW[s % 4], ROWS[s], start=True, stop=True).then_inc(seg_done, 1)

            pe.wait_ge(bn_go, 1)
            for t in range(T):
                last = mm(B[4][:, 0:D], ones[:, :], AG[:, t, :], start=(t == 0), stop=(t == T - 1))
            last.then_inc(bn_done, 1)
            pe.wait_ge(act_bn, 1)
            for t in range(T):
                n = P if t < T - 1 else LAST
                last = mm(B[5][:, 0:D], ones[0:n, :], SQ[0:n, t, :], start=(t == 0), stop=(t == T - 1))
            last.then_inc(bn_done, 1)

            def turn3(t, b):
                pe.wait_ge(n3_ready, t + 1)
                pe.wait_ge(t3_out, 2 * t + 2)
                for k in range(KT):
                    last = tr(B[b][:, P * k:P * k + P], ring_n[b][:, P * k:P * k + P], ident[:, :])
                last.then_inc(tp3_done, 1)

            def project3(t, b):
                pe.wait_ge(t3_out, 4 + 2 * t + 2)
                pe.wait_ge(h_out, t + 1)
                for k in range(KT):
                    last = mm(B[2 + b][:, 0:GH * NE], ring_t[b][:, k, :], Wg[:, k, :], start=(k == 0), stop=(k == KT - 1))
                last.then_inc(h_done, 1)
            tiles_ahead(pe, turn3, project3)

            pe.wait_ge(carry_go, 1)
            mm(B[4][:, 0:2 * P], ones[:, :], DG[:, 0:2, :].rearrange("p a b -> p (a b)"), start=True, stop=True).then_inc(carry_done, 1)
            pe.wait_ge(carry_go, 2)
            mm(B[5][:, 0:GH], M2, small[:, 0:GH], start=True, stop=True).then_inc(carry_done, 1)
            for k in range(2):
                pe.wait_ge(carry_go, 3 + k)
                mm(B[6 + k][:, :], ones[:, :], DG.rearrange("p a b -> p (a b)"), start=True, stop=True).then_inc(carry_done, 1)
            pe.wait_ge(carry_go, 5)
            mm(B[5][:, 32:32 + SUMS], M2, small[:, 32:32 + SUMS], start=True, stop=True).then_inc(carry_done, 1)

            pe.wait_ge(experts_in, 48)
            pe.wait_ge(moe_go, 1)

            def first(g, e, tiles):
                n = P * tiles
                for m in range(EM):
                    pe.wait_ge(ehid_out, 16 * g + 4 * e + m + 1)
                    for k in range(KT):
                        last = mm(B[2 + m % 2][:, 0:n], EW1[:, e, k, P * m:P * m + P],
                                  X2T[:, k, ds(g * 512, n)], start=(k == 0), stop=(k == KT - 1))
                    last.then_inc(ep_done, 1)

            def second(g, e, tiles):
                w2 = EW2a[:, e, :, :] if e < 2 else EW2b[:, e - 2, :, :]
                pe.wait_ge(ehid_out, 2 + 16 * g + 4 * e + 4)
                for j in range(tiles):
                    o, b = (4 * e + j, j % 2) if tiles == 4 else (e, e % 2)
                    pe.wait_ge(eo_added, 16 * g + o + 1)
                    for k in range(EM):
                        last = mm(B[4 + b][:, 0:D], EHID[e % 2][:, k, P * j:P * j + P], w2[:, k, :],
                                  start=(k == 0), stop=(k == EM - 1))
                    last.then_inc(eo_done, 1)

            def moe(g, tiles):
                first(g, 0, tiles)
                for e in range(NE):
                    if e + 1 < NE:
                        first(g, e + 1, tiles)
                    second(g, e, tiles)
            with pe.Fori(0, GROUPS) as g:
                moe(g, 4)
            moe(GROUPS, 1)

        @block.vector
        def _(ve):
            v = Chain(ve, vec_step)
            ts, tt, stt, cp = ve.tensor_scalar, ve.tensor_tensor, ve.scalar_tensor_tensor, ve.tensor_copy
            red, scan = ve.tensor_reduce, ve.tensor_tensor_scan
            ve.sem_inc(proj_out, 2)
            ve.sem_inc(at_out, 2)
            ve.sem_inc(op_added, 2)
            ve.sem_inc(seg_added, 4)
            ve.sem_inc(h_out, 2)
            ve.sem_inc(eo_added, 2)

            ve.wait_ge(consts, 10)
            v(ts(ident[:, :], iota_f[:, :], rowid[:, 0:1], None, ALU.is_equal))
            v(ts(tri[:, :], iota_f[:, :], rowid[:, 0:1], None, ALU.is_gt))
            v(ts(low[:, :], iota_f[:, :], rowid[:, 0:1], None, ALU.is_lt))
            ve.wait_ge(padded, 7)
            ts(SRC2I, flat_i[:, :], NP - 1, None, ALU.min).then_inc(padded2, 1)
            ts(DST2I, flat_i[:, :], NP - 1, None, ALU.min).then_inc(padded2, 1)

            def floor_div(o, i, d):
                v(ts(o, i, 1.0 / d, 0.5 / d - 0.5, ALU.mult, ALU.add))
                v(ts(o, o, ROUND, ROUND, ALU.add, ALU.subtract))

            def positions(k, C, keys, group, tmp, part, pos, whole_chunks):
                def is_key(i):
                    v(ts(onehot[:, ds(i * C, C)], K16[:, 0:C], iota_f[:, ds(i, 1)], None, ALU.is_equal))
                v.loop(keys, 1, is_key)
                oh, cn = onehot[:, 0:keys * C], counts[:, 0:keys * C]
                v(scan(cn, oh, oh, 0.0, ALU.add, ALU.max))
                count, at_end, total, upto, start, shift = (cnts[:, i, 0:keys] for i in range(6))
                v(cp(at_end, cn.rearrange("p (k c) -> p k c", c=C)[:, :, C - 1]))
                v(cp(count[:, 0:1], at_end[:, 0:1]))
                tt(count[:, 1:keys], at_end[:, 1:keys], at_end[:, 0:keys - 1], ALU.subtract).then_inc(cnt_ready, 1)
                ve.wait_ge(pre_ready, k)
                v(cp(total, B[7][:, 64:64 + keys]))
                if whole_chunks:
                    v(ts(total, total, float(P - 1), None, ALU.add))
                    floor_div(total, total, P)
                    v(ts(total, total, float(P), None, ALU.mult))
                v(scan(upto, total, total, 0.0, ALU.add, ALU.max))
                v(tt(start, upto, total, ALU.subtract))
                v(tt(shift, start, B[7][:, 0:keys], ALU.add))
                v(tt(shift, shift, at_end, ALU.subtract))
                v(stt(shift, shift, -1.0, count, ALU.add, ALU.add))

                def some_keys(i):
                    for q in range(group):
                        key = i * group + q
                        v(stt(tmp[:, q * C:(q + 1) * C], counts[:, ds(key * C, C)], shift_of(key),
                              onehot[:, ds(key * C, C)], ALU.add, ALU.mult))
                    v(red(part[:, ds(i * C, C)], tmp[:, 0:group * C].rearrange("p (q c) -> p c q", c=C), AX.X, ALU.add))
                shift_of = lambda key: cnts[:, 5, ds(key, 1)]
                v.loop(keys // group, group + 1, some_keys)
                v(red(pos, part[:, 0:(keys // group) * C].rearrange("p (g c) -> p c g", c=C), AX.X, ALU.add))

            ve.wait_ge(edges1_in, 96)
            blk, lo = K0[:, 0:C1], K1[:, 0:C1]
            v(cp(lo, SRC))
            floor_div(blk, lo, P)
            v(cp(K16[:, :], blk))
            v(stt(REC[:, 0:C1, 1], blk, -float(P), lo, ALU.mult, ALU.add))
            v(cp(REC[:, 0:C1, 0], DST))
            v(cp(REC[:, 0:C1, 2], WT))
            ve.wait_ge(recs_zeroed, 16)
            pos = K2[:, 0:C1]
            positions(1, C1, T, 5, tmp_s, part_s, pos, True)
            chunk = K0[:, 0:C1]
            floor_div(chunk, pos, P)
            v(stt(K1[:, 0:C1], chunk, -float(P), pos, ALU.mult, ALU.add))
            stt(POSI[:, 0:C1], K1[:, 0:C1], float(CH), chunk, ALU.mult, ALU.add).then_inc(pos1_ready, 1)
            v(ts(K2[0:1, :], jrow[0:1, :], cnts[0:1, 3, 0:1], None, ALU.is_ge))

            def block_ends(i):
                v(stt(K2[0:1, :], jrow[0:1, :], cnts[0:1, 3, ds(i, 1)], K2[0:1, :], ALU.is_ge, ALU.add))
            base = v.n
            with ve.Fori(1, T) as i:
                v.n = base + i - 1
                block_ends(i)
            v.n = base + T - 1
            v(ts(blk_i[0:1, :], K2[0:1, :], float(T - 1), None, ALU.min))

            ve.wait_ge(edges2_in, 96)
            v(cp(VAL[:, :], DST2I))
            v(cp(K1[:, 0:C2], SRC2I))
            v(stt(VAL[:, :], VAL[:, :], 4096.0, K1[:, 0:C2], ALU.mult, ALU.add))

            def statistics(src, m, k):
                with ve.Fori(0, T) as t:
                    ve.bn_stats(st6[:, t, :], src[:, t, :]).then_inc(tile_stats, 1)
                ve.wait_ge(tile_stats, k * T)
                mean, var = m[:, :, 0], m[:, :, 1]
                v(tt(mean, st6[:, :, 1], st6[:, :, 4], ALU.add))
                v(tt(st6[:, :, 1], st6[:, :, 1], st6[:, :, 4], ALU.subtract))
                v(stt(st6[:, :, 1], st6[:, :, 1], D / 4, st6[:, :, 1], ALU.mult, ALU.mult))
                v(tt(var, st6[:, :, 2], st6[:, :, 5], ALU.add))
                v(tt(var, var, st6[:, :, 1], ALU.add))
                v(ts(var, var, 1.0 / D, None, ALU.mult))
                v(ts(mean, mean, 0.5, None, ALU.mult))
                ve.sem_inc(stats_ready, 1)

            def reciprocal(k, r):
                ve.wait_ge(root_ready, k)
                v(ve.reciprocal(r, r))
            ve.wait_ge(x_in, 32)
            statistics(X, mv, 1)
            reciprocal(1, rstd[:, :])

            def normalize(t):
                v(ts(XN[:, t, :], X[:, t, :], mv[:, t, 0:1], rstd[:, ds(t, 1)], ALU.subtract, ALU.mult))
            v.loop(T, 1, normalize)
            statistics(XN, mv2, 2)
            reciprocal(2, rstd2[:, :])

            ve.wait_ge(weights_in, 16 * len(weights))
            for r, c in MINUS:
                w = WH[64 * (r % 2):64 * (r % 2) + 64, r // 2, 64 * c:64 * c + 64]
                v(ts(w, w, -1.0, None, ALU.mult))
            for k in range(KT):
                v(ts(bxb[:, k, :], ones[:, :], bxc[:, k:k + 1], None, ALU.mult))
            ve.sem_inc(signs, 1)
            ve.wait_ge(wc_ready, 1)
            for m in range(KT):
                cp(Wc[:, m, :], B[2 + m][:, 0:QKVN]).then_inc(wc_out, 1)
            cp(bc[:, :], B[4][:, 0:QKVN]).then_inc(wc_out, 1)
            ve.wait_ge(wc_out, 3)

            def center(t, b):
                ve.wait_ge(tp_done, t + 1)
                ts(ring_n[b][:, D:2 * D], XN[:, t, :], mv2[:, t, 0:1], rstd2[:, ds(t, 1)],
                   ALU.subtract, ALU.mult).then_inc(hh_ready, 1)

            def projected(t, b):
                ve.wait_ge(proj_done, 2 + t + 1)
                ve.wait_ge(sup_out[b], (t - b) * 8 + 16)
                cp(ring_s[b], B[2 + b][:, 0:D]).then_inc(sup_ready, 1)
                tt(QKV[:, t, :], B[4 + b][:, 0:QKVN], bc[:, :], ALU.add).then_inc(proj_out, 1)
            tiles_ahead(ve, center, projected)
            ve.wait_ge(proj_out, 2 + T)
            for b in range(2):
                ve.wait_ge(sup_out[b], 16 + 16 * ((T + 1 - b) // 2))

            q, kk = QKV[:, :, 0:QN], QKV[:, :, QN:2 * QN]
            kmax, ktail = small[:, 0:QN], small[:, 32:32 + QN]
            v(red(kmax, kk[:, 0:T - 1, :].rearrange("p t c -> p c t"), AX.X, ALU.max))
            v(tt(kmax[0:LAST, :], kmax[0:LAST, :], kk[0:LAST, T - 1, :], ALU.max))
            ve.sem_inc(kmax_in, 1)
            ve.wait_ge(kmax_out, 1)
            v(red(small[0:QN, 128:129], B[6][0:QN, 0:P], AX.X, ALU.max))
            v(ts(small[0:QN, 64:64 + QN], ident[0:QN, 0:QN], small[0:QN, 128:129], None, ALU.mult))
            ve.sem_inc(kmax_in, 1)
            ve.wait_ge(kmax_out, 2)
            v(cp(small[:, 32:32 + QN], B[7][:, 128:128 + QN]))
            tt(kk, kk, small[:, 32:32 + QN].unsqueeze(1).to_broadcast([P, T, QN]), ALU.subtract).then_inc(exp_go, 1)
            q4 = q.rearrange("p t (h r) -> p t h r", r=KR)
            K0q = K0[:, 0:T * HEADS].rearrange("p (t h) -> p t h", t=T)
            v(red(K0q, q4, AX.X, ALU.max))
            tt(q4, q4, K0q.unsqueeze(3).to_broadcast([P, T, HEADS, KR]), ALU.subtract).then_inc(exp_go, 1)
            ve.wait_ge(exp_done, 2)
            v(red(K0q, q4, AX.X, ALU.add))
            v(ve.reciprocal(K0[:, 0:T * HEADS], K0[:, 0:T * HEADS]))
            tt(q4, q4, K0q.unsqueeze(3).to_broadcast([P, T, HEADS, KR]), ALU.mult).then_inc(exp_go, 1)
            ve.wait_ge(kv_done, 1)
            v(ve.reciprocal(small[0:QN, 128:129], B[0][0:QN, 0:1]))
            stt(stat[0:QN, 0, :], B[6][0:QN, 0:D], small[0:QN, 128:129], hmask[:, :], ALU.mult, ALU.mult).then_inc(kv_out, 1)
            ve.wait_ge(kv_done, 2)
            cp(small[:, 96:96 + 2 * QN], B[4][:, 0:2 * QN]).then_inc(kv_out, 1)
            ve.wait_ge(kv_done, 3)
            cp(stat[0:QN, 1, :], B[5][0:QN, 0:D]).then_inc(kv_out, 1)

            v(tt(XN[:, :, :], XN[:, :, :], rowv[:, 0, :].unsqueeze(1).to_broadcast([P, T, D]), ALU.add))

            def attended(t, b):
                ve.wait_ge(at_done, 2 + t + 1)
                tt(XN[:, t, :], XN[:, t, :], B[2 + b][:, 0:D], ALU.add).then_inc(at_out, 1)
            tiles_in_pairs(ve, attended)
            ve.wait_ge(at_out, 2 + T)
            statistics(XN, mv, 3)
            reciprocal(3, rstd[:, :])

            def center2(g, b, tiles):
                for j in range(tiles):
                    t = 4 * g + j
                    ve.wait_ge(tp2_done, t + 1)
                    ts(ring_n[j % 2][:, 0:D], XN[:, t, :], mv[:, t, 0:1], rstd[:, ds(t, 1)],
                       ALU.subtract, ALU.mult).then_inc(n2_ready, 1)

            def mlp_added(g, b, tiles, ahead):
                ahead()
                for j in range(tiles):
                    t = 4 * g + j
                    ve.wait_ge(op_done, 8 + t + 1)
                    tt(X[:, t, :], X[:, t, :], B[4 + j % 2][:, 0:D], ALU.add).then_inc(op_added, 1)
            groups_ahead(ve, center2, mlp_added)
            ve.wait_ge(op_added, 2 + T)
            v(tt(X[:, :, :], X[:, :, :], XN[:, :, :], ALU.add))
            v(tt(X[:, :, :], X[:, :, :], rowv[:, 1, :].unsqueeze(1).to_broadcast([P, T, D]), ALU.add))
            ve.sem_inc(x1_ready, 1)

            def permute(k, pd, cd, width, val):
                def columns(c):
                    for s in range(4):
                        ve.wait_ge(perm_used, c + (k * C2 + s + 1))
                        ts(lhs[s], iota[:, 0:P], pd[:, ds(c + s, 1)], None, ALU.is_equal)
                        ts(rhs[s][:, 0:width], iota[:, 0:width], cd[:, ds(c + s, 1)], val[:, ds(c + s, 1)],
                           ALU.is_equal, ALU.mult).then_inc(perm_ready, 1)
                with ve.Fori(0, C2 // 4) as i:
                    columns(i * 4)
                ve.wait_ge(perm_used, 4 + (k + 1) * C2)

            def decode(sorted_i):
                v(ts(SRCSI[:, :], sorted_i, 12, None, ALU.arith_shift_right))
                v(cp(DSTS[:, :], SRCSI[:, :]))
                v(ts(SRCSI[:, :], sorted_i, 4095, None, ALU.bitwise_and))
            v(cp(KI[:, 0:C2], VAL[:, :]))
            decode(KI[:, 0:C2])
            for k in range(2):
                hi = K0[:, 0:C2]
                floor_div(hi, DSTS[:, :], KEYS2)
                if k == 0:
                    v(stt(K16[:, 0:C2], hi, -float(KEYS2), DSTS[:, :], ALU.mult, ALU.add))
                else:
                    v(cp(K16[:, 0:C2], hi))
                positions(2 + k, C2, KEYS2, 3, tmp_2, part_2, K2[:, 0:C2], False)
                floor_div(K0[:, 0:C2], K2[:, 0:C2], C2)
                v(stt(K1[:, 0:C2], K0[:, 0:C2], -float(C2), K2[:, 0:C2], ALU.mult, ALU.add))
                permute(k, K0, K1, C2, VAL)
                v(cp(VAL[:, :], B[6][:, 0:C2]))
                ve.sem_inc(perm_read, 1)
                v(cp(KI[:, 0:C2], VAL[:, :]))
                decode(KI[:, 0:C2])
            ve.sem_inc(idx2_ready, 1)
            ve.sem_inc(sorted2_ready, 1)
            ve.wait_ge(edge_in, 32)
            first_, goes_on, ends = (FLG[:, i, :] for i in range(3))
            v(tt(first_[:, 1:C2], DSTS[:, 1:C2], DSTS[:, 0:C2 - 1], ALU.not_equal))
            v(tt(first_[:, 0:1], DSTS[:, 0:1], dedge[:, 0:1], ALU.not_equal))
            v(cp(ends[:, 0:C2 - 1], first_[:, 1:C2]))
            v(tt(ends[:, C2 - 1:C2], DSTS[:, C2 - 1:C2], dedge[:, 1:2], ALU.not_equal))
            v(ts(goes_on, first_, -1.0, 1.0, ALU.mult, ALU.add))
            v(ve.memset(goes_on[:, 0:1], 1.0))
            v(cp(K2[:, 0:C2], flat_i[:, :]))
            v(tt(K2[:, 0:C2], K2[:, 0:C2], ends, ALU.mult))
            floor_div(K1[:, 0:C2], DSTS[:, :], P)
            v(stt(K0[:, 0:C2], K1[:, 0:C2], -float(P), DSTS[:, :], ALU.mult, ALU.add))
            permute(2, K0, K1, T, K2)
            v(cp(endi[:, :], B[6][:, 0:T]))
            ve.sem_inc(ends_ready, 1)

            ve.wait_ge(recs_back, 16)
            v(cp(POSI[:, :], REC[:, 0:CH, 0]))
            ve.sem_inc(chunks_ready, 1)
            v(ve.memset(AG, 0.0))

            def weigh(j, s):
                ts(SW[s % 4], iota[:, 0:P], REC[:, ds(j, 1), 1], REC[:, ds(j, 1), 2],
                   ALU.is_equal, ALU.mult).then_inc(sw_ready, 1)

            def chunks(i, first=False):
                _, at_block = nc.values_load_multi_w_load_instructions(
                    blk_i[0:1, ds(i * 16, 16)], engines=(mybir.EngineType.DVE,), min_val=0, max_val=T - 1)
                for s in range(16):
                    j = i * 16 + s
                    if not (first and s < 2):
                        ve.wait_ge(seg_done, j - 1)
                    weigh(j + 2, s + 2)
                    ve.wait_ge(seg_done, j + 1)
                    ve.wait_ge(seg_added, j + 4)
                    place = AG[:, ds(at_block[s], 1), :].rearrange("p a d -> p (a d)")
                    tt(place, place, B[s % 4][:, 0:D], ALU.add).then_inc(seg_added, 1)
            weigh(0, 0)
            weigh(1, 1)
            chunks(0, first=True)
            with ve.Fori(1, CH // 16) as i:
                chunks(i)
            ve.wait_ge(seg_added, 4 + CH)

            ve.sem_inc(bn_go, 1)
            ve.wait_ge(bn_done, 1)
            v(ts(stat[:, 0, :], B[4][:, 0:D], 1.0 / N, None, ALU.mult))
            wide = lambda r: r.unsqueeze(1).to_broadcast([P, T, D])
            tt(AG, AG, wide(stat[:, 0, :]), ALU.subtract).then_inc(bn_go, 1)
            ve.wait_ge(act_bn, 2)
            v(ve.reciprocal(stat[:, 1, :], stat[:, 1, :]))
            v(tt(stat[:, 1, :], stat[:, 1, :], rowv[:, 2, :], ALU.mult))
            v(tt(AG, AG, wide(stat[:, 1, :]), ALU.mult))
            tt(AG, AG, wide(rowv[:, 3, :]), ALU.add).then_inc(bn_go, 1)
            ve.wait_ge(act_bn, 3)
            v(tt(X[:, :, :], X[:, :, :], AG, ALU.add))

            statistics(X, mv, 4)
            reciprocal(4, rstd[:, :])

            def center3(t, b):
                ve.wait_ge(tp3_done, t + 1)
                ts(ring_n[b][:, 0:D], X[:, t, :], mv[:, t, 0:1], rstd[:, ds(t, 1)],
                   ALU.subtract, ALU.mult).then_inc(n3_ready, 1)

            def h_read(t, b):
                ve.wait_ge(h_done, 2 + t + 1)
                cp(HT[:, t, 2 * GH:ROW2], B[2 + b][:, 0:GH * NE]).then_inc(h_out, 1)
            tiles_ahead(ve, center3, h_read)
            ve.wait_ge(h_out, 2 + T)
            small_w = lambda i: attn_w[:, i, :].unsqueeze(1).to_broadcast([P, T, GH * NE])
            by_head = lambda a: a.rearrange("p t (h e) -> p t h e", e=NE)
            for i in range(2):
                v(tt(nodes2, HT[:, :, 2 * GH:ROW2], small_w(i), ALU.mult))
                v(red(HT[:, :, GH * i:GH * i + GH], by_head(nodes2), AX.X, ALU.add))
            ve.sem_inc(tab2_ready, 1)

            v(ts(DG[:, 0, :], ident[:, :], DSTS[:, 0:1], None, ALU.mult))
            ts(DG[:, 1, :], ident[:, :], DSTS[:, C2 - 1:C2], None, ALU.mult).then_inc(carry_go, 1)
            ve.wait_ge(carry_done, 1)
            v(stt(M2, B[4][:, 0:P], DSTS[:, C2 - 1:C2], tri[:, :], ALU.is_equal, ALU.mult))
            v(stt(MADD[0], B[4][:, P:2 * P], DSTS[:, 0:1], low[:, :], ALU.is_equal, ALU.mult))
            v(ts(MADD[0], MADD[0], BIG, BIG, ALU.mult, ALU.subtract))
            v(ts(MADD[1], M2, BIG, BIG, ALU.mult, ALU.subtract))

            with ve.Fori(0, C2 // 16) as i:
                for h in range(2):
                    for s in range(8):
                        ve.wait_ge(slot[8 * h + s], i * 16 + slot2[8 * h + s] + 16)
                    cp(G[:, ds(i * 16 + 8 * h, 8), :].rearrange("p c f -> p (c f)"), ROWS2[h]).then_inc(g_copied, 1)
            ve.wait_ge(g_copied, 2 * (C2 // 16))

            for h in range(GH):
                v(tt(MB[:, :, h], G[:, :, GH + h], first_, ALU.mult))
                v(scan(AD[:, :, h], goes_on, MB[:, :, h], 0.0, ALU.mult, ALU.add))
            v(cp(small[:, 0:GH], AD[:, C2 - 1, :]))
            ve.sem_inc(carry_go, 1)
            ve.wait_ge(carry_done, 2)
            v(cp(small[:, 8:8 + GH], B[5][:, 0:GH]))
            for h in range(GH):
                v(scan(AD[:, :, h], goes_on, MB[:, :, h], small[:, 8 + h:9 + h], ALU.mult, ALU.add))
            bar = K2[:, 0:C2]
            v(ts(bar, goes_on, BIG, BIG, ALU.mult, ALU.subtract))
            bar_back = K1[:, 0:C2]
            v(ve.memset(bar_back[:, C2 - 1:C2], 0.0))
            v(cp(bar_back[:, 0:C2 - 1], bar[:, 1:C2]))

            def largest(k, into, edge, src, barrier):
                for h in range(GH):
                    v(scan(into(h), barrier, src(h), (-BIG if k is None else small[:, k + h:k + h + 1]), ALU.add, ALU.max))
            fwd = (lambda h: MF[:, :, h], lambda h: G[:, :, h], bar)
            back = (lambda h: MB[:, ::-1, h], lambda h: G[:, ::-1, h], bar_back[:, ::-1])
            for n, (into, src, barrier) in enumerate((fwd, back)):
                largest(None, into, None, src, barrier)
                edge = C2 - 1 if n == 0 else 0
                for h in range(GH):
                    v(ts(DG[:, h, :], ident[:, :], (MF, MB)[n][:, edge, h:h + 1], None, ALU.mult))
                ve.sem_inc(carry_go, 1)
                ve.wait_ge(carry_done, 3 + n)
                v(tt(crows, B[6 + n][:, :].rearrange("p (h q) -> p h q", h=GH),
                     MADD[n].unsqueeze(1).to_broadcast([P, GH, P]), ALU.add))
                v(red(small[:, 16 + 4 * n:20 + 4 * n], crows, AX.X, ALU.max))
                largest(16 + 4 * n, into, None, src, barrier)
            v(tt(MF, MF, MB, ALU.max))
            v(tt(MF, MF, AD, ALU.add))
            v(stt(MB, MF, 0.2, MF, ALU.mult, ALU.max))
            v(tt(AD, AD, G[:, :, 0:GH], ALU.add))
            v(stt(MF, AD, 0.2, AD, ALU.mult, ALU.max))
            tt(MF, MF, MB, ALU.subtract).then_inc(esc_go, 1)
            ve.wait_ge(esc_done, 1)
            ee = G[:, :, GH:2 * GH]
            for h in range(GH):
                m = G[:, :, 2 * GH + NE * h:2 * GH + NE * h + NE]
                v(tt(m, m, ee[:, :, h:h + 1].to_broadcast([P, C2, NE]), ALU.mult))
            for f in range(SUMS):
                v(scan(SC[:, :, f], goes_on, G[:, :, GH + f], 0.0, ALU.mult, ALU.add))
            v(cp(small[:, 32:32 + SUMS], SC[:, C2 - 1, :]))
            ve.sem_inc(carry_go, 1)
            ve.wait_ge(carry_done, 5)
            v(cp(small[:, 64:64 + SUMS], B[5][:, 32:32 + SUMS]))
            for f in range(SUMS):
                v(scan(SC[:, :, f], goes_on, G[:, :, GH + f], small[:, 64 + f:65 + f], ALU.mult, ALU.add))
            ve.sem_inc(sums_ready, 1)

            ve.wait_ge(nodes_in, 16 * T)
            den, msg = nodes[:, :, 0:GH], nodes[:, :, GH:SUMS]
            v(ts(den, den, 1e-16, None, ALU.add))
            v(cp(small[:, 0:T * GH].rearrange("p (t h) -> p t h", t=T), den))
            v(ve.reciprocal(small[:, 0:T * GH], small[:, 0:T * GH]))
            inv = small[:, 0:T * GH].rearrange("p (t h) -> p t h", t=T)
            v(tt(by_head(nodes2), by_head(msg), inv.unsqueeze(3).to_broadcast([P, T, GH, NE]), ALU.mult))
            v(tt(nodes2, nodes2, small_w(2), ALU.add))
            v(red(gstat[:, :, 0], nodes2, AX.X, ALU.add))
            v(ts(gstat[:, :, 0], gstat[:, :, 0], 1.0 / (GH * NE), None, ALU.mult))
            v(tt(nodes2, nodes2, gstat[:, :, 0:1].to_broadcast([P, T, GH * NE]), ALU.subtract))
            v(tt(nodes3, nodes2, nodes2, ALU.mult))
            v(red(gstat[:, :, 1], nodes3, AX.X, ALU.add))
            v(ts(gstat[:, :, 1], gstat[:, :, 1], 1.0 / (GH * NE), None, ALU.mult))
            ve.sem_inc(stats_ready, 1)
            ve.wait_ge(root_ready, 5)
            v(cp(small[:, 128:128 + T], gstat[:, :, 1]))
            v(ve.reciprocal(small[:, 128:128 + T], small[:, 128:128 + T]))
            v(tt(nodes2, nodes2, small[:, 128:128 + T].unsqueeze(2).to_broadcast([P, T, GH * NE]), ALU.mult))
            v(tt(nodes2, nodes2, small_w(3), ALU.mult))
            v(tt(nodes2, nodes2, small_w(4), ALU.add))
            v(red(gates[:, :, :], nodes2.rearrange("p t (h e) -> p t e h", e=NE), AX.X, ALU.add))
            v(ts(gates[:, :, :], gates[:, :, :], 1.0 / GH, None, ALU.mult))
            for e in range(NE):
                me = gates[:, :, e:e + 1]
                if e:
                    v(tt(nodes3[:, :, 0:e], gates[:, :, 0:e], me.to_broadcast([P, T, e]), ALU.is_ge))
                v(ve.memset(nodes3[:, :, e:e + 1], 0.0))
                if e + 1 < NE:
                    v(tt(nodes3[:, :, e + 1:NE], gates[:, :, e + 1:NE], me.to_broadcast([P, T, NE - 1 - e]), ALU.is_gt))
                v(red(nodes3[:, :, 4 + e], nodes3[:, :, 0:NE], AX.X, ALU.add))
            v(ts(nodes3[:, :, 4:8], nodes3[:, :, 4:8], 1.5, None, ALU.is_lt))
            v(red(gstat[:, :, 0], gates[:, :, :], AX.X, ALU.max))
            tt(gates[:, :, :], gates[:, :, :], gstat[:, :, 0:1].to_broadcast([P, T, NE]), ALU.subtract).then_inc(gate_go, 1)
            ve.wait_ge(gate_done, 1)
            v(tt(gates[:, :, :], rank[:, :, :], nodes3[:, :, 4:8], ALU.mult))
            v(red(gstat[:, :, 0], gates[:, :, :], AX.X, ALU.add))
            v(cp(small[:, 0:T], gstat[:, :, 0]))
            v(ve.reciprocal(small[:, 0:T], small[:, 0:T]))
            v(tt(gates[:, :, :], gates[:, :, :], small[:, 0:T].unsqueeze(2).to_broadcast([P, T, NE]), ALU.mult))
            ve.sem_inc(moe_go, 1)

            def bias(t):
                for e in range(NE):
                    v(stt(X[:, t, :], eb2[:, e, :], gates[:, t, e:e + 1], X[:, t, :], ALU.mult, ALU.add))
            v.loop(T, NE, bias)

            def moe(g, tiles):
                for e in range(NE):
                    for j in range(tiles):
                        o, b = (4 * e + j, j % 2) if tiles == 4 else (e, e % 2)
                        t = 4 * g + j
                        ve.wait_ge(eo_done, 8 + 16 * g + o + 1)
                        ve.wait_ge(eo_added, 16 * g + o + 2)
                        stt(X[:, t, :], B[4 + b][:, 0:D], gates[:, t, e:e + 1], X[:, t, :],
                            ALU.mult, ALU.add).then_inc(eo_added, 1)
            with ve.Fori(0, GROUPS) as g:
                moe(g, 4)
            moe(GROUPS, 1)


def kernel(**inputs):
    import numpy as np
    import concourse.bacc as bacc
    from concourse.bass_utils import run_bass_kernel_spmd

    nc = bacc.Bacc("TRN2", target_bir_lowering=False, num_devices=1)
    arrays, args = {}, {}
    for name in LOADS:
        a = np.ascontiguousarray(inputs[name])
        arrays[f"in_{name}"] = a
        args[name] = nc.dram_tensor(f"in_{name}", a.shape, mybir.dt.from_np(a.dtype), kind="ExternalInput").ap()
    out = nc.dram_tensor("out_0", (N, D), F32, kind="ExternalOutput").ap()
    build(nc, args, out)
    r = run_bass_kernel_spmd(nc, [arrays], core_ids=[0])
    return r.results[0]["out_0"]
```

```python
from contextlib import ExitStack

import concourse.bass as bass
from concourse import mybir
from concourse.alu_op_type import AluOpType as ALU

ACT = mybir.ActivationFunctionType
AX = mybir.AxisListType
F32, F16, I32, U32 = mybir.dt.float32, mybir.dt.float16, mybir.dt.int32, mybir.dt.uint32
ds = bass.ds

P = 128
N, D = 3125, 256
T = 25
LAST = N - (T - 1) * P
NP = T * P
KT = D // P
EPS = 1e-5
E1, C1 = 50000, 392
FULL1, REST1 = E1 // C1, E1 % C1
CH = 2 * ((P * C1 + T * (2 * P - 1)) // (2 * P))
TURNS = CH // 16
LC = 14
E2, C2 = 32768, 288
KEYS2 = 57
HEADS, DH, KR = 8, 32, 4
QN = HEADS * KR
QKVN = 2 * QN + D
FF = 1024
FM = FF // P
NE, FE = 4, 512
EM = FE // P
GH = 4
ROW2 = 2 * GH + GH * NE
SUMS = GH + GH * NE
GROUPS = T // 4
SC2 = 12
HC = C2 // GROUPS
BIG = 1.0e30
ROUND = 12582912.0

LOADS = ["x", "src", "dst", "edge_weight", "L0_gnn_weight", "L0_gnn_gamma", "L0_gnn_beta", "L0_mix_ln1_g",
         "L0_mix_ln1_b", "L0_mix_Wx", "L0_mix_bx", "L0_mix_Wq", "L0_mix_Wk", "L0_mix_Wv", "L0_mix_Wo",
         "L0_mix_bo", "L0_mix_ln2_g", "L0_mix_ln2_b", "L0_mix_W1", "L0_mix_b1", "L0_mix_W2", "L0_mix_b2",
         "L0_ffn_W_gat", "L0_ffn_att_src", "L0_ffn_att_dst", "L0_ffn_b_gat", "L0_ffn_ln_gamma",
         "L0_ffn_ln_beta", "L0_ffn_W1", "L0_ffn_b1", "L0_ffn_W2", "L0_ffn_b2", "L0_ffn_edge_index"]


class Chain:

    def __init__(self, eng, sem):
        self.eng, self.sem, self.n = eng, sem, 0

    def __call__(self, ins):
        ins.then_inc(self.sem, 1)
        self.n = self.n + 1
        self.eng.wait_ge(self.sem, self.n)

    def go(self, ins):
        ins.then_inc(self.sem, 1)
        self.n = self.n + 1

    def join(self):
        self.eng.wait_ge(self.sem, self.n)

    def apart(self, count, at_once, step):
        with self.eng.Fori(0, count // at_once) as i:
            for q in range(at_once):
                step(i * at_once + q).then_inc(self.sem, 1)
        self.n = self.n + count
        self.join()

    def loop(self, count, per, body):
        base = self.n
        with self.eng.Fori(0, count) as i:
            self.n = base + i * per
            body(i)
        self.n = base + count * per


def tiles_in_pairs(eng, work):
    with eng.Fori(0, T // 2) as i:
        work(2 * i, 0)
        work(2 * i + 1, 1)
    work(T - 1, 0)


def tiles_ahead(eng, ahead, work):
    ahead(0, 0)
    with eng.Fori(0, T // 2) as i:
        ahead(2 * i + 1, 1)
        work(2 * i, 0)
        ahead(2 * i + 2, 0)
        work(2 * i + 1, 1)
    work(T - 1, 0)


def tiles_two_ahead(eng, ahead, work):
    ahead(0, 0)
    ahead(1, 1)
    with eng.Fori(0, (T - 3) // 2) as i:
        ahead(2 * i + 2, 0)
        work(2 * i, 0)
        ahead(2 * i + 3, 1)
        work(2 * i + 1, 1)
    ahead(T - 1, 0)
    for t in range(T - 3, T):
        work(t, (t - T + 1) % 2)


def groups_ahead(eng, ahead, work):
    ahead(0, 0, 4)

    def turn(g, b, tiles):
        work(g, b, tiles, lambda: ahead(g + 1, 1 - b, 4))
    turn(0, 0, 4)
    turn(1, 1, 4)
    with eng.Fori(1, 2) as i:
        turn(2 * i, 0, 4)
        turn(2 * i + 1, 1, 4)
    turn(4, 0, 4)
    work(5, 1, 4, lambda: ahead(6, 0, 1))
    work(6, 0, 1, lambda: None)


def build(nc, A, out):
    with ExitStack() as ctx:
        def sb(name, shape, dt=F32):
            return ctx.enter_context(nc.sbuf_tensor(name, shape, dt))

        def sem(name):
            return ctx.enter_context(nc.semaphore(name))

        X = sb("X", [P, T, D])
        XN = sb("XN", [P, T, D])
        RQ = sb("RQ", [P, KEYS2 * C2 // 2])
        RR = sb("RR", [P, 11232])
        RT = sb("RT", [P, 6400])

        def cut(region, start, *shape):
            size = 1
            for s in shape:
                size *= s
            v = region[:, start:start + size]
            if len(shape) == 2:
                return v.rearrange("p (a b) -> p a b", a=shape[0])
            if len(shape) == 3:
                return v.rearrange("p (a b c) -> p a b c", a=shape[0], b=shape[1])
            return v

        onehot = RQ[:, :].bitcast(F16)
        at = C1 * T // 2
        Wx = cut(RQ, at, KT, D); at += KT * D
        WxT = cut(RQ, at, KT, D); at += KT * D
        BD = cut(RQ, at, KT, QKVN); at += KT * QKVN
        bxb = cut(RQ, at, KT, P); at += KT * P
        SRC = cut(RQ, at, C1).bitcast(I32); at += C1
        DST = cut(RQ, at, C1).bitcast(I32); at += C1
        WT = cut(RQ, at, C1)
        QKV = cut(RQ, 0, T, QKVN)
        AG = cut(RQ, 0, T, D)
        of_place = [cut(RQ, 64 * s, 64).bitcast(F16) for s in range(4)]
        of_tile = [cut(RQ, 256 + 16 * s, 16).bitcast(F16)[:, 0:T] for s in range(4)]
        X2T = cut(RQ, 0, KT, NP)
        M2 = cut(RQ, KT * NP, P)
        MADD = [cut(RQ, KT * NP + P * (1 + i), P) for i in range(2)]
        DG = cut(RQ, KT * NP + 3 * P, GH, P)
        HT = cut(RQ, KT * NP + 7 * P, T, ROW2)
        counts = RR[:, 0:KEYS2 * C2 // 2].bitcast(F16)
        SRC2I = cut(RR, 5000, C2).bitcast(I32)
        DST2I = cut(RR, 5300, C2).bitcast(I32)
        jrow = cut(RR, 5600, CH // 2)
        W1s = cut(RR, 0, KT, FF)
        HID = [cut(RR, 2048 + 4096 * b, FM, 512) for b in range(2)]
        SQ = cut(RR, 0, T, D)
        G = cut(RR, 0, C2, ROW2)
        MF, MB, AD = (cut(RR, C2 * (ROW2 + GH * i), C2, GH) for i in range(3))
        FLG = cut(RR, C2 * (ROW2 + 3 * GH), 2, C2)
        nodes = cut(RR, 0, T, ROW2)
        nodes2 = cut(RR, T * ROW2, T, GH * NE)
        nodes3 = cut(RR, T * (ROW2 + GH * NE), T, GH * NE)
        tmp_s, part_s = RT[:, 0:5 * C1], RT[:, 5 * C1:10 * C1]
        tmp_2, part_2 = RT[:, 0:3 * C2], RT[:, 3 * C2:22 * C2]
        stat = cut(RT, 0, 3, D)
        ring_s = [cut(RT, 768 + D * b, D) for b in range(2)]
        lhs = [cut(RT, 4608 + P * s, P) for s in range(4)]
        rhs = [cut(RT, 5120 + C2 * s, C2) for s in range(4)]
        ROWS = [cut(RT, D * s, D) for s in range(16)]
        SW = [cut(RT, 4096 + P * r, P) for r in range(4)]
        H2T = [cut(RT, 1280 + 1024 * b, KT, 512) for b in range(2)]
        W2s = cut(RT, 3328, FM, D)
        ROWS2 = [cut(RT, 8 * ROW2 * h, 8 * ROW2) for h in range(2)]
        EHID = [cut(RT, 16 * ROW2 + 2048 * b, EM, 512) for b in range(2)]
        crows = cut(RT, 16 * ROW2 + 4096, GH, P)
        EW1 = XN[:, 0:16, :].rearrange("p t d -> p (t d)").rearrange("p (e k n) -> p e k n", e=NE, k=KT)
        EW2a = XN[:, 16:24, :].rearrange("p t d -> p (t d)").rearrange("p (e k n) -> p e k n", e=2, k=EM)

        iota = sb("iota", [P, 512], F16)
        iota_f = sb("iota_f", [P, P])
        flat_i = sb("flat_i", [P, C2], I32)
        rowid = sb("rowid", [P, 1])
        ident = sb("ident", [P, P])
        tri = sb("tri", [P, P])
        low = sb("low", [P, P])
        ones = sb("ones", [P, P])
        epsc = sb("epsc", [P, 1])
        hmask = sb("hmask", [QN, D])
        st6 = sb("st6", [P, T, 6])
        mv = sb("mv", [P, T, 2])
        rstd = sb("rstd", [P, T])
        mv2 = sb("mv2", [P, T, 2])
        rstd2 = sb("rstd2", [P, T])
        ring_n = [sb(f"ring_n{b}", [P, 2 * D]) for b in range(2)]
        ring_t = [sb(f"ring_t{b}", [P, 4, P]) for b in range(2)]
        g1, b1, g2, b2, bxc = (sb(n, [P, KT]) for n in ("g1", "b1", "g2", "b2", "bxc"))
        fb1 = sb("fb1", [P, FM])
        eb1 = sb("eb1", [P, NE, EM])
        rowv = sb("rowv", [P, 4, D])
        eb2 = sb("eb2", [NE, D])
        Wo, WH = sb("Wo", [P, KT, D]), sb("WH", [P, KT, D])
        Wc, bc = sb("Wc", [P, KT, QKVN]), sb("bc", [P, QKVN])
        Wg = sb("Wg", [P, KT, GH * NE])
        attn_w = sb("attn_w", [P, 5, GH * NE])
        RS = sb("RS", [P, 2048])
        REC = cut(RS, 0, CH + 16, 4)
        gT = [RS[0:NE, 512 * b:512 * b + 512] for b in range(2)]
        EW2b = cut(RS, 0, 2, EM * D).rearrange("p e (k n) -> p e k n", k=EM)
        K0, K1, K2 = sb("K0", [P, CH]), sb("K1", [P, CH]), sb("K2", [P, CH])
        K16 = sb("K16", [P, C1], F16)
        KI = sb("KI", [P, C2], I32)
        POSI = sb("POSI", [P, CH], I32)
        VAL = sb("VAL", [P, C2])
        cnts = sb("cnts", [P, 6, 64])
        blk_i = sb("blk_i", [P, CH // 2], I32)
        st_idx = [sb(f"st_idx{h}", [P, 8], I32) for h in range(2)]
        st_rec = [sb(f"st_rec{h}", [P, 8 * 4]) for h in range(2)]
        turnstile = sb("turnstile", [P, 1])
        DSTS = sb("DSTS", [P, C2])
        SRCSI = sb("SRCSI", [P, C2], I32)
        dedge = sb("dedge", [P, 1])
        endi = sb("endi", [P, T], I32)
        small = sb("small", [P, 256])
        gates = sb("gates", [P, T, NE])
        rank = sb("rank", [P, T, NE])
        gstat = sb("gstat", [P, T, 2])

        y_ring = [ring_n[0][:, :], ring_n[1][:, :]] + [r[:, :, :].rearrange("p a b -> p (a b)") for r in ring_t]
        y_of = lambda region, start, tiles: region[:, start:start + NE * tiles * D].rearrange(
            "p (e t d) -> p e t d", e=NE, t=tiles)
        xn_flat = XN[:, :, :].rearrange("p t d -> p (t d)")
        Y = [y_of(RR, 1600, 4), y_of(RR, 1600 + NE * 4 * D, 4), y_of(RQ, 0, 4), y_of(RQ, NE * 4 * D, 4),
             y_of(xn_flat, 0, 4), y_of(RT, 0, 4), y_of(RT, NE * 4 * D, 1)]

        B = [ctx.enter_context(nc.psum_tensor(f"bank{i}", [P, 512], F32)) for i in range(8)]

        table1 = nc.dram_tensor("table1", [NP, D], F32, kind="Internal").ap()
        recs = nc.dram_tensor("recs", [P * CH, 4], F32, kind="Internal").ap()
        table2 = nc.dram_tensor("table2", [NP, ROW2], F32, kind="Internal").ap()
        sums2 = nc.dram_tensor("sums2", [P * C2, ROW2], F32, kind="Internal").ap()

        y_dram = nc.dram_tensor("y_dram", [NE, NP, D], F32, kind="Internal").ap()

        (consts, padded, padded2, x_in, edges1_in, edges2_in, recs_zeroed, bd_zeroed, weights_in, signs,
         vec_step, stats_ready, root_ready, cnt_ready, pre_ready, pos1_ready, wxt_ready, wxt_out, wc_ready,
         wc_out, hh_ready, xr_ready, tp_done, t_out, proj_done, proj_out, sup_ready, mlp_in, recs_back,
         kmax_in, kmax_out, exp_go, exp_done, kv_done, kv_out, qc_ready, qt_done, qt_out, at_done, at_out,
         n2_ready, tp2_done, t2_out, hp_done, hid_out, op_done, fx_added, bias_added, op_added, perm_ready, perm_used, hist_ready, hist_used,
         perm_read, sorted2_ready, edge_in, idx2_ready, ends_ready, chunks_ready, staged, sw_ready, seg_done,
         seg_added, bn_go, bn_done, act_bn, x1_ready, experts_in, n3_ready, tp3_done, t3_out, h_done, h_out,
         tab2_ready, tab2_out, g_copied, carry_go, carry_done, esc_go, esc_done, sums_ready, sums_out,
         nodes_in, gate_go, gate_done, ep_done, ehid_out, eo_done, eo_out, gates_ready, gt_done, gt_out, gb_done, gb_added, combined, out_done) = (
            sem(n) for n in (
                "consts padded padded2 x_in edges1_in edges2_in recs_zeroed bd_zeroed weights_in signs "
                "vec_step stats_ready root_ready cnt_ready pre_ready pos1_ready wxt_ready wxt_out wc_ready "
                "wc_out hh_ready xr_ready tp_done t_out proj_done proj_out sup_ready mlp_in recs_back "
                "kmax_in kmax_out exp_go exp_done kv_done kv_out qc_ready qt_done qt_out at_done at_out "
                "n2_ready tp2_done t2_out hp_done hid_out op_done fx_added bias_added op_added perm_ready perm_used hist_ready hist_used "
                "perm_read sorted2_ready edge_in idx2_ready ends_ready chunks_ready staged sw_ready seg_done "
                "seg_added bn_go bn_done act_bn x1_ready experts_in n3_ready tp3_done t3_out h_done h_out "
                "tab2_ready tab2_out g_copied carry_go carry_done esc_go esc_done sums_ready sums_out "
                "nodes_in gate_go gate_done ep_done ehid_out eo_done eo_out gates_ready gt_done gt_out gb_done gb_added combined out_done").split())
        sup_out = [sem(f"sup_out{b}") for b in range(2)]
        y_out = [sem(f"y_out{i}") for i in range(4)]
        y_in = [sem(f"y_in{g}") for g in range(GROUPS + 1)]
        slot = [sem(f"slot{i}") for i in range(16)]
        slot1 = [16 * (C1 // LC) if s < LC else 0 for s in range(16)]
        slot2 = [n + 16 * (TURNS + (s < 8)) for s, n in enumerate(slot1)]
        N_CONSTS = 10

        col = lambda v, k: v.rearrange("(k p) -> p k", k=k)
        weights = [(g1[:, :], col(A["L0_mix_ln1_g"], KT)), (b1[:, :], col(A["L0_mix_ln1_b"], KT)),
                   (g2[:, :], col(A["L0_mix_ln2_g"], KT)), (b2[:, :], col(A["L0_mix_ln2_b"], KT)),
                   (bxc[:, :], col(A["L0_mix_bx"], KT)), (fb1[:, :], col(A["L0_mix_b1"], FM)),
                   (Wx, A["L0_mix_Wx"].rearrange("(k p) n -> p k n", p=P)),
                   (Wo[:, :, :], A["L0_mix_Wo"].rearrange("(k p) n -> p k n", p=P)),
                   (Wg[:, :, :], A["L0_ffn_W_gat"].rearrange("(k p) n -> p k n", p=P))]
        weights += [(rowv[:, i, :], A[n].partition_broadcast(P))
                    for i, n in enumerate(("L0_mix_bo", "L0_mix_b2", "L0_gnn_gamma", "L0_gnn_beta"))]
        weights.append((eb2[:, :], A["L0_ffn_b2"]))
        for e in range(NE):
            weights.append((eb1[:, e, :], col(A["L0_ffn_b1"][e, :], EM)))
        weights += [(attn_w[:, i, :], A[n].rearrange("h e -> (h e)").partition_broadcast(P))
                    for i, n in enumerate(("L0_ffn_att_src", "L0_ffn_att_dst"))]
        weights += [(attn_w[:, 2 + i, :], A[n].partition_broadcast(P))
                    for i, n in enumerate(("L0_ffn_b_gat", "L0_ffn_ln_gamma", "L0_ffn_ln_beta"))]
        for h in range(HEADS):
            k, q = h // 4, DH * (h % 4)
            weights.append((BD[q:q + DH, k, KR * h:KR * h + KR], A["L0_mix_Wq"]))
            weights.append((BD[q:q + DH, k, QN + KR * h:QN + KR * h + KR], A["L0_mix_Wk"]))
            weights.append((BD[q:q + DH, k, 2 * QN + DH * h:2 * QN + DH * h + DH], A["L0_mix_Wv"]))
        PARTS = ((0, 1, 2, 3), (1, 0, 3, 2), (2, 3, 0, 1), (3, 2, 1, 0))
        MINUS = ((1, 0), (2, 0), (3, 0), (1, 3), (2, 1), (3, 2))
        for r in range(4):
            for c in range(4):
                weights.append((WH[64 * (r % 2):64 * (r % 2) + 64, r // 2, 64 * c:64 * c + 64],
                                A["L0_gnn_weight"][:, 64 * PARTS[r][c]:64 * PARTS[r][c] + 64]))

        def load_y(eng, g):
            tiles = 4 if g < GROUPS else 1
            for e in range(NE):
                eng.dma_start(Y[g][:, e, :, :], y_dram[e, g * 512:g * 512 + tiles * P, :].rearrange(
                    "(t p) d -> p t d", p=P)).then_inc(y_in[g], 16)

        block = ctx.enter_context(nc.Block())

        @block.sync
        def _(sp):
            for b in range(2):
                sp.sem_inc(sup_out[b], 16)
            for s in range(4):
                sp.sem_inc(y_out[s], 16)
            sp.wait_ge(padded, 7)
            sp.dma_start(recs.rearrange("(p c) f -> p (c f)", p=P), RT[:, 0:CH * 4]).then_inc(recs_zeroed, 16)
            for name, tile in (("src", SRC), ("dst", DST), ("edge_weight", WT)):
                a = A[name]
                sp.dma_start(tile[0:FULL1, :], a[0:FULL1 * C1].rearrange("(p c) -> p c", c=C1)).then_inc(edges1_in, 16)
                sp.dma_start(tile[FULL1:FULL1 + 1, 0:REST1],
                             a[FULL1 * C1:E1].rearrange("(p c) -> p c", p=1)).then_inc(edges1_in, 16)
            x = A["x"]
            sp.dma_start(X[:, 0:T - 1, :], x[0:(T - 1) * P, :].rearrange("(t p) d -> p t d", p=P)).then_inc(x_in, 16)
            sp.dma_start(X[0:LAST, T - 1, :], x[(T - 1) * P:N, :]).then_inc(x_in, 16)
            sp.wait_ge(padded2, 2)
            p0, c0 = NP // C2, NP % C2
            head = C2 - c0
            full = (E2 - head) // C2
            rest = E2 - head - full * C2
            for r, tile in ((0, SRC2I), (1, DST2I)):
                e = A["L0_ffn_edge_index"][r:r + 1, :]
                sp.dma_start(tile[p0:p0 + 1, c0:C2], e[:, 0:head]).then_inc(edges2_in, 16)
                sp.dma_start(tile[p0 + 1:p0 + 1 + full, :],
                             e[:, head:head + full * C2].rearrange("a (p c) -> (a p) c", c=C2)).then_inc(edges2_in, 16)
                sp.dma_start(tile[p0 + 1 + full:p0 + 2 + full, 0:rest], e[:, E2 - rest:E2]).then_inc(edges2_in, 16)

            def store(t, b):
                sp.wait_ge(sup_ready, t + 1)
                sp.dma_start(table1[ds(t * P, P), :], ring_s[b]).then_inc(sup_out[b], 16)
            tiles_in_pairs(sp, store)
            sp.dma_start(W1s, A["L0_mix_W1"].rearrange("(k p) n -> p k n", p=P)).then_inc(mlp_in, 16)
            sp.dma_start(W2s, A["L0_mix_W2"].rearrange("(k p) n -> p k n", p=P)).then_inc(mlp_in, 16)
            for s in range(LC):
                sp.wait_ge(slot[s], slot1[s])
            sp.dma_start(REC[:, 0:CH, :], recs.rearrange("(p c) f -> p c f", p=P)).then_inc(recs_back, 16)
            sp.wait_ge(sorted2_ready, 1)
            sp.dma_start(dedge[1:P, 0:1], DSTS[0:P - 1, C2 - 1:C2]).then_inc(edge_in, 16)
            sp.wait_ge(x1_ready, 1)
            sp.dma_start(EW1, A["L0_ffn_W1"].rearrange("e (k p) n -> p e k n", p=P)).then_inc(experts_in, 16)
            sp.dma_start(EW2a, A["L0_ffn_W2"][0:2].rearrange("e (k p) n -> p e k n", p=P)).then_inc(experts_in, 16)
            sp.wait_ge(seg_added, 4 + CH // 2)
            sp.dma_start(EW2b, A["L0_ffn_W2"][2:4].rearrange("e (k p) n -> p e k n", p=P)).then_inc(experts_in, 16)
            sp.wait_ge(tab2_ready, 1)
            sp.dma_start(table2.rearrange("(t p) f -> p t f", p=P), HT).then_inc(tab2_out, 16)

            with sp.Fori(0, GROUPS) as g:
                for e in range(NE):
                    for h in range(2):
                        sp.wait_ge(eo_out, g * 8 + (2 + 2 * e + h + 1))
                        sp.dma_start(y_dram[e, ds((4 * g + 2 * h) * P, 2 * P), :].rearrange("(t p) d -> p t d", p=P),
                                     y_ring[(2 * e + h) % 4].rearrange("p (t d) -> p t d", t=2)).then_inc(y_out[(2 * e + h) % 4], 16)
            for e in range(NE):
                sp.wait_ge(eo_out, 2 + 8 * GROUPS + e + 1)
                sp.dma_start(y_dram[e, (T - 1) * P:NP, :], y_ring[e][:, 0:D]).then_inc(y_out[e], 16)
            for s in range(4):
                sp.wait_ge(y_out[s], 16 + 16 * (2 * GROUPS + 1))
            sp.wait_ge(sums_out, 16)
            for g in range(2, GROUPS + 1):
                load_y(sp, g)
            for g in range(GROUPS):
                sp.wait_ge(combined, g + 1)
                sp.dma_start(out[g * 512:(g + 1) * 512, :].rearrange("(t p) d -> p t d", p=P),
                             X[:, 4 * g:4 * g + 4, :]).then_inc(out_done, 16)
            sp.wait_ge(combined, GROUPS + 1)
            sp.dma_start(out[(T - 1) * P:N, :], X[0:LAST, T - 1, :]).then_inc(out_done, 16)
            sp.wait_ge(out_done, 16 * (GROUPS + 1))

        @block.gpsimd
        def _(gp):
            gp.memset(RT[:, 0:CH * 4], 0.0).then_inc(padded, 1)
            gp.memset(SRC, 0).then_inc(padded, 1)
            gp.memset(DST, 0).then_inc(padded, 1)
            gp.memset(WT, 0.0).then_inc(padded, 1)
            gp.memset(X[:, T - 1, :], 0.0).then_inc(padded, 1)
            gp.memset(REC[:, :, :], 0.0).then_inc(padded, 1)
            gp.iota(flat_i[:, :], pattern=[[1, C2]], base=0, channel_multiplier=C2).then_inc(padded, 1)
            gp.iota(iota[:, :], pattern=[[1, 512]], base=0, channel_multiplier=0,
                    allow_small_or_imprecise_dtypes=True).then_inc(consts, 1)
            gp.iota(iota_f[:, :], pattern=[[1, P]], base=0, channel_multiplier=0,
                    allow_small_or_imprecise_dtypes=True).then_inc(consts, 1)
            gp.iota(rowid[:, :], pattern=[[0, 1]], base=0, channel_multiplier=1,
                    allow_small_or_imprecise_dtypes=True).then_inc(consts, 1)
            gp.iota(jrow, pattern=[[2 * P, CH // 2]], base=0, channel_multiplier=0,
                    allow_small_or_imprecise_dtypes=True).then_inc(consts, 1)
            gp.memset(ones[:, :], 1.0).then_inc(consts, 1)
            gp.memset(epsc[:, :], EPS).then_inc(consts, 1)
            gp.memset(dedge[:, :], -1.0).then_inc(consts, 1)
            gp.memset(BD, 0.0).then_inc(bd_zeroed, 1)
            gp.memset(hmask[:, :], 1.0).then_inc(consts, 1)
            gp.wait_ge(consts, 8)
            hm = hmask[:, :].rearrange("p (h d) -> p h d", h=HEADS)
            gp.affine_select(out=hm, in_=hm, compare_op=ALU.is_ge, fill=0.0, base=0,
                             pattern=[[-KR, HEADS], [0, DH]], channel_multiplier=1).then_inc(consts, 1)
            gp.wait_ge(consts, 9)
            gp.affine_select(out=hm, in_=hm, compare_op=ALU.is_ge, fill=0.0, base=KR - 1,
                             pattern=[[KR, HEADS], [0, DH]], channel_multiplier=-1).then_inc(consts, 1)

            def pass_through():
                gp.tensor_tensor(turnstile[:, :], rowid[:, :], rowid[:, :], ALU.add)

            gp.wait_ge(pos1_ready, 1)
            gp.wait_ge(recs_zeroed, 16)
            half = LC // 2
            flat_rec = REC[:, :, :].rearrange("p c f -> p (c f)")

            def scatter(i, first=False):
                for h in range(2):
                    if not first:
                        for s in range(half):
                            gp.wait_ge(slot[half * h + s], i * 16)
                    c = i * LC + half * h
                    gp.tensor_copy(st_idx[h][:, 0:half], POSI[:, ds(c, half)]).then_inc(staged, 1)
                    gp.tensor_copy(st_rec[h][:, 0:4 * half], flat_rec[:, ds(c * 4, 4 * half)]).then_inc(staged, 1)
                    gp.wait_ge(staged, i * 4 + 2 * h + 2)
                    pass_through()
                    for s in range(half):
                        gp.indirect_dma_start(
                            recs, bass.IndirectOffsetOnAxis(ap=st_idx[h][:, s:s + 1].bitcast(U32), axis=0),
                            st_rec[h][:, 4 * s:4 * s + 4], None).then_inc(slot[half * h + s], 16)
            scatter(0, first=True)
            with gp.Fori(1, C1 // LC) as i:
                scatter(i)
            n = 4 * (C1 // LC)

            def gather(i, h, rows, table, first, used):
                if used is not None:
                    gp.wait_ge(*used)
                gp.tensor_copy(st_idx[h][:, :], (POSI if table is table1 else SRCSI)[:, ds(i * 16 + 8 * h, 8)]).then_inc(staged, 1)
                gp.wait_ge(staged, i * 2 + first + h + 1)
                pass_through()
                for s in range(8):
                    gp.indirect_dma_start(
                        rows(h, s), None, table,
                        bass.IndirectOffsetOnAxis(ap=st_idx[h][:, s:s + 1].bitcast(U32), axis=0)
                    ).then_inc(slot[8 * h + s], 16)

            gp.wait_ge(chunks_ready, 1)
            for b in range(2):
                gp.wait_ge(sup_out[b], 16 + 16 * ((T + 1 - b) // 2))
            rows1 = lambda h, s: ROWS[8 * h + s]
            for h in range(2):
                gather(0, h, rows1, table1, n, None)
            with gp.Fori(1, TURNS) as i:
                for h in range(2):
                    gather(i, h, rows1, table1, n, (seg_done, i * 16 + 8 * h - 8))
            gather(TURNS, 0, rows1, table1, n, (seg_done, TURNS * 16 - 8))
            n += 2 * TURNS + 1

            gp.wait_ge(tab2_out, 16)
            gp.wait_ge(idx2_ready, 1)
            rows2 = lambda h, s: ROWS2[h][:, ROW2 * s:ROW2 * s + ROW2]
            for h in range(2):
                gather(0, h, rows2, table2, n, None)
            with gp.Fori(1, C2 // 16) as i:
                for h in range(2):
                    gather(i, h, rows2, table2, n, (g_copied, i * 2 + h - 1))

            gp.wait_ge(sums_ready, 1)
            gp.dma_start(sums2.rearrange("(p c) f -> p c f", p=P), G).then_inc(sums_out, 16)
            gp.wait_ge(sums_out, 16)
            gp.wait_ge(ends_ready, 1)
            for t in range(T):
                gp.indirect_dma_start(
                    nodes[:, t, :], None, sums2,
                    bass.IndirectOffsetOnAxis(ap=endi[:, t:t + 1].bitcast(U32), axis=0)).then_inc(nodes_in, 16)
            for s in range(4):
                gp.wait_ge(y_out[s], 16 + 16 * 4)
            for g in range(2):
                load_y(gp, g)

        @block.scalar
        def _(act):
            act.sem_inc(t_out, 6)
            act.sem_inc(qt_out, 2)
            act.sem_inc(t2_out, 4)
            act.sem_inc(hid_out, 2)
            act.sem_inc(t3_out, 4)
            act.sem_inc(ehid_out, 2)
            act.sem_inc(eo_out, 2)
            act.wait_ge(bd_zeroed, 1)
            for dst, src in weights:
                act.dma_start(dst, src, allow_slow_non_contiguous=True).then_inc(weights_in, 16)

            def root(k, tile, var):
                act.wait_ge(stats_ready, k)
                act.activation(tile, var, ACT.Sqrt, bias=epsc[:, 0:1], scale=1.0).then_inc(root_ready, 1)
            act.wait_ge(consts, N_CONSTS)
            root(1, rstd[:, :], mv[:, :, 1])
            root(2, rstd2[:, :], mv2[:, :, 1])

            act.wait_ge(wxt_ready, 1)
            for k in range(KT):
                act.activation(WxT[:, k, :], B[k][:, 0:D], ACT.Copy).then_inc(wxt_out, 1)

            act.wait_ge(weights_in, 16 * len(weights))

            def place(t, b):
                act.wait_ge(tp_done, t + 1)
                act.activation(ring_n[b][:, 0:D], XN[:, t, :], ACT.Copy).then_inc(xr_ready, 1)

            def turned(t, b):
                act.wait_ge(tp_done, 2 + t + 1)
                act.wait_ge(proj_done, t + 1)
                act.activation(ring_t[b][:, 0:2, :].rearrange("p k n -> p (k n)"), B[b][:, 0:D], ACT.Copy).then_inc(t_out, 1)
                for k in range(KT):
                    act.activation(ring_t[b][:, 2 + k, :], B[b][:, D + P * k:D + P * k + P], ACT.Identity,
                                   bias=b1[:, k:k + 1], scale=g1[:, k:k + 1]).then_inc(t_out, 1)
            tiles_ahead(act, place, turned)

            act.wait_ge(exp_go, 1)
            act.activation(QKV[:, :, QN:2 * QN], QKV[:, :, QN:2 * QN], ACT.Exp).then_inc(exp_done, 1)
            act.wait_ge(exp_go, 2)
            act.activation(QKV[:, :, 0:QN], QKV[:, :, 0:QN], ACT.Exp).then_inc(exp_done, 1)

            act.wait_ge(exp_go, 3)

            def place_q(t, b):
                act.wait_ge(qt_done, t + 1)
                act.activation(ring_n[b][:, 0:QN], QKV[:, t, 0:QN], ACT.Copy).then_inc(qc_ready, 1)

            def turned_q(t, b):
                act.wait_ge(qt_done, 2 + t + 1)
                act.wait_ge(at_done, t + 1)
                act.activation(ring_t[b][0:QN, 0, :], B[b][0:QN, 0:P], ACT.Copy).then_inc(qt_out, 1)
            tiles_ahead(act, place_q, turned_q)

            root(3, rstd[:, :], mv[:, :, 1])

            def turned2(g, b, tiles):
                act.wait_ge(hp_done, 8 * g + 8)
                for j in range(tiles):
                    act.wait_ge(tp2_done, 2 + 4 * g + j + 1)
                    for k in range(KT):
                        act.activation(H2T[b][:, k, P * j:P * j + P], B[j % 2][:, P * k:P * k + P], ACT.Identity,
                                       bias=b2[:, k:k + 1], scale=g2[:, k:k + 1]).then_inc(t2_out, 1)

            def gelu(g, b, tiles, ahead):
                act.wait_ge(op_done, 4 * g + 4)
                for m in range(FM):
                    act.wait_ge(hp_done, 16 + FM * g + m + 1)
                    act.activation(HID[b][:, m, 0:P * tiles], B[2 + m % 2][:, 0:P * tiles], ACT.Gelu,
                                   bias=fb1[:, m:m + 1], scale=1.0).then_inc(hid_out, 1)
                ahead()
            groups_ahead(act, turned2, gelu)

            act.wait_ge(bn_go, 2)
            act.activation(SQ, AG, ACT.Square).then_inc(act_bn, 1)
            act.wait_ge(bn_done, 2)
            act.activation(stat[:, 1, :], B[5][:, 0:D], ACT.Sqrt, bias=epsc[:, 0:1], scale=1.0 / N).then_inc(act_bn, 1)
            act.wait_ge(bn_go, 3)
            act.activation(AG, AG, ACT.Tanh).then_inc(act_bn, 1)

            root(4, rstd[:, :], mv[:, :, 1])

            def turned3(t, b):
                act.wait_ge(tp3_done, 2 + t + 1)
                act.wait_ge(h_done, t + 1)
                act.activation(ring_t[b][:, 0:2, :].rearrange("p k n -> p (k n)"), B[b][:, 0:D], ACT.Copy).then_inc(t3_out, 1)
                act.activation(X2T[:, :, ds(t * P, P)], B[b][:, 0:D].rearrange("p (k n) -> p k n", k=KT), ACT.Copy).then_inc(t3_out, 1)
            tiles_in_pairs(act, turned3)

            def gelus(g, e, tiles):
                act.wait_ge(eo_done, (8 * g + 2 * e + 2) if tiles == 4 or e < 2 else 8 * GROUPS + 3 + e)
                for m in range(EM):
                    act.wait_ge(ep_done, 2 + 16 * g + 4 * e + m + 1)
                    act.activation(EHID[e % 2][:, m, 0:P * tiles], B[2 + m % 2][:, 0:P * tiles], ACT.Gelu,
                                   bias=eb1[:, e, m:m + 1], scale=1.0).then_inc(ehid_out, 1)

            def emit(g, e, tiles):
                for h in range(2 if tiles == 4 else 1):
                    n, place, b = (2 * e + h, (2 * e + h) % 4, h) if tiles == 4 else (e, e, e % 2)
                    width = 2 * D if tiles == 4 else D
                    act.wait_ge(eo_done, 4 + 8 * g + n + 1)
                    act.wait_ge(y_out[place], 16 + 32 * g + (16 * (e // 2) if tiles == 4 else 0))
                    act.activation(y_ring[place][:, 0:width], B[4 + b][:, 0:width], ACT.Copy).then_inc(eo_out, 1)

            def moe(g, tiles, between=None):
                gelus(g, 0, tiles)
                for e in range(NE):
                    if e + 1 < NE:
                        gelus(g, e + 1, tiles)
                    emit(g, e, tiles)
                    if between and e == 0:
                        between()

            def exp_scores():
                act.wait_ge(esc_go, 1)
                act.activation(G[:, :, GH:2 * GH], MF, ACT.Exp).then_inc(esc_done, 1)
            with act.Fori(0, GROUPS - 1) as g:
                moe(g, 4)
            moe(GROUPS - 1, 4, exp_scores)
            moe(GROUPS, 1)
            root(5, gstat[:, :, 1], gstat[:, :, 1])
            act.wait_ge(gate_go, 1)
            act.activation(rank[:, :, :], gates[:, :, :], ACT.Exp).then_inc(gate_done, 1)
            for g in range(GROUPS + 1):
                width = 4 * P if g < GROUPS else P
                act.wait_ge(gt_done, g + 1)
                if g >= 2:
                    act.wait_ge(gb_done, g - 1)
                act.activation(gT[g % 2][:, 0:width], B[g % 2][0:NE, 0:width], ACT.Copy).then_inc(gt_out, 1)

        @block.tensor
        def _(pe):
            mm, tr = nc.tensor.matmul, nc.tensor.transpose
            pe.sem_inc(tp_done, 2)
            pe.sem_inc(proj_done, 2)
            pe.sem_inc(qt_done, 2)
            pe.sem_inc(at_done, 2)
            pe.sem_inc(tp2_done, 2)
            pe.sem_inc(hp_done, 16)
            pe.sem_inc(op_done, 8)
            pe.sem_inc(perm_used, 4)
            pe.sem_inc(hist_used, 4)
            pe.sem_inc(tp3_done, 2)
            pe.sem_inc(h_done, 2)
            pe.sem_inc(ep_done, 2)
            pe.sem_inc(eo_done, 4)
            pe.wait_ge(consts, N_CONSTS)

            def prefix(k, keys):
                pe.wait_ge(cnt_ready, k)
                mm(B[7][:, 0:keys], tri[:, :], cnts[:, 0, 0:keys], start=True, stop=True)
                mm(B[7][:, 64:64 + keys], ones[:, :], cnts[:, 0, 0:keys], start=True, stop=True).then_inc(pre_ready, 1)
            prefix(1, T)

            pe.wait_ge(weights_in, 16 * len(weights))
            for k in range(KT):
                for m in range(KT):
                    last = tr(B[k][:, P * m:P * m + P], Wx[:, m, P * k:P * k + P], ident[:, :])
            last.then_inc(wxt_ready, 1)
            pe.wait_ge(wxt_out, 2)
            for m in range(KT):
                for k in range(KT):
                    mm(B[2 + m][:, 0:QKVN], WxT[:, k, P * m:P * m + P], BD[:, k, :], start=(k == 0), stop=(k == KT - 1))
            pe.wait_ge(signs, 1)
            for k in range(KT):
                last = mm(B[4][:, 0:QKVN], bxb[:, k, :], BD[:, k, :], start=(k == 0), stop=(k == KT - 1))
            last.then_inc(wc_ready, 1)
            pe.wait_ge(wc_out, 3)

            def turn(t, b):
                pe.wait_ge(hh_ready, t + 1)
                pe.wait_ge(xr_ready, t + 1)
                pe.wait_ge(t_out, 3 * t + 3)
                for k in range(4):
                    last = tr(B[b][:, P * k:P * k + P], ring_n[b][:, P * k:P * k + P], ident[:, :])
                last.then_inc(tp_done, 1)

            def project(t, b):
                pe.wait_ge(t_out, 6 + 3 * t + 3)
                pe.wait_ge(proj_out, t + 1)
                for k in range(KT):
                    mm(B[2 + b][:, 0:D], ring_t[b][:, k, :], WH[:, k, :], start=(k == 0), stop=(k == KT - 1))
                for k in range(KT):
                    last = mm(B[4 + b][:, 0:QKVN], ring_t[b][:, 2 + k, :], Wc[:, k, :], start=(k == 0), stop=(k == KT - 1))
                last.then_inc(proj_done, 1)
            tiles_ahead(pe, turn, project)

            pe.wait_ge(kmax_in, 1)
            tr(B[6][0:QN, 0:P], small[:, 0:QN], ident[:, :]).then_inc(kmax_out, 1)
            pe.wait_ge(kmax_in, 2)
            mm(B[7][:, 128:128 + QN], ones[0:QN, :], small[0:QN, 64:64 + QN], start=True, stop=True).then_inc(kmax_out, 1)
            pe.wait_ge(exp_done, 1)
            for t in range(T):
                n = P if t < T - 1 else LAST
                mm(B[6][0:QN, 0:D], QKV[0:n, t, QN:2 * QN], QKV[0:n, t, 2 * QN:QKVN], start=(t == 0), stop=(t == T - 1))
                last = mm(B[0][0:QN, 0:1], QKV[0:n, t, QN:2 * QN], ones[0:n, 0:1], start=(t == 0), stop=(t == T - 1))
            last.then_inc(kv_done, 1)
            pe.wait_ge(kv_out, 1)
            for k in range(KT):
                last = tr(B[4][:, QN * k:QN * k + QN], stat[0:QN, 0, P * k:P * k + P], ident[0:QN, 0:QN])
            last.then_inc(kv_done, 1)
            pe.wait_ge(kv_out, 2)
            for k in range(KT):
                last = mm(B[5][0:QN, 0:D], small[:, 96 + QN * k:96 + QN * k + QN], Wo[:, k, :], start=(k == 0), stop=(k == KT - 1))
            last.then_inc(kv_done, 1)
            pe.wait_ge(kv_out, 3)

            def turn_q(t, b):
                pe.wait_ge(qc_ready, t + 1)
                pe.wait_ge(qt_out, t + 1)
                tr(B[b][0:QN, 0:P], ring_n[b][:, 0:QN], ident[:, :]).then_inc(qt_done, 1)

            def attend(t, b):
                pe.wait_ge(qt_out, 2 + t + 1)
                pe.wait_ge(at_out, t + 1)
                mm(B[2 + b][:, 0:D], ring_t[b][0:QN, 0, :], stat[0:QN, 1, :], start=True, stop=True).then_inc(at_done, 1)
            tiles_ahead(pe, turn_q, attend)

            pe.wait_ge(mlp_in, 32)

            def turn2(g, b, tiles):
                for j in range(tiles):
                    pe.wait_ge(n2_ready, 4 * g + j + 1)
                    pe.wait_ge(t2_out, 8 * g + 2 * j + 2)
                    for k in range(KT):
                        last = tr(B[j % 2][:, P * k:P * k + P], ring_n[j % 2][:, P * k:P * k + P], ident[:, :])
                    last.then_inc(tp2_done, 1)

            def histogram(g, m):
                for q in range(HC // FM):
                    j = m * (HC // FM) + q
                    pe.wait_ge(hist_ready, g * HC + j + 1)
                    mm(B[6][:, 0:T], of_place[j % 4], of_tile[j % 4], start=(isinstance(g, int) and g == 0 and j == 0),
                       stop=(isinstance(g, int) and g == GROUPS - 1 and j == HC - 1),
                       skip_group_check=True).then_inc(hist_used, 1)

            def mlp(g, b, tiles, ahead):
                n = P * tiles
                pe.wait_ge(t2_out, 4 + 8 * g + 2 * tiles)
                for m in range(FM):
                    pe.wait_ge(hid_out, FM * g + m + 1)
                    for k in range(KT):
                        last = mm(B[2 + m % 2][:, 0:n], W1s[:, k, P * m:P * m + P], H2T[b][:, k, 0:n], start=(k == 0), stop=(k == KT - 1))
                    last.then_inc(hp_done, 1)
                    if tiles == 4:
                        histogram(g, m)
                ahead()
                pe.wait_ge(hid_out, 2 + FM * g + FM)
                for j in range(tiles):
                    pe.wait_ge(op_added, 4 * g + j + 1)
                    for k in range(FM):
                        last = mm(B[4 + j % 2][:, 0:D], HID[b][:, k, P * j:P * j + P], W2s[:, k, :], start=(k == 0), stop=(k == FM - 1))
                    last.then_inc(op_done, 1)
            groups_ahead(pe, turn2, mlp)

            def column(c, s, first=False, final=False):
                pe.wait_ge(perm_ready, c + (s + 1))
                mm(B[6][:, 0:C2], lhs[s % 4], rhs[s % 4], start=first, stop=final,
                   skip_group_check=True).then_inc(perm_used, 1)

            prefix(2, T)
            prefix(3, KEYS2)
            for s in range(4):
                column(0, s, first=(s == 0))
            with pe.Fori(1, C2 // 4 - 1) as i:
                for s in range(4):
                    column(i * 4, s)
            for s in range(4):
                column(C2 - 4, s, final=(s == 3))
            prefix(4, KEYS2)
            pe.wait_ge(perm_read, 1)

            def chunks(i, sort=True, count=16):
                for s in range(count):
                    pe.wait_ge(sw_ready, i * 16 + s + 1)
                    pe.wait_ge(slot[s], i * 16 + slot1[s] + 16)
                    if s % 2 == 0:
                        pe.wait_ge(seg_added, i * 8 + s // 2 + 1)
                    mm(B[s // 2 % 4][:, 0:D], SW[s % 4], ROWS[s], start=(s % 2 == 0), stop=(s % 2 == 1)).then_inc(seg_done, 1)
                    q = s - 3
                    if sort and 0 <= q < SC2:
                        known = isinstance(i, int)
                        column(i * SC2 + C2, q, first=(known and i == 0 and q == 0),
                               final=(known and i == C2 // SC2 - 1 and q == SC2 - 1))
            chunks(0)
            with pe.Fori(1, C2 // SC2 - 1) as i:
                chunks(i)
            chunks(C2 // SC2 - 1)
            with pe.Fori(C2 // SC2, TURNS) as i:
                chunks(i, sort=False)
            chunks(TURNS, sort=False, count=8)

            pe.wait_ge(bn_go, 1)
            for t in range(T):
                last = mm(B[4][:, 0:D], ones[:, :], AG[:, t, :], start=(t == 0), stop=(t == T - 1))
            last.then_inc(bn_done, 1)
            pe.wait_ge(act_bn, 1)
            for t in range(T):
                n = P if t < T - 1 else LAST
                last = mm(B[5][:, 0:D], ones[0:n, :], SQ[0:n, t, :], start=(t == 0), stop=(t == T - 1))
            last.then_inc(bn_done, 1)

            def turn3(t, b):
                pe.wait_ge(n3_ready, t + 1)
                pe.wait_ge(t3_out, 2 * t + 2)
                for k in range(KT):
                    last = tr(B[b][:, P * k:P * k + P], ring_n[b][:, P * k:P * k + P], ident[:, :])
                last.then_inc(tp3_done, 1)

            def project3(t, b):
                pe.wait_ge(t3_out, 4 + 2 * t + 2)
                pe.wait_ge(h_out, t + 1)
                for k in range(KT):
                    last = mm(B[2 + b][:, 0:GH * NE], ring_t[b][:, k, :], Wg[:, k, :], start=(k == 0), stop=(k == KT - 1))
                last.then_inc(h_done, 1)
            tiles_ahead(pe, turn3, project3)

            pe.wait_ge(carry_go, 1)
            mm(B[6][:, 0:2 * P], ones[:, :], DG[:, 0:2, :].rearrange("p a b -> p (a b)"), start=True, stop=True).then_inc(carry_done, 1)

            def carry_scores():
                pe.wait_ge(carry_go, 2)
                mm(B[1][:, 0:GH], M2, small[:, 0:GH], start=True, stop=True).then_inc(carry_done, 1)
                for k in range(2):
                    pe.wait_ge(carry_go, 3 + k)
                    mm(B[6 + k][:, :], ones[:, :], DG.rearrange("p a b -> p (a b)"), start=True, stop=True).then_inc(carry_done, 1)

            def carry_sums():
                pe.wait_ge(carry_go, 5)
                mm(B[1][:, 32:32 + SUMS], M2, small[:, 32:32 + SUMS], start=True, stop=True).then_inc(carry_done, 1)

            pe.wait_ge(experts_in, 48)

            def first(g, e, tiles):
                n = P * tiles
                for m in range(EM):
                    pe.wait_ge(ehid_out, 16 * g + 4 * e + m + 1)
                    for k in range(KT):
                        last = mm(B[2 + m % 2][:, 0:n], EW1[:, e, k, P * m:P * m + P],
                                  X2T[:, k, ds(g * 512, n)], start=(k == 0), stop=(k == KT - 1))
                    last.then_inc(ep_done, 1)

            def second(g, e, tiles):
                w2 = EW2a[:, e, :, :] if e < 2 else EW2b[:, e - 2, :, :]
                pe.wait_ge(ehid_out, 2 + 16 * g + 4 * e + 4)
                for h in range(2 if tiles == 4 else 1):
                    n, b = (2 * e + h, h) if tiles == 4 else (e, e % 2)
                    pe.wait_ge(eo_out, 8 * g + n + 1)
                    for j in range(2 if tiles == 4 else 1):
                        for k in range(EM):
                            last = mm(B[4 + b][:, D * j:D * j + D], EHID[e % 2][:, k, P * (2 * h + j):P * (2 * h + j) + P],
                                      w2[:, k, :], start=(k == 0), stop=(k == EM - 1))
                    last.then_inc(eo_done, 1)

            def moe(g, tiles, between=(None, None)):
                first(g, 0, tiles)
                for e in range(NE):
                    if e + 1 < NE:
                        first(g, e + 1, tiles)
                    second(g, e, tiles)
                    if e < 2 and between[e]:
                        between[e]()
            with pe.Fori(0, GROUPS - 1) as g:
                moe(g, 4)
            moe(GROUPS - 1, 4, (carry_scores, carry_sums))
            moe(GROUPS, 1)

            pe.wait_ge(gates_ready, 1)

            def turn_gates(g):
                if g >= 2:
                    pe.wait_ge(gt_out, g - 1)
                for j in range(4 if g < GROUPS else 1):
                    last = tr(B[g % 2][0:NE, P * j:P * j + P], gates[:, 4 * g + j, :], ident[:, :])
                last.then_inc(gt_done, 1)
            turn_gates(0)
            for g in range(GROUPS + 1):
                if g < GROUPS:
                    turn_gates(g + 1)
                pe.wait_ge(gt_out, g + 1)
                if g >= 2:
                    pe.wait_ge(gb_added, g - 1)
                for j in range(4 if g < GROUPS else 1):
                    last = mm(B[2 + 2 * (g % 2) + j // 2][:, D * (j % 2):D * (j % 2) + D], gT[g % 2][:, P * j:P * j + P],
                              eb2[:, :], start=True, stop=True)
                last.then_inc(gb_done, 1)

        @block.vector
        def _(ve):
            v = Chain(ve, vec_step)
            ts, tt, stt, cp = ve.tensor_scalar, ve.tensor_tensor, ve.scalar_tensor_tensor, ve.tensor_copy
            red, scan = ve.tensor_reduce, ve.tensor_tensor_scan
            ve.sem_inc(proj_out, 2)
            ve.sem_inc(at_out, 2)
            ve.sem_inc(op_added, 2)
            ve.sem_inc(seg_added, 4)
            ve.sem_inc(h_out, 2)

            ve.wait_ge(consts, 10)
            v(ts(ident[:, :], iota_f[:, :], rowid[:, 0:1], None, ALU.is_equal))
            v(ts(tri[:, :], iota_f[:, :], rowid[:, 0:1], None, ALU.is_gt))
            v(ts(low[:, :], iota_f[:, :], rowid[:, 0:1], None, ALU.is_lt))
            ve.wait_ge(padded, 7)
            ts(SRC2I, flat_i[:, :], NP - 1, None, ALU.min).then_inc(padded2, 1)
            ts(DST2I, flat_i[:, :], NP - 1, None, ALU.min).then_inc(padded2, 1)

            def decode(sorted_i):
                v(ts(SRCSI[:, :], sorted_i, 12, None, ALU.arith_shift_right))
                v(cp(DSTS[:, :], SRCSI[:, :]))
                v(ts(SRCSI[:, :], sorted_i, 4095, None, ALU.bitwise_and))

            def floor_div(o, i, d):
                v(ts(o, i, 1.0 / d, 0.5 / d - 0.5, ALU.mult, ALU.add))
                v(ts(o, o, ROUND, ROUND, ALU.add, ALU.subtract))

            def positions(k, C, keys, group, tmp, part, pos, whole_pairs):
                v.apart(keys, keys // group, lambda i: ts(
                    onehot[:, ds(i * C, C)], K16[:, 0:C], iota_f[:, ds(i, 1)], None, ALU.is_equal))
                oh, cn = onehot[:, 0:keys * C], counts[:, 0:keys * C]
                v(scan(cn, oh, oh, 0.0, ALU.add, ALU.max))
                count, at_end, total, upto, start, shift = (cnts[:, i, 0:keys] for i in range(6))
                v(cp(at_end, cn.rearrange("p (k c) -> p k c", c=C)[:, :, C - 1]))
                v(cp(count[:, 0:1], at_end[:, 0:1]))
                tt(count[:, 1:keys], at_end[:, 1:keys], at_end[:, 0:keys - 1], ALU.subtract).then_inc(cnt_ready, 1)
                ve.wait_ge(pre_ready, k)
                v(cp(total, B[7][:, 64:64 + keys]))
                if whole_pairs:
                    v(ts(total, total, float(2 * P - 1), None, ALU.add))
                    floor_div(total, total, 2 * P)
                    v(ts(total, total, float(2 * P), None, ALU.mult))
                v(scan(upto, total, total, 0.0, ALU.add, ALU.max))
                v(tt(start, upto, total, ALU.subtract))
                v(tt(shift, start, B[7][:, 0:keys], ALU.add))
                v(tt(shift, shift, at_end, ALU.subtract))
                v(stt(shift, shift, -1.0, count, ALU.add, ALU.add))

                def some_keys(i):
                    for q in range(group):
                        key = i * group + q
                        v.go(stt(tmp[:, q * C:(q + 1) * C], counts[:, ds(key * C, C)], shift_of(key),
                                 onehot[:, ds(key * C, C)], ALU.add, ALU.mult))
                    v.join()
                    v(red(part[:, ds(i * C, C)], tmp[:, 0:group * C].rearrange("p (q c) -> p c q", c=C), AX.X, ALU.add))
                shift_of = lambda key: cnts[:, 5, ds(key, 1)]
                v.loop(keys // group, group + 1, some_keys)
                v(red(pos, part[:, 0:(keys // group) * C].rearrange("p (g c) -> p c g", c=C), AX.X, ALU.add))

            ve.wait_ge(edges1_in, 96)
            blk, lo = K0[:, 0:C1], K1[:, 0:C1]
            v(cp(lo, SRC))
            floor_div(blk, lo, P)
            v(cp(K16[:, :], blk))
            v(stt(REC[:, 0:C1, 1], blk, -float(P), lo, ALU.mult, ALU.add))
            v(cp(REC[:, 0:C1, 0], DST))
            v(cp(REC[:, 0:C1, 2], WT))
            ve.wait_ge(recs_zeroed, 16)
            pos = K2[:, 0:C1]
            positions(1, C1, T, 5, tmp_s, part_s, pos, True)
            chunk = K0[:, 0:C1]
            floor_div(chunk, pos, P)
            v(stt(K1[:, 0:C1], chunk, -float(P), pos, ALU.mult, ALU.add))
            stt(POSI[:, 0:C1], K1[:, 0:C1], float(CH), chunk, ALU.mult, ALU.add).then_inc(pos1_ready, 1)
            ends_before = K2[0:1, 0:CH // 2]
            v(ts(ends_before, jrow[0:1, :], cnts[0:1, 3, 0:1], None, ALU.is_ge))

            def block_ends(i):
                for q in range(6):
                    v(stt(ends_before, jrow[0:1, :], cnts[0:1, 3, ds(i * 6 + q + 1, 1)], ends_before, ALU.is_ge, ALU.add))
            v.loop((T - 1) // 6, 6, block_ends)
            v(ts(blk_i[0:1, :], ends_before, float(T - 1), None, ALU.min))

            ve.wait_ge(edges2_in, 96)
            v(cp(VAL[:, :], DST2I))
            v(cp(K1[:, 0:C2], SRC2I))
            v(stt(VAL[:, :], VAL[:, :], 4096.0, K1[:, 0:C2], ALU.mult, ALU.add))

            def statistics(src, m, k):
                v.apart(T, 5, lambda t: ve.bn_stats(st6[:, t, :], src[:, t, :]))
                mean, var = m[:, :, 0], m[:, :, 1]
                v(tt(mean, st6[:, :, 1], st6[:, :, 4], ALU.add))
                v(tt(st6[:, :, 1], st6[:, :, 1], st6[:, :, 4], ALU.subtract))
                v(stt(st6[:, :, 1], st6[:, :, 1], D / 4, st6[:, :, 1], ALU.mult, ALU.mult))
                v(tt(var, st6[:, :, 2], st6[:, :, 5], ALU.add))
                v(tt(var, var, st6[:, :, 1], ALU.add))
                v(ts(var, var, 1.0 / D, None, ALU.mult))
                v(ts(mean, mean, 0.5, None, ALU.mult))
                ve.sem_inc(stats_ready, 1)

            def reciprocal(k, r):
                ve.wait_ge(root_ready, k)
                v(ve.reciprocal(r, r))
            ve.wait_ge(x_in, 32)
            statistics(X, mv, 1)
            reciprocal(1, rstd[:, :])

            v.apart(T, 5, lambda t: ts(
                XN[:, t, :], X[:, t, :], mv[:, t, 0:1], rstd[:, ds(t, 1)], ALU.subtract, ALU.mult))
            statistics(XN, mv2, 2)
            reciprocal(2, rstd2[:, :])

            ve.wait_ge(weights_in, 16 * len(weights))
            for r, c in MINUS:
                w = WH[64 * (r % 2):64 * (r % 2) + 64, r // 2, 64 * c:64 * c + 64]
                v(ts(w, w, -1.0, None, ALU.mult))
            for k in range(KT):
                v(ts(bxb[:, k, :], ones[:, :], bxc[:, k:k + 1], None, ALU.mult))
            ve.sem_inc(signs, 1)
            ve.wait_ge(wc_ready, 1)
            for m in range(KT):
                cp(Wc[:, m, :], B[2 + m][:, 0:QKVN]).then_inc(wc_out, 1)
            cp(bc[:, :], B[4][:, 0:QKVN]).then_inc(wc_out, 1)
            ve.wait_ge(wc_out, 3)

            def center(t, b):
                ve.wait_ge(tp_done, t + 1)
                ts(ring_n[b][:, D:2 * D], XN[:, t, :], mv2[:, t, 0:1], rstd2[:, ds(t, 1)],
                   ALU.subtract, ALU.mult).then_inc(hh_ready, 1)

            def projected(t, b):
                ve.wait_ge(proj_done, 2 + t + 1)
                ve.wait_ge(sup_out[b], (t - b) * 8 + 16)
                cp(ring_s[b], B[2 + b][:, 0:D]).then_inc(sup_ready, 1)
                tt(QKV[:, t, :], B[4 + b][:, 0:QKVN], bc[:, :], ALU.add).then_inc(proj_out, 1)
            tiles_two_ahead(ve, center, projected)
            ve.wait_ge(proj_out, 2 + T)
            for b in range(2):
                ve.wait_ge(sup_out[b], 16 + 16 * ((T + 1 - b) // 2))

            q, kk = QKV[:, :, 0:QN], QKV[:, :, QN:2 * QN]
            kmax, ktail = small[:, 0:QN], small[:, 32:32 + QN]
            v(red(kmax, kk[:, 0:T - 1, :].rearrange("p t c -> p c t"), AX.X, ALU.max))
            v(tt(kmax[0:LAST, :], kmax[0:LAST, :], kk[0:LAST, T - 1, :], ALU.max))
            ve.sem_inc(kmax_in, 1)
            ve.wait_ge(kmax_out, 1)
            v(red(small[0:QN, 128:129], B[6][0:QN, 0:P], AX.X, ALU.max))
            v(ts(small[0:QN, 64:64 + QN], ident[0:QN, 0:QN], small[0:QN, 128:129], None, ALU.mult))
            ve.sem_inc(kmax_in, 1)
            ve.wait_ge(kmax_out, 2)
            v(cp(small[:, 32:32 + QN], B[7][:, 128:128 + QN]))
            tt(kk, kk, small[:, 32:32 + QN].unsqueeze(1).to_broadcast([P, T, QN]), ALU.subtract).then_inc(exp_go, 1)
            q4 = q.rearrange("p t (h r) -> p t h r", r=KR)
            K0q = K0[:, 0:T * HEADS].rearrange("p (t h) -> p t h", t=T)
            v(red(K0q, q4, AX.X, ALU.max))
            tt(q4, q4, K0q.unsqueeze(3).to_broadcast([P, T, HEADS, KR]), ALU.subtract).then_inc(exp_go, 1)
            ve.wait_ge(exp_done, 2)
            v(red(K0q, q4, AX.X, ALU.add))
            v(ve.reciprocal(K0[:, 0:T * HEADS], K0[:, 0:T * HEADS]))
            tt(q4, q4, K0q.unsqueeze(3).to_broadcast([P, T, HEADS, KR]), ALU.mult).then_inc(exp_go, 1)
            ve.wait_ge(kv_done, 1)
            v(ve.reciprocal(small[0:QN, 128:129], B[0][0:QN, 0:1]))
            stt(stat[0:QN, 0, :], B[6][0:QN, 0:D], small[0:QN, 128:129], hmask[:, :], ALU.mult, ALU.mult).then_inc(kv_out, 1)
            ve.wait_ge(kv_done, 2)
            cp(small[:, 96:96 + 2 * QN], B[4][:, 0:2 * QN]).then_inc(kv_out, 1)
            ve.wait_ge(kv_done, 3)
            cp(stat[0:QN, 1, :], B[5][0:QN, 0:D]).then_inc(kv_out, 1)

            v(tt(XN[:, :, :], XN[:, :, :], rowv[:, 0, :].unsqueeze(1).to_broadcast([P, T, D]), ALU.add))

            def attended(t, b):
                ve.wait_ge(at_done, 2 + t + 1)
                tt(XN[:, t, :], XN[:, t, :], B[2 + b][:, 0:D], ALU.add).then_inc(at_out, 1)
            tiles_in_pairs(ve, attended)
            ve.wait_ge(at_out, 2 + T)
            statistics(XN, mv, 3)
            reciprocal(3, rstd[:, :])

            def center2(g, b, tiles):
                for j in range(tiles):
                    t = 4 * g + j
                    ve.wait_ge(tp2_done, t + 1)
                    ts(ring_n[j % 2][:, 0:D], XN[:, t, :], mv[:, t, 0:1], rstd[:, ds(t, 1)],
                       ALU.subtract, ALU.mult).then_inc(n2_ready, 1)

            def count_edges(g):
                for j in range(HC):
                    ve.wait_ge(hist_used, g * HC + j + 1)
                    ts(of_place[j % 4], iota[:, 0:P], K0[:, ds(g * HC + j, 1)], None, ALU.is_equal)
                    ts(of_tile[j % 4], iota[:, 0:T], K1[:, ds(g * HC + j, 1)], None, ALU.is_equal).then_inc(hist_ready, 1)

            def mlp_added(g, b, tiles, ahead):
                if tiles == 4:
                    count_edges(g)
                ahead()
                for j in range(tiles):
                    t = 4 * g + j
                    tt(X[:, t, :], X[:, t, :], XN[:, t, :], ALU.add).then_inc(fx_added, 1)
                for j in range(tiles):
                    t = 4 * g + j
                    ve.wait_ge(fx_added, t + 1)
                    tt(X[:, t, :], X[:, t, :], rowv[:, 1, :], ALU.add).then_inc(bias_added, 1)
                for j in range(tiles):
                    t = 4 * g + j
                    ve.wait_ge(op_done, 8 + t + 1)
                    ve.wait_ge(bias_added, t + 1)
                    tt(X[:, t, :], X[:, t, :], B[4 + j % 2][:, 0:D], ALU.add).then_inc(op_added, 1)
            v(cp(KI[:, 0:C2], VAL[:, :]))
            decode(KI[:, 0:C2])
            floor_div(K1[:, 0:C2], DSTS[:, :], P)
            v(stt(K0[:, 0:C2], K1[:, 0:C2], -float(P), DSTS[:, :], ALU.mult, ALU.add))
            groups_ahead(ve, center2, mlp_added)
            ve.wait_ge(op_added, 2 + T)
            ve.sem_inc(x1_ready, 1)

            def column(k, c, s):
                ve.wait_ge(perm_used, c + (k * C2 + s + 1))
                ts(lhs[s % 4], iota[:, 0:P], K0[:, ds(c + s, 1)], None, ALU.is_equal)
                ts(rhs[s % 4], iota[:, 0:C2], K1[:, ds(c + s, 1)], VAL[:, ds(c + s, 1)],
                   ALU.is_equal, ALU.mult).then_inc(perm_ready, 1)

            ve.wait_ge(hist_used, 4 + C2)
            count, total, upto, end = (cnts[:, i, 0:T] for i in range(4))
            cp(count, B[6][:, 0:T]).then_inc(cnt_ready, 1)
            ve.wait_ge(pre_ready, 2)
            v(cp(total, B[7][:, 64:64 + T]))
            v(scan(upto, total, total, 0.0, ALU.add, ALU.max))
            v(tt(end, upto, total, ALU.subtract))
            v(tt(end, end, count, ALU.add))
            v(tt(end, end, B[7][:, 0:T], ALU.add))
            v(ts(end, end, -1.0, None, ALU.add))
            v(cp(endi[:, :], end))
            ve.sem_inc(ends_ready, 1)

            for k in range(2):
                hi = K0[:, 0:C2]
                floor_div(hi, DSTS[:, :], KEYS2)
                if k == 0:
                    v(stt(K16[:, 0:C2], hi, -float(KEYS2), DSTS[:, :], ALU.mult, ALU.add))
                else:
                    v(cp(K16[:, 0:C2], hi))
                positions(3 + k, C2, KEYS2, 3, tmp_2, part_2, K2[:, 0:C2], False)
                floor_div(K0[:, 0:C2], K2[:, 0:C2], C2)
                v(stt(K1[:, 0:C2], K0[:, 0:C2], -float(C2), K2[:, 0:C2], ALU.mult, ALU.add))
                if k == 0:
                    with ve.Fori(0, C2 // 8) as i:
                        for s in range(8):
                            column(0, i * 8, s)
                    ve.wait_ge(perm_used, 4 + C2)
                    v(cp(VAL[:, :], B[6][:, 0:C2]))
                    ve.sem_inc(perm_read, 1)
                    v(cp(KI[:, 0:C2], VAL[:, :]))
                    decode(KI[:, 0:C2])

            ve.wait_ge(recs_back, 16)
            v(cp(POSI[:, :], REC[:, 0:CH, 0]))
            ve.sem_inc(chunks_ready, 1)
            v(ve.memset(AG, 0.0))

            def weigh(j, s):
                ts(SW[s % 4], iota[:, 0:P], REC[:, ds(j, 1), 1], REC[:, ds(j, 1), 2],
                   ALU.is_equal, ALU.mult).then_inc(sw_ready, 1)

            def chunks(i, first=False, sort=True, count=16):
                _, at_block = nc.values_load_multi_w_load_instructions(
                    blk_i[0:1, ds(i * 8, count // 2)], engines=(mybir.EngineType.DVE,), min_val=0, max_val=T - 1)
                for s in range(count):
                    j = i * 16 + s
                    if not (first and s < 2):
                        ve.wait_ge(seg_done, j - 1)
                    weigh(j + 2, s + 2)
                    if s % 2:
                        pair = s // 2
                        ve.wait_ge(seg_done, j + 1)
                        ve.wait_ge(seg_added, i * 8 + pair + 4)
                        place = AG[:, ds(at_block[pair], 1), :].rearrange("p a d -> p (a d)")
                        tt(place, place, B[pair % 4][:, 0:D], ALU.add).then_inc(seg_added, 1)
                    if sort and s < SC2:
                        column(1, i * SC2, s)
            weigh(0, 0)
            weigh(1, 1)
            chunks(0, first=True)
            with ve.Fori(1, C2 // SC2) as i:
                chunks(i)
            with ve.Fori(C2 // SC2, TURNS) as i:
                chunks(i, sort=False)
            chunks(TURNS, sort=False, count=8)
            ve.wait_ge(seg_added, 4 + CH // 2)

            ve.wait_ge(perm_used, 4 + 2 * C2)
            v(cp(VAL[:, :], B[6][:, 0:C2]))
            v(cp(KI[:, 0:C2], VAL[:, :]))
            decode(KI[:, 0:C2])
            ve.sem_inc(idx2_ready, 1)
            ve.sem_inc(sorted2_ready, 1)
            first_, goes_on = (FLG[:, i, :] for i in range(2))

            ve.sem_inc(bn_go, 1)
            ve.wait_ge(bn_done, 1)
            v(ts(stat[:, 0, :], B[4][:, 0:D], 1.0 / N, None, ALU.mult))
            wide = lambda r: r.unsqueeze(1).to_broadcast([P, T, D])
            tt(AG, AG, wide(stat[:, 0, :]), ALU.subtract).then_inc(bn_go, 1)
            ve.wait_ge(act_bn, 2)
            v(ve.reciprocal(stat[:, 1, :], stat[:, 1, :]))
            v(tt(stat[:, 1, :], stat[:, 1, :], rowv[:, 2, :], ALU.mult))
            v(tt(AG, AG, wide(stat[:, 1, :]), ALU.mult))
            tt(AG, AG, wide(rowv[:, 3, :]), ALU.add).then_inc(bn_go, 1)
            ve.wait_ge(act_bn, 3)
            v(tt(X[:, :, :], X[:, :, :], AG, ALU.add))

            statistics(X, mv, 4)
            reciprocal(4, rstd[:, :])

            def center3(t, b):
                ve.wait_ge(tp3_done, t + 1)
                ts(ring_n[b][:, 0:D], X[:, t, :], mv[:, t, 0:1], rstd[:, ds(t, 1)],
                   ALU.subtract, ALU.mult).then_inc(n3_ready, 1)

            def h_read(t, b):
                ve.wait_ge(h_done, 2 + t + 1)
                cp(HT[:, t, 2 * GH:ROW2], B[2 + b][:, 0:GH * NE]).then_inc(h_out, 1)
            tiles_two_ahead(ve, center3, h_read)
            ve.wait_ge(h_out, 2 + T)
            small_w = lambda i: attn_w[:, i, :].unsqueeze(1).to_broadcast([P, T, GH * NE])
            by_head = lambda a: a.rearrange("p t (h e) -> p t h e", e=NE)
            for i in range(2):
                v(tt(nodes2, HT[:, :, 2 * GH:ROW2], small_w(i), ALU.mult))
                v(red(HT[:, :, GH * i:GH * i + GH], by_head(nodes2), AX.X, ALU.add))
            ve.sem_inc(tab2_ready, 1)
            ve.wait_ge(edge_in, 16)
            v(tt(first_[:, 1:C2], DSTS[:, 1:C2], DSTS[:, 0:C2 - 1], ALU.not_equal))
            v(tt(first_[:, 0:1], DSTS[:, 0:1], dedge[:, 0:1], ALU.not_equal))
            v(ts(goes_on, first_, -1.0, 1.0, ALU.mult, ALU.add))
            v(ve.memset(goes_on[:, 0:1], 1.0))

            v(ts(DG[:, 0, :], ident[:, :], DSTS[:, 0:1], None, ALU.mult))
            ts(DG[:, 1, :], ident[:, :], DSTS[:, C2 - 1:C2], None, ALU.mult).then_inc(carry_go, 1)
            ve.wait_ge(carry_done, 1)
            v(stt(M2, B[6][:, 0:P], DSTS[:, C2 - 1:C2], tri[:, :], ALU.is_equal, ALU.mult))
            v(stt(MADD[0], B[6][:, P:2 * P], DSTS[:, 0:1], low[:, :], ALU.is_equal, ALU.mult))
            v(ts(MADD[0], MADD[0], BIG, BIG, ALU.mult, ALU.subtract))
            v(ts(MADD[1], M2, BIG, BIG, ALU.mult, ALU.subtract))

            with ve.Fori(0, C2 // 16) as i:
                for h in range(2):
                    for s in range(8):
                        ve.wait_ge(slot[8 * h + s], i * 16 + slot2[8 * h + s] + 16)
                    cp(G[:, ds(i * 16 + 8 * h, 8), :].rearrange("p c f -> p (c f)"), ROWS2[h]).then_inc(g_copied, 1)
            ve.wait_ge(g_copied, 2 * (C2 // 16))

            for h in range(GH):
                v(tt(MB[:, :, h], G[:, :, GH + h], first_, ALU.mult))
                v(scan(AD[:, :, h], goes_on, MB[:, :, h], 0.0, ALU.mult, ALU.add))
            v(cp(small[:, 0:GH], AD[:, C2 - 1, :]))
            ve.sem_inc(carry_go, 1)
            ve.wait_ge(carry_done, 2)
            v(cp(small[:, 8:8 + GH], B[1][:, 0:GH]))
            for h in range(GH):
                v.go(scan(AD[:, :, h], goes_on, MB[:, :, h], small[:, 8 + h:9 + h], ALU.mult, ALU.add))
            v.join()
            bar = K2[:, 0:C2]
            v(ts(bar, goes_on, BIG, BIG, ALU.mult, ALU.subtract))
            bar_back = K1[:, 0:C2]
            v(ve.memset(bar_back[:, C2 - 1:C2], 0.0))
            v(cp(bar_back[:, 0:C2 - 1], bar[:, 1:C2]))

            def largest(k, into, edge, src, barrier):
                for h in range(GH):
                    v.go(scan(into(h), barrier, src(h), (-BIG if k is None else small[:, k + h:k + h + 1]), ALU.add, ALU.max))
                v.join()
            fwd = (lambda h: MF[:, :, h], lambda h: G[:, :, h], bar)
            back = (lambda h: MB[:, ::-1, h], lambda h: G[:, ::-1, h], bar_back[:, ::-1])
            for n, (into, src, barrier) in enumerate((fwd, back)):
                largest(None, into, None, src, barrier)
                edge = C2 - 1 if n == 0 else 0
                for h in range(GH):
                    v.go(ts(DG[:, h, :], ident[:, :], (MF, MB)[n][:, edge, h:h + 1], None, ALU.mult))
                v.join()
                ve.sem_inc(carry_go, 1)
                ve.wait_ge(carry_done, 3 + n)
                v(tt(crows, B[6 + n][:, :].rearrange("p (h q) -> p h q", h=GH),
                     MADD[n].unsqueeze(1).to_broadcast([P, GH, P]), ALU.add))
                v(red(small[:, 16 + 4 * n:20 + 4 * n], crows, AX.X, ALU.max))
                largest(16 + 4 * n, into, None, src, barrier)
            v(tt(MF, MF, MB, ALU.max))
            v(tt(MF, MF, AD, ALU.add))
            v(stt(MB, MF, 0.2, MF, ALU.mult, ALU.max))
            v(tt(AD, AD, G[:, :, 0:GH], ALU.add))
            v(stt(MF, AD, 0.2, AD, ALU.mult, ALU.max))
            tt(MF, MF, MB, ALU.subtract).then_inc(esc_go, 1)
            ve.wait_ge(esc_done, 1)
            ee = G[:, :, GH:2 * GH]
            for h in range(GH):
                m = G[:, :, 2 * GH + NE * h:2 * GH + NE * h + NE]
                v.go(tt(m, m, ee[:, :, h:h + 1].to_broadcast([P, C2, NE]), ALU.mult))
            v.join()
            for f in range(SUMS):
                v.go(scan(G[:, :, GH + f], goes_on, G[:, :, GH + f], 0.0, ALU.mult, ALU.add))
            v.join()
            v(cp(small[:, 32:32 + SUMS], G[:, C2 - 1, GH:ROW2]))
            ve.sem_inc(carry_go, 1)
            held = bar
            v(scan(held, goes_on, goes_on, 1.0, ALU.mult, ALU.mult))
            ve.wait_ge(carry_done, 5)
            v(cp(small[:, 64:64 + SUMS], B[1][:, 32:32 + SUMS]))
            for f in range(SUMS):
                v.go(stt(G[:, :, GH + f], held, small[:, 64 + f:65 + f], G[:, :, GH + f], ALU.mult, ALU.add))
            v.join()
            ve.sem_inc(sums_ready, 1)

            ve.wait_ge(nodes_in, 16 * T)
            den, msg = nodes[:, :, GH:2 * GH], nodes[:, :, 2 * GH:ROW2]
            v(ts(den, den, 1e-16, None, ALU.add))
            v(cp(small[:, 0:T * GH].rearrange("p (t h) -> p t h", t=T), den))
            v(ve.reciprocal(small[:, 0:T * GH], small[:, 0:T * GH]))
            inv = small[:, 0:T * GH].rearrange("p (t h) -> p t h", t=T)
            v(tt(by_head(nodes2), by_head(msg), inv.unsqueeze(3).to_broadcast([P, T, GH, NE]), ALU.mult))
            v(tt(nodes2, nodes2, small_w(2), ALU.add))
            v(red(gstat[:, :, 0], nodes2, AX.X, ALU.add))
            v(ts(gstat[:, :, 0], gstat[:, :, 0], 1.0 / (GH * NE), None, ALU.mult))
            v(tt(nodes2, nodes2, gstat[:, :, 0:1].to_broadcast([P, T, GH * NE]), ALU.subtract))
            v(tt(nodes3, nodes2, nodes2, ALU.mult))
            v(red(gstat[:, :, 1], nodes3, AX.X, ALU.add))
            v(ts(gstat[:, :, 1], gstat[:, :, 1], 1.0 / (GH * NE), None, ALU.mult))
            ve.sem_inc(stats_ready, 1)
            ve.wait_ge(root_ready, 5)
            v(cp(small[:, 128:128 + T], gstat[:, :, 1]))
            v(ve.reciprocal(small[:, 128:128 + T], small[:, 128:128 + T]))
            v(tt(nodes2, nodes2, small[:, 128:128 + T].unsqueeze(2).to_broadcast([P, T, GH * NE]), ALU.mult))
            v(tt(nodes2, nodes2, small_w(3), ALU.mult))
            v(tt(nodes2, nodes2, small_w(4), ALU.add))
            v(red(gates[:, :, :], nodes2.rearrange("p t (h e) -> p t e h", e=NE), AX.X, ALU.add))
            v(ts(gates[:, :, :], gates[:, :, :], 1.0 / GH, None, ALU.mult))
            for e in range(NE):
                me = gates[:, :, e:e + 1]
                if e:
                    v(tt(nodes3[:, :, 0:e], gates[:, :, 0:e], me.to_broadcast([P, T, e]), ALU.is_ge))
                v(ve.memset(nodes3[:, :, e:e + 1], 0.0))
                if e + 1 < NE:
                    v(tt(nodes3[:, :, e + 1:NE], gates[:, :, e + 1:NE], me.to_broadcast([P, T, NE - 1 - e]), ALU.is_gt))
                v(red(nodes3[:, :, 4 + e], nodes3[:, :, 0:NE], AX.X, ALU.add))
            v(ts(nodes3[:, :, 4:8], nodes3[:, :, 4:8], 1.5, None, ALU.is_lt))
            v(red(gstat[:, :, 0], gates[:, :, :], AX.X, ALU.max))
            tt(gates[:, :, :], gates[:, :, :], gstat[:, :, 0:1].to_broadcast([P, T, NE]), ALU.subtract).then_inc(gate_go, 1)
            ve.wait_ge(gate_done, 1)
            v(tt(gates[:, :, :], rank[:, :, :], nodes3[:, :, 4:8], ALU.mult))
            v(red(gstat[:, :, 0], gates[:, :, :], AX.X, ALU.add))
            v(cp(small[:, 0:T], gstat[:, :, 0]))
            v(ve.reciprocal(small[:, 0:T], small[:, 0:T]))
            v(tt(gates[:, :, :], gates[:, :, :], small[:, 0:T].unsqueeze(2).to_broadcast([P, T, NE]), ALU.mult))

            ve.sem_inc(gates_ready, 1)

            for g in range(GROUPS + 1):
                ve.wait_ge(y_in[g], 16 * NE)
                for e in range(NE):
                    for j in range(4 if g < GROUPS else 1):
                        t = 4 * g + j
                        v.go(stt(X[:, t, :], Y[g][:, e, j, :], gates[:, t, e:e + 1], X[:, t, :], ALU.mult, ALU.add))
                    v.join()
                ve.wait_ge(gb_done, g + 1)
                for k in range(2 if g < GROUPS else 1):
                    tiles = X[:, 4 * g + 2 * k:min(T, 4 * g + 2 * k + 2), :].rearrange("p t d -> p (t d)")
                    v.go(tt(tiles, tiles, B[2 + 2 * (g % 2) + k][:, 0:(2 * D if g < GROUPS else D)], ALU.add))
                v.join()
                ve.sem_inc(gb_added, 1)
                ve.sem_inc(combined, 1)


def kernel(**inputs):
    import numpy as np
    import concourse.bacc as bacc
    from concourse.bass_utils import run_bass_kernel_spmd

    nc = bacc.Bacc("TRN2", target_bir_lowering=False, num_devices=1)
    arrays, args = {}, {}
    for name in LOADS:
        a = np.ascontiguousarray(inputs[name])
        arrays[f"in_{name}"] = a
        args[name] = nc.dram_tensor(f"in_{name}", a.shape, mybir.dt.from_np(a.dtype), kind="ExternalInput").ap()
    out = nc.dram_tensor("out_0", (N, D), F32, kind="ExternalOutput").ap()
    build(nc, args, out)
    r = run_bass_kernel_spmd(nc, [arrays], core_ids=[0])
    return r.results[0]["out_0"]
```

```python
from contextlib import ExitStack

import concourse.bass as bass
from concourse import mybir
from concourse.alu_op_type import AluOpType as ALU

ACT = mybir.ActivationFunctionType
AX = mybir.AxisListType
F32, F16, I32, U32 = mybir.dt.float32, mybir.dt.float16, mybir.dt.int32, mybir.dt.uint32
ds = bass.ds

P = 128
N, D = 3125, 256
T = 25
LAST = N - (T - 1) * P
NP = T * P
KT = D // P
EPS = 1e-5
E1, C1 = 50000, 392
FULL1, REST1 = E1 // C1, E1 % C1
CH = 2 * ((P * C1 + T * (2 * P - 1)) // (2 * P))
TURNS = CH // 16
LC = 28
E2, C2 = 32768, 288
KEYS2 = 57
HEADS, DH, KR = 8, 32, 4
QN = HEADS * KR
QKVN = 2 * QN + D
FF = 1024
FM = FF // P
NE, FE = 4, 512
EM = FE // P
GH = 4
ROW2 = 2 * GH + GH * NE
SUMS = GH + GH * NE
PART = 5
PARTS_N = T // PART
GROUPS = T // 4
SC2 = 24
PT = C2 // SC2
assert CH // 16 == 2 * PT + 3
PASS_AT = (1, PT + 3)
HC = C2 // GROUPS
BIG = 1.0e30
ROUND = 12582912.0

LOADS = ["x", "src", "dst", "edge_weight", "L0_gnn_weight", "L0_gnn_gamma", "L0_gnn_beta", "L0_mix_ln1_g",
         "L0_mix_ln1_b", "L0_mix_Wx", "L0_mix_bx", "L0_mix_Wq", "L0_mix_Wk", "L0_mix_Wv", "L0_mix_Wo",
         "L0_mix_bo", "L0_mix_ln2_g", "L0_mix_ln2_b", "L0_mix_W1", "L0_mix_b1", "L0_mix_W2", "L0_mix_b2",
         "L0_ffn_W_gat", "L0_ffn_att_src", "L0_ffn_att_dst", "L0_ffn_b_gat", "L0_ffn_ln_gamma",
         "L0_ffn_ln_beta", "L0_ffn_W1", "L0_ffn_b1", "L0_ffn_W2", "L0_ffn_b2", "L0_ffn_edge_index"]


class Chain:

    def __init__(self, eng, sem):
        self.eng, self.sem, self.n = eng, sem, 0

    def __call__(self, ins):
        ins.then_inc(self.sem, 1)
        self.n = self.n + 1
        self.eng.wait_ge(self.sem, self.n)

    def go(self, ins):
        ins.then_inc(self.sem, 1)
        self.n = self.n + 1

    def join(self):
        self.eng.wait_ge(self.sem, self.n)

    def apart(self, count, at_once, step):
        with self.eng.Fori(0, count // at_once) as i:
            for q in range(at_once):
                step(i * at_once + q).then_inc(self.sem, 1)
        self.n = self.n + count
        self.join()

    def loop(self, count, per, body):
        base = self.n
        with self.eng.Fori(0, count) as i:
            self.n = base + i * per
            body(i)
        self.n = base + count * per


def columns_at(s):
    return (3 * (s // 2), 3 * (s // 2) + 1) if s % 2 == 0 else (3 * (s // 2) + 2,)


def tiles_in_pairs(eng, work):
    with eng.Fori(0, T // 2) as i:
        work(2 * i, 0)
        work(2 * i + 1, 1)
    work(T - 1, 0)


def tiles_ahead(eng, ahead, work):
    ahead(0, 0)
    with eng.Fori(0, T // 2) as i:
        ahead(2 * i + 1, 1)
        work(2 * i, 0)
        ahead(2 * i + 2, 0)
        work(2 * i + 1, 1)
    work(T - 1, 0)


def tiles_two_ahead(eng, ahead, work):
    ahead(0, 0)
    ahead(1, 1)
    with eng.Fori(0, (T - 3) // 2) as i:
        ahead(2 * i + 2, 0)
        work(2 * i, 0)
        ahead(2 * i + 3, 1)
        work(2 * i + 1, 1)
    ahead(T - 1, 0)
    for t in range(T - 3, T):
        work(t, (t - T + 1) % 2)


def groups_ahead(eng, ahead, work):
    ahead(0, 0, 4)

    def turn(g, b, tiles):
        work(g, b, tiles, lambda: ahead(g + 1, 1 - b, 4))
    turn(0, 0, 4)
    turn(1, 1, 4)
    with eng.Fori(1, 2) as i:
        turn(2 * i, 0, 4)
        turn(2 * i + 1, 1, 4)
    turn(4, 0, 4)
    work(5, 1, 4, lambda: ahead(6, 0, 1))
    work(6, 0, 1, lambda: None)


def build(nc, A, out):
    with ExitStack() as ctx:
        def sb(name, shape, dt=F32):
            return ctx.enter_context(nc.sbuf_tensor(name, shape, dt))

        def sem(name):
            return ctx.enter_context(nc.semaphore(name))

        X = sb("X", [P, T, D])
        XN = sb("XN", [P, T, D])
        RQ = sb("RQ", [P, KEYS2 * C2 // 2])
        RR = sb("RR", [P, 11232])
        RT = sb("RT", [P, 6400])

        def cut(region, start, *shape):
            size = 1
            for s in shape:
                size *= s
            v = region[:, start:start + size]
            if len(shape) == 2:
                return v.rearrange("p (a b) -> p a b", a=shape[0])
            if len(shape) == 3:
                return v.rearrange("p (a b c) -> p a b c", a=shape[0], b=shape[1])
            return v

        xn_flat = XN[:, :, :].rearrange("p t d -> p (t d)")
        onehot = RQ[:, :].bitcast(F16)
        at = C1 * T // 2
        Wx = cut(RQ, at, KT, D); at += KT * D
        WxT = cut(RQ, at, KT, D); at += KT * D
        BD = cut(RQ, at, KT, QKVN); at += KT * QKVN
        bxb = cut(RQ, at, KT, P); at += KT * P
        SRC = cut(RQ, at, C1).bitcast(I32); at += C1
        DST = cut(RQ, at, C1).bitcast(I32); at += C1
        WT = cut(RQ, at, C1)
        QKV = cut(RQ, 0, T, QKVN)
        AG = XN[:, :, :]
        X2T = XN[:, :, :].rearrange("p t d -> p (t d)").rearrange("p (k n) -> p k n", k=KT)
        of_place = [cut(RQ, 64 * s, 64).bitcast(F16) for s in range(8)]
        of_tile = [cut(RQ, 512 + 16 * s, 16).bitcast(F16)[:, 0:T] for s in range(8)]
        EW1 = cut(RQ, 0, NE, KT * FE).rearrange("p e (k n) -> p e k n", k=KT)
        EW2 = cut(RQ, NE * KT * FE, NE, EM * D).rearrange("p e (k n) -> p e k n", k=EM)
        counts = RR[:, 0:KEYS2 * C2 // 2].bitcast(F16)
        SRC2I = cut(RR, 5000, C2).bitcast(I32)
        DST2I = cut(RR, 5300, C2).bitcast(I32)
        jrow = cut(RR, 5600, CH // 2)
        W1s = cut(RR, 0, KT, FF)
        HID = [cut(RR, 2048 + 4096 * b, FM, 512) for b in range(2)]
        SQ = cut(RR, 0, T, D)
        G = cut(RR, 0, C2, ROW2)
        MF, MB, AD = (cut(RR, C2 * (ROW2 + GH * i), C2, GH) for i in range(3))
        FLG = cut(RR, C2 * (ROW2 + 3 * GH), 2, C2)
        nodes = cut(RR, 0, T, ROW2)
        nodes2 = cut(RR, T * ROW2, T, GH * NE)
        nodes3 = cut(RR, T * (ROW2 + GH * NE), T, GH * NE)
        tmp_s = RT[:, 0:13 * C1]
        tmp_2 = RR[:, KEYS2 * C2 // 2:KEYS2 * C2 // 2 + 10 * C2]
        stat = cut(RT, 0, 3, D)
        ring_s = [cut(RT, 768 + D * b, D) for b in range(2)]
        lhs = [cut(RR, 9408 + P * s, P) for s in range(6)]
        rhs = [cut(RT, 4608 + C2 * s, C2) for s in range(6)]
        ROWS = [cut(RT, D * s, D) for s in range(16)]
        SW = [cut(RT, 4096 + P * r, P) for r in range(4)]
        H2T = [cut(RT, 1280 + 1024 * b, KT, 512) for b in range(2)]
        W2s = cut(RT, 3328, FM, D)
        ROWS2 = [cut(RT, 8 * ROW2 * h, 8 * ROW2) for h in range(2)]
        EHID = [cut(RT, 16 * ROW2 + 2048 * b, EM, 512) for b in range(2)]
        crows = cut(RT, 16 * ROW2 + 4096, GH, P)

        iota = sb("iota", [P, 512], F16)
        iota_f = sb("iota_f", [P, P])
        flat_i = sb("flat_i", [P, C2], I32)
        rowid = sb("rowid", [P, 1])
        ident = sb("ident", [P, P])
        tri = sb("tri", [P, P])
        low = sb("low", [P, P])
        ones = sb("ones", [P, P])
        epsc = sb("epsc", [P, 1])
        hmask = sb("hmask", [QN, D])
        st6 = sb("st6", [P, T, 6])
        mv = sb("mv", [P, T, 2])
        rstd = sb("rstd", [P, T])
        mv2 = sb("mv2", [P, T, 2])
        rstd2 = sb("rstd2", [P, T])
        ring_n = [sb(f"ring_n{b}", [P, 2 * D]) for b in range(2)]
        ring_t = [sb(f"ring_t{b}", [P, 4, P]) for b in range(2)]
        g1, b1, g2, b2, bxc = (sb(n, [P, KT]) for n in ("g1", "b1", "g2", "b2", "bxc"))
        fb1 = sb("fb1", [P, FM])
        eb1 = sb("eb1", [P, NE, EM])
        rowv = sb("rowv", [P, 4, D])
        eb2 = sb("eb2", [NE, D])
        Wo, WH = sb("Wo", [P, KT, D]), sb("WH", [P, KT, D])
        Wc, bc = sb("Wc", [P, KT, QKVN]), sb("bc", [P, QKVN])
        Wg = sb("Wg", [P, KT, GH * NE])
        attn_w = sb("attn_w", [P, 5, GH * NE])
        RS = sb("RS", [P, 2048])
        REC = cut(RS, 0, CH + 16, 4)
        diag = [cut(xn_flat, NE * 4 * D + 8 * P * b, 2, 4 * P).rearrange("p e (t n) -> p e t n", t=4) for b in range(2)]
        gT = [RS[0:NE, 512 * b:512 * b + 512] for b in range(2)]
        M2 = cut(RS, 0, P)
        MADD = [cut(RS, P * (1 + i), P) for i in range(2)]
        DG = cut(RS, 3 * P, GH, P)
        HT = cut(RS, 7 * P, T, ROW2)
        DG2 = cut(RS, 7 * P + T * ROW2, GH, P)
        K0, K1, K2 = sb("K0", [P, CH]), sb("K1", [P, CH]), sb("K2", [P, CH])
        K16 = sb("K16", [P, C1], F16)
        KI = sb("KI", [P, C2], I32)
        POSI = sb("POSI", [P, CH], I32)
        VAL = sb("VAL", [P, C2])
        cnts = sb("cnts", [P, 6, 64])
        blk_i = sb("blk_i", [P, CH // 2], I32)
        st_idx = [sb(f"st_idx{h}", [P, LC // 2], I32) for h in range(2)]
        st_rec = [sb(f"st_rec{h}", [P, LC // 2 * 4]) for h in range(2)]
        turnstile = sb("turnstile", [P, 1])
        DSTS = sb("DSTS", [P, C2])
        SRCSI = sb("SRCSI", [P, C2], I32)
        dedge = sb("dedge", [P, 1])
        endi = sb("endi", [P, T], I32)
        small = sb("small", [P, 256])
        gates = sb("gates", [P, T, NE])
        rank = sb("rank", [P, T, NE])
        gstat = sb("gstat", [P, T, 2])

        y_ring = [ring_n[0][:, :], ring_n[1][:, :]] + [r[:, :, :].rearrange("p a b -> p (a b)") for r in ring_t]
        y_of = lambda region, start, tiles: region[:, start:start + NE * tiles * D].rearrange(
            "p (e t d) -> p e t d", e=NE, t=tiles)
        Y = [y_of(RR, 1600, 4), y_of(RR, 1600 + NE * 4 * D, 4), y_of(RQ, 0, 4), y_of(RQ, NE * 4 * D, 4),
             y_of(xn_flat, 0, 4), y_of(RT, 0, 4), y_of(RT, NE * 4 * D, 1)]

        B = [ctx.enter_context(nc.psum_tensor(f"bank{i}", [P, 512], F32)) for i in range(8)]

        table1 = nc.dram_tensor("table1", [NP, D], F32, kind="Internal").ap()
        recs = nc.dram_tensor("recs", [P * CH, 4], F32, kind="Internal").ap()
        table2 = nc.dram_tensor("table2", [NP, ROW2], F32, kind="Internal").ap()
        sums2 = nc.dram_tensor("sums2", [P * C2, ROW2], F32, kind="Internal").ap()

        y_dram = nc.dram_tensor("y_dram", [NE, NP, D], F32, kind="Internal").ap()

        (consts, padded, padded2, x_in, edges1_in, edges2_in, recs_zeroed, bd_zeroed, weights_in, signs,
         vec_step, stats_ready, root_ready, cnt_ready, pre_ready, pos1_ready, wxt_ready, wxt_out, wc_ready,
         wc_out, hh_ready, xr_ready, tp_done, t_out, proj_done, proj_out, sup_ready, mlp_in, recs_back,
         kmax_in, kmax_out, exp_go, exp_done, kv_done, kv_out, qc_ready, qt_done, qt_out, at_done, at_out,
         n2_ready, tp2_done, t2_out, hp_done, hid_out, op_done, fx_added, bias_added, op_added, perm_ready, perm_used, hist_ready, hist_used,
         perm_read, sorted2_ready, edge_in, idx2_ready, ends_ready, chunks_ready, staged, sw_ready, seg_done,
         seg_added, bn_go, bn_done, act_bn, experts_in, n3_ready, tp3_done, t3_out, h_done, h_out,
         tab2_ready, tab2_out, g_copied, carry_go, carry_done, esc_go, esc_done, sums_ready, sums_out,
         nodes_in, gate_go, gate_done, ep_done, ehid_out, eo_done, eo_out, gates_ready, gt_done, gt_out, diag_ready, gb_done, gb_added, combined, out_done) = (
            sem(n) for n in (
                "consts padded padded2 x_in edges1_in edges2_in recs_zeroed bd_zeroed weights_in signs "
                "vec_step stats_ready root_ready cnt_ready pre_ready pos1_ready wxt_ready wxt_out wc_ready "
                "wc_out hh_ready xr_ready tp_done t_out proj_done proj_out sup_ready mlp_in recs_back "
                "kmax_in kmax_out exp_go exp_done kv_done kv_out qc_ready qt_done qt_out at_done at_out "
                "n2_ready tp2_done t2_out hp_done hid_out op_done fx_added bias_added op_added perm_ready perm_used hist_ready hist_used "
                "perm_read sorted2_ready edge_in idx2_ready ends_ready chunks_ready staged sw_ready seg_done "
                "seg_added bn_go bn_done act_bn experts_in n3_ready tp3_done t3_out h_done h_out "
                "tab2_ready tab2_out g_copied carry_go carry_done esc_go esc_done sums_ready sums_out "
                "nodes_in gate_go gate_done ep_done ehid_out eo_done eo_out gates_ready gt_done gt_out diag_ready gb_done gb_added combined out_done").split())
        sup_out = [sem(f"sup_out{b}") for b in range(2)]
        y_out = [sem(f"y_out{i}") for i in range(4)]
        y_in = [sem(f"y_in{g}") for g in range(GROUPS + 1)]
        scattered = [sem(f"scattered{h}") for h in range(2)]
        slot = [sem(f"slot{i}") for i in range(16)]
        slot2 = [16 * (TURNS + (s < 8)) for s in range(16)]
        N_CONSTS = 10

        col = lambda v, k: v.rearrange("(k p) -> p k", k=k)
        weights = [(g1[:, :], col(A["L0_mix_ln1_g"], KT)), (b1[:, :], col(A["L0_mix_ln1_b"], KT)),
                   (g2[:, :], col(A["L0_mix_ln2_g"], KT)), (b2[:, :], col(A["L0_mix_ln2_b"], KT)),
                   (bxc[:, :], col(A["L0_mix_bx"], KT)), (fb1[:, :], col(A["L0_mix_b1"], FM)),
                   (Wx, A["L0_mix_Wx"].rearrange("(k p) n -> p k n", p=P)),
                   (Wo[:, :, :], A["L0_mix_Wo"].rearrange("(k p) n -> p k n", p=P)),
                   (Wg[:, :, :], A["L0_ffn_W_gat"].rearrange("(k p) n -> p k n", p=P))]
        weights += [(rowv[:, i, :], A[n].partition_broadcast(P))
                    for i, n in enumerate(("L0_mix_bo", "L0_mix_b2", "L0_gnn_gamma", "L0_gnn_beta"))]
        weights.append((eb2[:, :], A["L0_ffn_b2"]))
        for e in range(NE):
            weights.append((eb1[:, e, :], col(A["L0_ffn_b1"][e, :], EM)))
        weights += [(attn_w[:, i, :], A[n].rearrange("h e -> (h e)").partition_broadcast(P))
                    for i, n in enumerate(("L0_ffn_att_src", "L0_ffn_att_dst"))]
        weights += [(attn_w[:, 2 + i, :], A[n].partition_broadcast(P))
                    for i, n in enumerate(("L0_ffn_b_gat", "L0_ffn_ln_gamma", "L0_ffn_ln_beta"))]
        for h in range(HEADS):
            k, q = h // 4, DH * (h % 4)
            weights.append((BD[q:q + DH, k, KR * h:KR * h + KR], A["L0_mix_Wq"]))
            weights.append((BD[q:q + DH, k, QN + KR * h:QN + KR * h + KR], A["L0_mix_Wk"]))
            weights.append((BD[q:q + DH, k, 2 * QN + DH * h:2 * QN + DH * h + DH], A["L0_mix_Wv"]))
        PARTS = ((0, 1, 2, 3), (1, 0, 3, 2), (2, 3, 0, 1), (3, 2, 1, 0))
        MINUS = ((1, 0), (2, 0), (3, 0), (1, 3), (2, 1), (3, 2))
        for r in range(4):
            for c in range(4):
                weights.append((WH[64 * (r % 2):64 * (r % 2) + 64, r // 2, 64 * c:64 * c + 64],
                                A["L0_gnn_weight"][:, 64 * PARTS[r][c]:64 * PARTS[r][c] + 64]))

        def load_y(eng, g):
            tiles = 4 if g < GROUPS else 1
            for e in range(NE):
                eng.dma_start(Y[g][:, e, :, :], y_dram[e, g * 512:g * 512 + tiles * P, :].rearrange(
                    "(t p) d -> p t d", p=P)).then_inc(y_in[g], 16)

        block = ctx.enter_context(nc.Block())

        @block.sync
        def _(sp):
            for b in range(2):
                sp.sem_inc(sup_out[b], 16)
            for s in range(4):
                sp.sem_inc(y_out[s], 16)
            sp.wait_ge(padded, 7)
            sp.dma_start(recs.rearrange("(p c) f -> p (c f)", p=P), RT[:, 0:CH * 4]).then_inc(recs_zeroed, 16)
            for name, tile in (("src", SRC), ("dst", DST), ("edge_weight", WT)):
                a = A[name]
                sp.dma_start(tile[0:FULL1, :], a[0:FULL1 * C1].rearrange("(p c) -> p c", c=C1)).then_inc(edges1_in, 16)
                sp.dma_start(tile[FULL1:FULL1 + 1, 0:REST1],
                             a[FULL1 * C1:E1].rearrange("(p c) -> p c", p=1)).then_inc(edges1_in, 16)
            x = A["x"]
            sp.dma_start(X[:, 0:T - 1, :], x[0:(T - 1) * P, :].rearrange("(t p) d -> p t d", p=P)).then_inc(x_in, 16)
            sp.dma_start(X[0:LAST, T - 1, :], x[(T - 1) * P:N, :]).then_inc(x_in, 16)
            sp.wait_ge(padded2, 2)
            p0, c0 = NP // C2, NP % C2
            head = C2 - c0
            full = (E2 - head) // C2
            rest = E2 - head - full * C2
            for r, tile in ((0, SRC2I), (1, DST2I)):
                e = A["L0_ffn_edge_index"][r:r + 1, :]
                sp.dma_start(tile[p0:p0 + 1, c0:C2], e[:, 0:head]).then_inc(edges2_in, 16)
                sp.dma_start(tile[p0 + 1:p0 + 1 + full, :],
                             e[:, head:head + full * C2].rearrange("a (p c) -> (a p) c", c=C2)).then_inc(edges2_in, 16)
                sp.dma_start(tile[p0 + 1 + full:p0 + 2 + full, 0:rest], e[:, E2 - rest:E2]).then_inc(edges2_in, 16)

            def store(t, b):
                sp.wait_ge(sup_ready, t + 1)
                sp.dma_start(table1[ds(t * P, P), :], ring_s[b]).then_inc(sup_out[b], 16)
            tiles_in_pairs(sp, store)
            sp.dma_start(W1s, A["L0_mix_W1"].rearrange("(k p) n -> p k n", p=P)).then_inc(mlp_in, 16)
            sp.dma_start(W2s, A["L0_mix_W2"].rearrange("(k p) n -> p k n", p=P)).then_inc(mlp_in, 16)
            for h in range(2):
                sp.wait_ge(scattered[h], 16 * C1 // 2)
            sp.dma_start(REC[:, 0:CH, :], recs.rearrange("(p c) f -> p c f", p=P)).then_inc(recs_back, 16)
            sp.wait_ge(sorted2_ready, 1)
            sp.dma_start(dedge[1:P, 0:1], DSTS[0:P - 1, C2 - 1:C2]).then_inc(edge_in, 16)
            sp.wait_ge(seg_added, 4 + CH // 2)
            sp.dma_start(EW1, A["L0_ffn_W1"].rearrange("e (k p) n -> p e k n", p=P)).then_inc(experts_in, 16)
            sp.dma_start(EW2, A["L0_ffn_W2"].rearrange("e (k p) n -> p e k n", p=P)).then_inc(experts_in, 16)
            sp.wait_ge(tab2_ready, 1)
            sp.dma_start(table2.rearrange("(t p) f -> p t f", p=P), HT).then_inc(tab2_out, 16)

            with sp.Fori(0, GROUPS) as g:
                for e in range(NE):
                    for h in range(2):
                        sp.wait_ge(eo_out, g * 8 + (2 + 2 * e + h + 1))
                        sp.dma_start(y_dram[e, ds((4 * g + 2 * h) * P, 2 * P), :].rearrange("(t p) d -> p t d", p=P),
                                     y_ring[(2 * e + h) % 4].rearrange("p (t d) -> p t d", t=2)).then_inc(y_out[(2 * e + h) % 4], 16)
            for e in range(NE):
                sp.wait_ge(eo_out, 2 + 8 * GROUPS + e + 1)
                sp.dma_start(y_dram[e, (T - 1) * P:NP, :], y_ring[e][:, 0:D]).then_inc(y_out[e], 16)
            for s in range(4):
                sp.wait_ge(y_out[s], 16 + 16 * (2 * GROUPS + 1))
            sp.wait_ge(sums_out, 16)
            for g in range(2, GROUPS + 1):
                load_y(sp, g)
            for g in range(GROUPS):
                sp.wait_ge(combined, g + 1)
                sp.dma_start(out[g * 512:(g + 1) * 512, :].rearrange("(t p) d -> p t d", p=P),
                             X[:, 4 * g:4 * g + 4, :]).then_inc(out_done, 16)
            sp.wait_ge(combined, GROUPS + 1)
            sp.dma_start(out[(T - 1) * P:N, :], X[0:LAST, T - 1, :]).then_inc(out_done, 16)
            sp.wait_ge(out_done, 16 * (GROUPS + 1))

        @block.gpsimd
        def _(gp):
            gp.memset(RT[:, 0:CH * 4], 0.0).then_inc(padded, 1)
            gp.memset(SRC, 0).then_inc(padded, 1)
            gp.memset(DST, 0).then_inc(padded, 1)
            gp.memset(WT, 0.0).then_inc(padded, 1)
            gp.memset(X[:, T - 1, :], 0.0).then_inc(padded, 1)
            gp.memset(REC[:, :, :], 0.0).then_inc(padded, 1)
            gp.iota(flat_i[:, :], pattern=[[1, C2]], base=0, channel_multiplier=C2).then_inc(padded, 1)
            gp.iota(iota[:, :], pattern=[[1, 512]], base=0, channel_multiplier=0,
                    allow_small_or_imprecise_dtypes=True).then_inc(consts, 1)
            gp.iota(iota_f[:, :], pattern=[[1, P]], base=0, channel_multiplier=0,
                    allow_small_or_imprecise_dtypes=True).then_inc(consts, 1)
            gp.iota(rowid[:, :], pattern=[[0, 1]], base=0, channel_multiplier=1,
                    allow_small_or_imprecise_dtypes=True).then_inc(consts, 1)
            gp.iota(jrow, pattern=[[2 * P, CH // 2]], base=0, channel_multiplier=0,
                    allow_small_or_imprecise_dtypes=True).then_inc(consts, 1)
            gp.memset(ones[:, :], 1.0).then_inc(consts, 1)
            gp.memset(epsc[:, :], EPS).then_inc(consts, 1)
            gp.memset(dedge[:, :], -1.0).then_inc(consts, 1)
            gp.memset(BD, 0.0).then_inc(bd_zeroed, 1)
            gp.memset(hmask[:, :], 1.0).then_inc(consts, 1)
            gp.wait_ge(consts, 8)
            hm = hmask[:, :].rearrange("p (h d) -> p h d", h=HEADS)
            gp.affine_select(out=hm, in_=hm, compare_op=ALU.is_ge, fill=0.0, base=0,
                             pattern=[[-KR, HEADS], [0, DH]], channel_multiplier=1).then_inc(consts, 1)
            gp.wait_ge(consts, 9)
            gp.affine_select(out=hm, in_=hm, compare_op=ALU.is_ge, fill=0.0, base=KR - 1,
                             pattern=[[KR, HEADS], [0, DH]], channel_multiplier=-1).then_inc(consts, 1)

            def pass_through():
                gp.tensor_tensor(turnstile[:, :], rowid[:, :], rowid[:, :], ALU.add)

            gp.wait_ge(pos1_ready, 1)
            gp.wait_ge(recs_zeroed, 16)
            half = LC // 2
            flat_rec = REC[:, :, :].rearrange("p c f -> p (c f)")

            def scatter(i, first=False):
                for h in range(2):
                    if not first:
                        gp.wait_ge(scattered[h], i * (16 * half))
                    c = i * LC + half * h
                    gp.tensor_copy(st_idx[h][:, 0:half], POSI[:, ds(c, half)]).then_inc(staged, 1)
                    gp.tensor_copy(st_rec[h][:, 0:4 * half], flat_rec[:, ds(c * 4, 4 * half)]).then_inc(staged, 1)
                    gp.wait_ge(staged, i * 4 + 2 * h + 2)
                    pass_through()
                    for s in range(half):
                        gp.indirect_dma_start(
                            recs, bass.IndirectOffsetOnAxis(ap=st_idx[h][:, s:s + 1].bitcast(U32), axis=0),
                            st_rec[h][:, 4 * s:4 * s + 4], None).then_inc(scattered[h], 16)
            scatter(0, first=True)
            with gp.Fori(1, C1 // LC) as i:
                scatter(i)
            n = 4 * (C1 // LC)

            def gather(i, h, rows, table, first, used):
                if used is not None:
                    gp.wait_ge(*used)
                gp.tensor_copy(st_idx[h][:, 0:8], (POSI if table is table1 else SRCSI)[:, ds(i * 16 + 8 * h, 8)]).then_inc(staged, 1)
                gp.wait_ge(staged, i * 2 + first + h + 1)
                pass_through()
                for s in range(8):
                    gp.indirect_dma_start(
                        rows(h, s), None, table,
                        bass.IndirectOffsetOnAxis(ap=st_idx[h][:, s:s + 1].bitcast(U32), axis=0)
                    ).then_inc(slot[8 * h + s], 16)

            gp.wait_ge(chunks_ready, 1)
            for b in range(2):
                gp.wait_ge(sup_out[b], 16 + 16 * ((T + 1 - b) // 2))
            rows1 = lambda h, s: ROWS[8 * h + s]
            for h in range(2):
                gather(0, h, rows1, table1, n, None)
            with gp.Fori(1, TURNS) as i:
                for h in range(2):
                    gather(i, h, rows1, table1, n, (seg_done, i * 16 + 8 * h - 8))
            gather(TURNS, 0, rows1, table1, n, (seg_done, TURNS * 16 - 8))
            n += 2 * TURNS + 1

            gp.wait_ge(tab2_out, 16)
            gp.wait_ge(idx2_ready, 1)
            rows2 = lambda h, s: ROWS2[h][:, ROW2 * s:ROW2 * s + ROW2]
            for h in range(2):
                gather(0, h, rows2, table2, n, None)
            with gp.Fori(1, C2 // 16) as i:
                for h in range(2):
                    gather(i, h, rows2, table2, n, (g_copied, i * 2 + h - 1))

            gp.wait_ge(sums_ready, 1)
            gp.dma_start(sums2.rearrange("(p c) f -> p c f", p=P), G).then_inc(sums_out, 16)
            gp.wait_ge(sums_out, 16)
            gp.wait_ge(ends_ready, 1)
            for t in range(T):
                gp.indirect_dma_start(
                    nodes[:, t, :], None, sums2,
                    bass.IndirectOffsetOnAxis(ap=endi[:, t:t + 1].bitcast(U32), axis=0)).then_inc(nodes_in, 16)
            for s in range(4):
                gp.wait_ge(y_out[s], 16 + 16 * 4)
            for g in range(2):
                load_y(gp, g)

        @block.scalar
        def _(act):
            act.sem_inc(t_out, 6)
            act.sem_inc(qt_out, 2)
            act.sem_inc(t2_out, 4)
            act.sem_inc(hid_out, 2)
            act.sem_inc(t3_out, 4)
            act.sem_inc(ehid_out, 2)
            act.sem_inc(eo_out, 2)
            act.wait_ge(bd_zeroed, 1)
            for dst, src in weights:
                act.dma_start(dst, src, allow_slow_non_contiguous=True).then_inc(weights_in, 16)

            def root(k, tile, var):
                act.wait_ge(stats_ready, k)
                act.activation(tile, var, ACT.Sqrt, bias=epsc[:, 0:1], scale=1.0).then_inc(root_ready, 1)
            act.wait_ge(consts, N_CONSTS)
            root(1, rstd[:, :], mv[:, :, 1])
            root(2, rstd2[:, :], mv2[:, :, 1])

            act.wait_ge(wxt_ready, 1)
            for k in range(KT):
                act.activation(WxT[:, k, :], B[k][:, 0:D], ACT.Copy).then_inc(wxt_out, 1)

            act.wait_ge(weights_in, 16 * len(weights))

            def place(t, b):
                act.wait_ge(tp_done, t + 1)
                act.activation(ring_n[b][:, 0:D], XN[:, t, :], ACT.Copy).then_inc(xr_ready, 1)

            def turned(t, b):
                act.wait_ge(tp_done, 2 + t + 1)
                act.wait_ge(proj_done, t + 1)
                act.activation(ring_t[b][:, 0:2, :].rearrange("p k n -> p (k n)"), B[b][:, 0:D], ACT.Copy).then_inc(t_out, 1)
                for k in range(KT):
                    act.activation(ring_t[b][:, 2 + k, :], B[b][:, D + P * k:D + P * k + P], ACT.Identity,
                                   bias=b1[:, k:k + 1], scale=g1[:, k:k + 1]).then_inc(t_out, 1)
            tiles_ahead(act, place, turned)

            act.wait_ge(exp_go, 1)
            act.activation(QKV[:, :, QN:2 * QN], QKV[:, :, QN:2 * QN], ACT.Exp).then_inc(exp_done, 1)
            act.wait_ge(exp_go, 2)
            act.activation(QKV[:, :, 0:QN], QKV[:, :, 0:QN], ACT.Exp).then_inc(exp_done, 1)

            act.wait_ge(exp_go, 3)

            def place_q(t, b):
                act.wait_ge(qt_done, t + 1)
                act.activation(ring_n[b][:, 0:QN], QKV[:, t, 0:QN], ACT.Copy).then_inc(qc_ready, 1)

            def turned_q(t, b):
                act.wait_ge(qt_done, 2 + t + 1)
                act.wait_ge(at_done, t + 1)
                act.activation(ring_t[b][0:QN, 0, :], B[b][0:QN, 0:P], ACT.Copy).then_inc(qt_out, 1)
            tiles_ahead(act, place_q, turned_q)

            root(3, rstd[:, :], mv[:, :, 1])

            def turned2(g, b, tiles):
                act.wait_ge(hp_done, 8 * g + 8)
                for j in range(tiles):
                    act.wait_ge(tp2_done, 2 + 4 * g + j + 1)
                    for k in range(KT):
                        act.activation(H2T[b][:, k, P * j:P * j + P], B[j % 2][:, P * k:P * k + P], ACT.Identity,
                                       bias=b2[:, k:k + 1], scale=g2[:, k:k + 1]).then_inc(t2_out, 1)

            def gelu(g, b, tiles, ahead):
                act.wait_ge(op_done, 4 * g + 4)
                for m in range(FM):
                    act.wait_ge(hp_done, 16 + FM * g + m + 1)
                    act.activation(HID[b][:, m, 0:P * tiles], B[2 + m % 2][:, 0:P * tiles], ACT.Gelu,
                                   bias=fb1[:, m:m + 1], scale=1.0).then_inc(hid_out, 1)
                ahead()
            groups_ahead(act, turned2, gelu)

            parts = [(n, AG[:, PART * n:PART * n + PART, :], SQ[:, PART * n:PART * n + PART, :]) for n in range(PARTS_N)]
            for n, ag, sq in parts:
                act.wait_ge(bn_go, 1 + n + 1)
                act.activation(sq, ag, ACT.Square).then_inc(act_bn, 1)
            act.wait_ge(bn_done, 2)
            act.activation(stat[:, 1, :], B[5][:, 0:D], ACT.Sqrt, bias=epsc[:, 0:1], scale=1.0 / N).then_inc(act_bn, 1)
            for n, ag, sq in parts:
                act.wait_ge(bn_go, 1 + PARTS_N + n + 1)
                act.activation(ag, ag, ACT.Tanh).then_inc(act_bn, 1)

            root(4, rstd[:, :], mv[:, :, 1])

            def turned3(t, b):
                act.wait_ge(tp3_done, 2 + t + 1)
                act.wait_ge(h_done, t + 1)
                act.activation(ring_t[b][:, 0:2, :].rearrange("p k n -> p (k n)"), B[b][:, 0:D], ACT.Copy).then_inc(t3_out, 1)
                act.activation(X2T[:, :, ds(t * P, P)], B[b][:, 0:D].rearrange("p (k n) -> p k n", k=KT), ACT.Copy).then_inc(t3_out, 1)
            tiles_in_pairs(act, turned3)

            def gelus(g, e, tiles):
                act.wait_ge(eo_done, (8 * g + 2 * e + 2) if tiles == 4 or e < 2 else 8 * GROUPS + 3 + e)
                for m in range(EM):
                    act.wait_ge(ep_done, 2 + 16 * g + 4 * e + m + 1)
                    act.activation(EHID[e % 2][:, m, 0:P * tiles], B[2 + m % 2][:, 0:P * tiles], ACT.Gelu,
                                   bias=eb1[:, e, m:m + 1], scale=1.0).then_inc(ehid_out, 1)

            def emit(g, e, tiles):
                for h in range(2 if tiles == 4 else 1):
                    n, place, b = (2 * e + h, (2 * e + h) % 4, h) if tiles == 4 else (e, e, e % 2)
                    width = 2 * D if tiles == 4 else D
                    act.wait_ge(eo_done, 4 + 8 * g + n + 1)
                    act.wait_ge(y_out[place], 16 + 32 * g + (16 * (e // 2) if tiles == 4 else 0))
                    act.activation(y_ring[place][:, 0:width], B[4 + b][:, 0:width], ACT.Copy).then_inc(eo_out, 1)

            def moe(g, tiles, between=None):
                gelus(g, 0, tiles)
                for e in range(NE):
                    if e + 1 < NE:
                        gelus(g, e + 1, tiles)
                    emit(g, e, tiles)
                    if between and e == 0:
                        between()

            def exp_scores():
                act.wait_ge(esc_go, 1)
                act.activation(G[:, :, GH:2 * GH], MF, ACT.Exp).then_inc(esc_done, 1)
            with act.Fori(0, GROUPS - 1) as g:
                moe(g, 4)
            moe(GROUPS - 1, 4, exp_scores)
            moe(GROUPS, 1)
            root(5, gstat[:, :, 1], gstat[:, :, 1])
            act.wait_ge(gate_go, 1)
            act.activation(rank[:, :, :], gates[:, :, :], ACT.Exp).then_inc(gate_done, 1)
            act.wait_ge(gates_ready, 1)
            for g in range(GROUPS + 1):
                width = 4 * P if g < GROUPS else P
                act.wait_ge(gt_done, g + 1)
                if g >= 2:
                    act.wait_ge(gb_done, g - 1)
                act.activation(gT[g % 2][:, 0:width], B[g % 2][0:NE, 0:width], ACT.Copy).then_inc(gt_out, 1)
                if g == 0:
                    act.wait_ge(eo_done, 4 + 8 * GROUPS + NE)
                for j in range(4 if g < GROUPS else 1):
                    for e in range(2):
                        last = act.activation(diag[g % 2][:, e, j, :], ident[:, :], ACT.Copy,
                                              scale=gates[:, 4 * g + j, 2 + e:3 + e])
                    last.then_inc(diag_ready, 1)

        @block.tensor
        def _(pe):
            mm, tr = nc.tensor.matmul, nc.tensor.transpose
            pe.sem_inc(tp_done, 2)
            pe.sem_inc(proj_done, 2)
            pe.sem_inc(qt_done, 2)
            pe.sem_inc(at_done, 2)
            pe.sem_inc(tp2_done, 2)
            pe.sem_inc(hp_done, 16)
            pe.sem_inc(op_done, 8)
            pe.sem_inc(perm_used, 6)
            pe.sem_inc(hist_used, 8)
            pe.sem_inc(tp3_done, 2)
            pe.sem_inc(h_done, 2)
            pe.sem_inc(ep_done, 2)
            pe.sem_inc(eo_done, 4)
            pe.wait_ge(consts, N_CONSTS)

            def prefix(k, keys):
                pe.wait_ge(cnt_ready, k)
                mm(B[7][:, 0:keys], tri[:, :], cnts[:, 0, 0:keys], start=True, stop=True)
                mm(B[7][:, 64:64 + keys], ones[:, :], cnts[:, 0, 0:keys], start=True, stop=True).then_inc(pre_ready, 1)
            prefix(1, T)

            pe.wait_ge(weights_in, 16 * len(weights))
            for k in range(KT):
                for m in range(KT):
                    last = tr(B[k][:, P * m:P * m + P], Wx[:, m, P * k:P * k + P], ident[:, :])
            last.then_inc(wxt_ready, 1)
            pe.wait_ge(wxt_out, 2)
            for m in range(KT):
                for k in range(KT):
                    mm(B[2 + m][:, 0:QKVN], WxT[:, k, P * m:P * m + P], BD[:, k, :], start=(k == 0), stop=(k == KT - 1))
            pe.wait_ge(signs, 1)
            for k in range(KT):
                last = mm(B[4][:, 0:QKVN], bxb[:, k, :], BD[:, k, :], start=(k == 0), stop=(k == KT - 1))
            last.then_inc(wc_ready, 1)
            pe.wait_ge(wc_out, 3)

            def turn(t, b):
                pe.wait_ge(hh_ready, t + 1)
                pe.wait_ge(xr_ready, t + 1)
                pe.wait_ge(t_out, 3 * t + 3)
                for k in range(4):
                    last = tr(B[b][:, P * k:P * k + P], ring_n[b][:, P * k:P * k + P], ident[:, :])
                last.then_inc(tp_done, 1)

            def project(t, b):
                pe.wait_ge(t_out, 6 + 3 * t + 3)
                pe.wait_ge(proj_out, t + 1)
                for k in range(KT):
                    mm(B[2 + b][:, 0:D], ring_t[b][:, k, :], WH[:, k, :], start=(k == 0), stop=(k == KT - 1))
                for k in range(KT):
                    last = mm(B[4 + b][:, 0:QKVN], ring_t[b][:, 2 + k, :], Wc[:, k, :], start=(k == 0), stop=(k == KT - 1))
                last.then_inc(proj_done, 1)
            tiles_ahead(pe, turn, project)

            pe.wait_ge(kmax_in, 1)
            tr(B[6][0:QN, 0:P], small[:, 0:QN], ident[:, :]).then_inc(kmax_out, 1)
            pe.wait_ge(kmax_in, 2)
            mm(B[7][:, 128:128 + QN], ones[0:QN, :], small[0:QN, 64:64 + QN], start=True, stop=True).then_inc(kmax_out, 1)
            pe.wait_ge(exp_done, 1)
            for t in range(T):
                n = P if t < T - 1 else LAST
                mm(B[6][0:QN, 0:D], QKV[0:n, t, QN:2 * QN], QKV[0:n, t, 2 * QN:QKVN], start=(t == 0), stop=(t == T - 1))
                last = mm(B[0][0:QN, 0:1], QKV[0:n, t, QN:2 * QN], ones[0:n, 0:1], start=(t == 0), stop=(t == T - 1))
            last.then_inc(kv_done, 1)
            pe.wait_ge(kv_out, 1)
            for k in range(KT):
                last = tr(B[4][:, QN * k:QN * k + QN], stat[0:QN, 0, P * k:P * k + P], ident[0:QN, 0:QN])
            last.then_inc(kv_done, 1)
            pe.wait_ge(kv_out, 2)
            for k in range(KT):
                last = mm(B[5][0:QN, 0:D], small[:, 96 + QN * k:96 + QN * k + QN], Wo[:, k, :], start=(k == 0), stop=(k == KT - 1))
            last.then_inc(kv_done, 1)
            pe.wait_ge(kv_out, 3)

            def turn_q(t, b):
                pe.wait_ge(qc_ready, t + 1)
                pe.wait_ge(qt_out, t + 1)
                tr(B[b][0:QN, 0:P], ring_n[b][:, 0:QN], ident[:, :]).then_inc(qt_done, 1)

            def attend(t, b):
                pe.wait_ge(qt_out, 2 + t + 1)
                pe.wait_ge(at_out, t + 1)
                mm(B[2 + b][:, 0:D], ring_t[b][0:QN, 0, :], stat[0:QN, 1, :], start=True, stop=True).then_inc(at_done, 1)
            tiles_ahead(pe, turn_q, attend)

            pe.wait_ge(mlp_in, 32)

            def turn2(g, b, tiles):
                for j in range(tiles):
                    pe.wait_ge(n2_ready, 4 * g + j + 1)
                    pe.wait_ge(t2_out, 8 * g + 2 * j + 2)
                    for k in range(KT):
                        last = tr(B[j % 2][:, P * k:P * k + P], ring_n[j % 2][:, P * k:P * k + P], ident[:, :])
                    last.then_inc(tp2_done, 1)

            def histogram(g, columns):
                known = isinstance(g, int)
                for j in columns:
                    pe.wait_ge(hist_ready, g * HC + j + 1)
                    mm(B[6][:, 0:T], of_place[j % 8], of_tile[j % 8], start=(known and g == 0 and j == 0),
                       stop=(known and g == GROUPS - 1 and j == HC - 1), skip_group_check=True).then_inc(hist_used, 1)

            def mlp(g, b, tiles, ahead):
                n = P * tiles
                pe.wait_ge(t2_out, 4 + 8 * g + 2 * tiles)
                for m in range(FM):
                    pe.wait_ge(hid_out, FM * g + m + 1)
                    for k in range(KT):
                        last = mm(B[2 + m % 2][:, 0:n], W1s[:, k, P * m:P * m + P], H2T[b][:, k, 0:n], start=(k == 0), stop=(k == KT - 1))
                    last.then_inc(hp_done, 1)
                    if tiles == 4:
                        histogram(g, range(3 * m, 3 * m + 3))
                ahead()
                pe.wait_ge(hid_out, 2 + FM * g + FM)
                for j in range(tiles):
                    pe.wait_ge(op_added, 4 * g + j + 1)
                    for k in range(FM):
                        last = mm(B[4 + j % 2][:, 0:D], HID[b][:, k, P * j:P * j + P], W2s[:, k, :], start=(k == 0), stop=(k == FM - 1))
                    last.then_inc(op_done, 1)
                    if tiles == 4:
                        histogram(g, range(HC // 2 + 6 * j, HC // 2 + 6 * j + 6))
            groups_ahead(pe, turn2, mlp)

            prefix(2, T)
            prefix(3, KEYS2)

            def columns(i, s, first=False, final=False):
                for q in columns_at(s):
                    pe.wait_ge(perm_ready, i * SC2 + q + 1)
                    mm(B[6][:, 0:C2], lhs[q % 6], rhs[q % 6], start=(first and q == 0), stop=(final and q == SC2 - 1),
                       skip_group_check=True).then_inc(perm_used, 1)

            def chunks(i, k=None, first=False, count=16):
                for s in range(count):
                    pe.wait_ge(sw_ready, i * 16 + s + 1)
                    pe.wait_ge(slot[s], i * 16 + 16)
                    if s % 2 == 0:
                        pe.wait_ge(seg_added, i * 8 + s // 2 + 1)
                    mm(B[s // 2 % 4][:, 0:D], SW[s % 4], ROWS[s], start=(s % 2 == 0), stop=(s % 2 == 1)).then_inc(seg_done, 1)
                    if k is not None and s >= 2:
                        columns(i - (PASS_AT[k] - k * PT), s - 2, first=first)
                    elif k is not None and not first:
                        columns(i - (PASS_AT[k] - k * PT + 1), s + 14)

            def chunks_with_pass(k):
                chunks(PASS_AT[k], k, first=True)
                with pe.Fori(PASS_AT[k] + 1, PASS_AT[k] + PT) as i:
                    chunks(i, k)
                columns(k * PT + PT - 1, 14)
                columns(k * PT + PT - 1, 15, final=True)
            chunks(0)
            chunks_with_pass(0)
            chunks(PT + 1)
            prefix(4, KEYS2)
            chunks(PT + 2)
            pe.wait_ge(perm_read, 1)
            chunks_with_pass(1)
            chunks(TURNS, count=8)

            pe.wait_ge(bn_go, 1)
            for t in range(T):
                last = mm(B[4][:, 0:D], ones[:, :], AG[:, t, :], start=(t == 0), stop=(t == T - 1))
            last.then_inc(bn_done, 1)
            for t in range(T):
                if t % PART == 0:
                    pe.wait_ge(act_bn, t // PART + 1)
                n = P if t < T - 1 else LAST
                last = mm(B[5][:, 0:D], ones[0:n, :], SQ[0:n, t, :], start=(t == 0), stop=(t == T - 1))
            last.then_inc(bn_done, 1)

            def turn3(t, b):
                pe.wait_ge(n3_ready, t + 1)
                pe.wait_ge(t3_out, 2 * t + 2)
                for k in range(KT):
                    last = tr(B[b][:, P * k:P * k + P], ring_n[b][:, P * k:P * k + P], ident[:, :])
                last.then_inc(tp3_done, 1)

            def project3(t, b):
                pe.wait_ge(t3_out, 4 + 2 * t + 2)
                pe.wait_ge(h_out, t + 1)
                for k in range(KT):
                    last = mm(B[2 + b][:, 0:GH * NE], ring_t[b][:, k, :], Wg[:, k, :], start=(k == 0), stop=(k == KT - 1))
                last.then_inc(h_done, 1)
            tiles_ahead(pe, turn3, project3)

            pe.wait_ge(carry_go, 1)
            mm(B[6][:, 0:2 * P], ones[:, :], DG[:, 0:2, :].rearrange("p a b -> p (a b)"), start=True, stop=True).then_inc(carry_done, 1)

            def carry_scores():
                pe.wait_ge(carry_go, 2)
                mm(B[1][:, 0:GH], M2, small[:, 0:GH], start=True, stop=True)
                mm(B[6][:, :], ones[:, :], DG.rearrange("p a b -> p (a b)"), start=True, stop=True).then_inc(carry_done, 1)
                pe.wait_ge(carry_go, 3)
                mm(B[7][:, :], ones[:, :], DG2.rearrange("p a b -> p (a b)"), start=True, stop=True).then_inc(carry_done, 1)

            def carry_sums():
                pe.wait_ge(carry_go, 4)
                mm(B[1][:, 32:32 + SUMS], M2, small[:, 32:32 + SUMS], start=True, stop=True).then_inc(carry_done, 1)

            pe.wait_ge(experts_in, 32)

            def first(g, e, tiles):
                n = P * tiles
                for m in range(EM):
                    pe.wait_ge(ehid_out, 16 * g + 4 * e + m + 1)
                    for k in range(KT):
                        last = mm(B[2 + m % 2][:, 0:n], EW1[:, e, k, P * m:P * m + P],
                                  X2T[:, k, ds(g * 512, n)], start=(k == 0), stop=(k == KT - 1))
                    last.then_inc(ep_done, 1)

            def second(g, e, tiles):
                pe.wait_ge(ehid_out, 2 + 16 * g + 4 * e + 4)
                for h in range(2 if tiles == 4 else 1):
                    n, b = (2 * e + h, h) if tiles == 4 else (e, e % 2)
                    pe.wait_ge(eo_out, 8 * g + n + 1)
                    for j in range(2 if tiles == 4 else 1):
                        for k in range(EM):
                            last = mm(B[4 + b][:, D * j:D * j + D], EHID[e % 2][:, k, P * (2 * h + j):P * (2 * h + j) + P],
                                      EW2[:, e, k, :], start=(k == 0), stop=(k == EM - 1))
                    last.then_inc(eo_done, 1)

            def moe(g, tiles, between=(None, None)):
                first(g, 0, tiles)
                for e in range(NE):
                    if e + 1 < NE:
                        first(g, e + 1, tiles)
                    second(g, e, tiles)
                    if e < 2 and between[e]:
                        between[e]()
            with pe.Fori(0, GROUPS - 1) as g:
                moe(g, 4)
            moe(GROUPS - 1, 4, (carry_scores, carry_sums))
            moe(GROUPS, 1)

            pe.wait_ge(gates_ready, 1)

            def turn_gates(g):
                if g >= 2:
                    pe.wait_ge(gt_out, g - 1)
                for j in range(4 if g < GROUPS else 1):
                    last = tr(B[g % 2][0:NE, P * j:P * j + P], gates[:, 4 * g + j, :], ident[:, :])
                last.then_inc(gt_done, 1)
            turn_gates(0)
            for g in range(GROUPS + 1):
                if g < GROUPS:
                    turn_gates(g + 1)
                pe.wait_ge(gt_out, g + 1)
                if g >= 2:
                    pe.wait_ge(gb_added, g - 1)
                pe.wait_ge(y_in[g], 16 * NE)
                for j in range(4 if g < GROUPS else 1):
                    pe.wait_ge(diag_ready, 4 * g + j + 1)
                    o = B[2 + 2 * (g % 2) + j // 2][:, D * (j % 2):D * (j % 2) + D]
                    mm(o, gT[g % 2][:, P * j:P * j + P], eb2[:, :], start=True, stop=False)
                    mm(o, diag[g % 2][:, 0, j, :], Y[g][:, 2, j, :], start=False, stop=False)
                    last = mm(o, diag[g % 2][:, 1, j, :], Y[g][:, 3, j, :], start=False, stop=True)
                last.then_inc(gb_done, 1)

        @block.vector
        def _(ve):
            v = Chain(ve, vec_step)
            ts, tt, stt, cp = ve.tensor_scalar, ve.tensor_tensor, ve.scalar_tensor_tensor, ve.tensor_copy
            red, scan = ve.tensor_reduce, ve.tensor_tensor_scan
            ve.sem_inc(proj_out, 2)
            ve.sem_inc(at_out, 2)
            ve.sem_inc(op_added, 2)
            ve.sem_inc(seg_added, 4)
            ve.sem_inc(h_out, 2)

            ve.wait_ge(consts, 10)
            v(ts(ident[:, :], iota_f[:, :], rowid[:, 0:1], None, ALU.is_equal))
            v(ts(tri[:, :], iota_f[:, :], rowid[:, 0:1], None, ALU.is_gt))
            v(ts(low[:, :], iota_f[:, :], rowid[:, 0:1], None, ALU.is_lt))
            ve.wait_ge(padded, 7)
            ts(SRC2I, flat_i[:, :], NP - 1, None, ALU.min).then_inc(padded2, 1)
            ts(DST2I, flat_i[:, :], NP - 1, None, ALU.min).then_inc(padded2, 1)

            def decode(sorted_i):
                v(ts(SRCSI[:, :], sorted_i, 12, None, ALU.arith_shift_right))
                v(cp(DSTS[:, :], SRCSI[:, :]))
                v(ts(SRCSI[:, :], sorted_i, 4095, None, ALU.bitwise_and))

            def floor_div(o, i, d):
                v(ts(o, i, 1.0 / d, 0.5 / d - 0.5, ALU.mult, ALU.add))
                v(ts(o, o, ROUND, ROUND, ALU.add, ALU.subtract))

            def positions(k, C, keys, at_once, group, tmp, pos, whole_pairs, meanwhile=(None, None)):
                v.apart(keys, at_once, lambda i: ts(
                    onehot[:, ds(i * C, C)], K16[:, 0:C], iota_f[:, ds(i, 1)], None, ALU.is_equal))
                if meanwhile[0]:
                    meanwhile[0]()
                oh, cn = onehot[:, 0:keys * C], counts[:, 0:keys * C]
                v(scan(cn, oh, oh, 0.0, ALU.add, ALU.max))
                count, at_end, total, upto, start, shift = (cnts[:, i, 0:keys] for i in range(6))
                v(cp(at_end, cn.rearrange("p (k c) -> p k c", c=C)[:, :, C - 1]))
                v(cp(count[:, 0:1], at_end[:, 0:1]))
                tt(count[:, 1:keys], at_end[:, 1:keys], at_end[:, 0:keys - 1], ALU.subtract).then_inc(cnt_ready, 1)
                ve.wait_ge(pre_ready, k)
                v(cp(total, B[7][:, 64:64 + keys]))
                if whole_pairs:
                    v(ts(total, total, float(2 * P - 1), None, ALU.add))
                    floor_div(total, total, 2 * P)
                    v(ts(total, total, float(2 * P), None, ALU.mult))
                v(scan(upto, total, total, 0.0, ALU.add, ALU.max))
                v(tt(start, upto, total, ALU.subtract))
                v(tt(shift, start, B[7][:, 0:keys], ALU.add))
                v(tt(shift, shift, at_end, ALU.subtract))
                v(stt(shift, shift, -1.0, count, ALU.add, ALU.add))

                if meanwhile[1]:
                    meanwhile[1]()

                of_group = tmp[:, group * C:(group + 1) * C]
                v(ve.memset(pos, 0.0))

                def some_keys(i, some=group):
                    for q in range(some):
                        key = i * group + q
                        v.go(stt(tmp[:, q * C:(q + 1) * C], counts[:, ds(key * C, C)], cnts[:, 5, ds(key, 1)],
                                 onehot[:, ds(key * C, C)], ALU.add, ALU.mult))
                    v.join()
                    v(red(of_group, tmp[:, 0:some * C].rearrange("p (q c) -> p c q", c=C), AX.X, ALU.add))
                    v(tt(pos, pos, of_group, ALU.add))
                v.loop(keys // group, group + 2, some_keys)
                some_keys(keys // group, keys % group)

            ve.wait_ge(edges1_in, 96)
            blk, lo = K0[:, 0:C1], K1[:, 0:C1]
            v(cp(lo, SRC))
            floor_div(blk, lo, P)
            v(cp(K16[:, :], blk))
            v(stt(REC[:, 0:C1, 1], blk, -float(P), lo, ALU.mult, ALU.add))
            v(cp(REC[:, 0:C1, 0], DST))
            v(cp(REC[:, 0:C1, 2], WT))
            ve.wait_ge(recs_zeroed, 16)
            pos = K2[:, 0:C1]
            positions(1, C1, T, 5, 12, tmp_s, pos, True)
            chunk = K0[:, 0:C1]
            floor_div(chunk, pos, P)
            v(stt(K1[:, 0:C1], chunk, -float(P), pos, ALU.mult, ALU.add))
            stt(POSI[:, 0:C1], K1[:, 0:C1], float(CH), chunk, ALU.mult, ALU.add).then_inc(pos1_ready, 1)
            ends_before = K2[0:1, 0:CH // 2]
            v(ts(ends_before, jrow[0:1, :], cnts[0:1, 3, 0:1], None, ALU.is_ge))

            def block_ends(i):
                for q in range(6):
                    v(stt(ends_before, jrow[0:1, :], cnts[0:1, 3, ds(i * 6 + q + 1, 1)], ends_before, ALU.is_ge, ALU.add))
            v.loop((T - 1) // 6, 6, block_ends)
            v(ts(blk_i[0:1, :], ends_before, float(T - 1), None, ALU.min))

            ve.wait_ge(edges2_in, 96)
            v(cp(VAL[:, :], DST2I))
            v(cp(K1[:, 0:C2], SRC2I))
            v(stt(VAL[:, :], VAL[:, :], 4096.0, K1[:, 0:C2], ALU.mult, ALU.add))

            def statistics(src, m, k):
                v.apart(T, 5, lambda t: ve.bn_stats(st6[:, t, :], src[:, t, :]))
                mean, var = m[:, :, 0], m[:, :, 1]
                v(tt(mean, st6[:, :, 1], st6[:, :, 4], ALU.add))
                v(tt(st6[:, :, 1], st6[:, :, 1], st6[:, :, 4], ALU.subtract))
                v(stt(st6[:, :, 1], st6[:, :, 1], D / 4, st6[:, :, 1], ALU.mult, ALU.mult))
                v(tt(var, st6[:, :, 2], st6[:, :, 5], ALU.add))
                v(tt(var, var, st6[:, :, 1], ALU.add))
                v(ts(var, var, 1.0 / D, None, ALU.mult))
                v(ts(mean, mean, 0.5, None, ALU.mult))
                ve.sem_inc(stats_ready, 1)

            def reciprocal(k, r):
                ve.wait_ge(root_ready, k)
                v(ve.reciprocal(r, r))
            ve.wait_ge(x_in, 32)
            statistics(X, mv, 1)
            reciprocal(1, rstd[:, :])

            v.apart(T, 5, lambda t: ts(
                XN[:, t, :], X[:, t, :], mv[:, t, 0:1], rstd[:, ds(t, 1)], ALU.subtract, ALU.mult))
            statistics(XN, mv2, 2)
            reciprocal(2, rstd2[:, :])

            ve.wait_ge(weights_in, 16 * len(weights))
            for r, c in MINUS:
                w = WH[64 * (r % 2):64 * (r % 2) + 64, r // 2, 64 * c:64 * c + 64]
                v(ts(w, w, -1.0, None, ALU.mult))
            for k in range(KT):
                v(ts(bxb[:, k, :], ones[:, :], bxc[:, k:k + 1], None, ALU.mult))
            ve.sem_inc(signs, 1)
            ve.wait_ge(wc_ready, 1)
            for m in range(KT):
                cp(Wc[:, m, :], B[2 + m][:, 0:QKVN]).then_inc(wc_out, 1)
            cp(bc[:, :], B[4][:, 0:QKVN]).then_inc(wc_out, 1)
            ve.wait_ge(wc_out, 3)

            def center(t, b):
                ve.wait_ge(tp_done, t + 1)
                ts(ring_n[b][:, D:2 * D], XN[:, t, :], mv2[:, t, 0:1], rstd2[:, ds(t, 1)],
                   ALU.subtract, ALU.mult).then_inc(hh_ready, 1)

            def projected(t, b):
                ve.wait_ge(proj_done, 2 + t + 1)
                ve.wait_ge(sup_out[b], (t - b) * 8 + 16)
                cp(ring_s[b], B[2 + b][:, 0:D]).then_inc(sup_ready, 1)
                tt(QKV[:, t, :], B[4 + b][:, 0:QKVN], bc[:, :], ALU.add).then_inc(proj_out, 1)
            tiles_two_ahead(ve, center, projected)
            ve.wait_ge(proj_out, 2 + T)
            for b in range(2):
                ve.wait_ge(sup_out[b], 16 + 16 * ((T + 1 - b) // 2))

            q, kk = QKV[:, :, 0:QN], QKV[:, :, QN:2 * QN]
            kmax = small[:, 0:QN]
            v(red(kmax, kk[:, 0:T - 1, :].rearrange("p t c -> p c t"), AX.X, ALU.max))
            v(tt(kmax[0:LAST, :], kmax[0:LAST, :], kk[0:LAST, T - 1, :], ALU.max))
            ve.sem_inc(kmax_in, 1)
            ve.wait_ge(kmax_out, 1)
            v(red(small[0:QN, 128:129], B[6][0:QN, 0:P], AX.X, ALU.max))
            v(ts(small[0:QN, 64:64 + QN], ident[0:QN, 0:QN], small[0:QN, 128:129], None, ALU.mult))
            ve.sem_inc(kmax_in, 1)
            ve.wait_ge(kmax_out, 2)
            v(cp(small[:, 32:32 + QN], B[7][:, 128:128 + QN]))
            tt(kk, kk, small[:, 32:32 + QN].unsqueeze(1).to_broadcast([P, T, QN]), ALU.subtract).then_inc(exp_go, 1)
            q4 = q.rearrange("p t (h r) -> p t h r", r=KR)
            K0q = K0[:, 0:T * HEADS].rearrange("p (t h) -> p t h", t=T)
            v(red(K0q, q4, AX.X, ALU.max))
            tt(q4, q4, K0q.unsqueeze(3).to_broadcast([P, T, HEADS, KR]), ALU.subtract).then_inc(exp_go, 1)
            ve.wait_ge(exp_done, 2)
            v(red(K0q, q4, AX.X, ALU.add))
            v(ve.reciprocal(K0[:, 0:T * HEADS], K0[:, 0:T * HEADS]))
            tt(q4, q4, K0q.unsqueeze(3).to_broadcast([P, T, HEADS, KR]), ALU.mult).then_inc(exp_go, 1)
            v(tt(XN[:, :, :], XN[:, :, :], rowv[:, 0, :].unsqueeze(1).to_broadcast([P, T, D]), ALU.add))
            ve.wait_ge(kv_done, 1)
            v(ve.reciprocal(small[0:QN, 128:129], B[0][0:QN, 0:1]))
            stt(stat[0:QN, 0, :], B[6][0:QN, 0:D], small[0:QN, 128:129], hmask[:, :], ALU.mult, ALU.mult).then_inc(kv_out, 1)
            ve.wait_ge(kv_done, 2)
            cp(small[:, 96:96 + 2 * QN], B[4][:, 0:2 * QN]).then_inc(kv_out, 1)
            ve.wait_ge(kv_done, 3)
            cp(stat[0:QN, 1, :], B[5][0:QN, 0:D]).then_inc(kv_out, 1)


            def attended(t, b):
                ve.wait_ge(at_done, 2 + t + 1)
                tt(XN[:, t, :], XN[:, t, :], B[2 + b][:, 0:D], ALU.add).then_inc(at_out, 1)
            tiles_in_pairs(ve, attended)
            ve.wait_ge(at_out, 2 + T)
            statistics(XN, mv, 3)
            reciprocal(3, rstd[:, :])

            def center2(g, b, tiles):
                for j in range(tiles):
                    t = 4 * g + j
                    ve.wait_ge(tp2_done, t + 1)
                    ts(ring_n[j % 2][:, 0:D], XN[:, t, :], mv[:, t, 0:1], rstd[:, ds(t, 1)],
                       ALU.subtract, ALU.mult).then_inc(n2_ready, 1)

            def count_edges(g, columns):
                for j in columns:
                    ve.wait_ge(hist_used, g * HC + j + 1)
                    ts(of_place[j % 8], iota[:, 0:P], K0[:, ds(g * HC + j, 1)], None, ALU.is_equal)
                    ts(of_tile[j % 8], iota[:, 0:T], K1[:, ds(g * HC + j, 1)], None, ALU.is_equal).then_inc(hist_ready, 1)

            def mlp_added(g, b, tiles, ahead):
                if tiles == 4:
                    count_edges(g, range(HC // 2))
                ahead()
                for j in range(tiles):
                    t = 4 * g + j
                    tt(X[:, t, :], X[:, t, :], XN[:, t, :], ALU.add).then_inc(fx_added, 1)
                for j in range(tiles):
                    t = 4 * g + j
                    ve.wait_ge(fx_added, t + 1)
                    tt(X[:, t, :], X[:, t, :], rowv[:, 1, :], ALU.add).then_inc(bias_added, 1)
                for j in range(tiles):
                    t = 4 * g + j
                    if tiles == 4:
                        count_edges(g, range(HC // 2 + 6 * j, HC // 2 + 6 * j + 6))
                    ve.wait_ge(op_done, 8 + t + 1)
                    ve.wait_ge(bias_added, t + 1)
                    tt(X[:, t, :], X[:, t, :], B[4 + j % 2][:, 0:D], ALU.add).then_inc(op_added, 1)
            v(cp(KI[:, 0:C2], VAL[:, :]))
            decode(KI[:, 0:C2])
            floor_div(K1[:, 0:C2], DSTS[:, :], P)
            v(stt(K0[:, 0:C2], K1[:, 0:C2], -float(P), DSTS[:, :], ALU.mult, ALU.add))
            groups_ahead(ve, center2, mlp_added)
            ve.wait_ge(op_added, 2 + T)

            ve.wait_ge(hist_used, 8 + C2)
            count, total, upto, end = (cnts[:, i, 0:T] for i in range(4))
            cp(count, B[6][:, 0:T]).then_inc(cnt_ready, 1)
            ve.wait_ge(pre_ready, 2)
            v(cp(total, B[7][:, 64:64 + T]))
            v(scan(upto, total, total, 0.0, ALU.add, ALU.max))
            v(tt(end, upto, total, ALU.subtract))
            v(tt(end, end, count, ALU.add))
            v(tt(end, end, B[7][:, 0:T], ALU.add))
            v(ts(end, end, -1.0, None, ALU.add))
            v(cp(endi[:, :], end))
            ve.sem_inc(ends_ready, 1)

            v(ve.memset(AG, 0.0))

            def start_gathers():
                ve.wait_ge(recs_back, 16)
                v(cp(POSI[:, :], REC[:, 0:CH, 0]))
                ve.sem_inc(chunks_ready, 1)

            def sort_places(k, meanwhile):
                hi = K0[:, 0:C2]
                floor_div(hi, DSTS[:, :], KEYS2)
                if k == 0:
                    v(stt(K16[:, 0:C2], hi, -float(KEYS2), DSTS[:, :], ALU.mult, ALU.add))
                else:
                    v(cp(K16[:, 0:C2], hi))
                positions(3 + k, C2, KEYS2, 19, 9, tmp_2, K2[:, 0:C2], False, meanwhile)
                floor_div(K0[:, 0:C2], K2[:, 0:C2], C2)
                v(stt(K1[:, 0:C2], K0[:, 0:C2], -float(C2), K2[:, 0:C2], ALU.mult, ALU.add))

            def sorted_values():
                v(cp(VAL[:, :], B[6][:, 0:C2]))
                v(cp(KI[:, 0:C2], VAL[:, :]))
                decode(KI[:, 0:C2])

            def weigh(j, s):
                ts(SW[s % 4], iota[:, 0:P], REC[:, ds(j, 1), 1], REC[:, ds(j, 1), 2],
                   ALU.is_equal, ALU.mult).then_inc(sw_ready, 1)

            def chunks(i, first=False, sort=None, count=16):
                _, at_block = nc.values_load_multi_w_load_instructions(
                    blk_i[0:1, ds(i * 8, count // 2)], engines=(mybir.EngineType.DVE,), min_val=0, max_val=T - 1)

                def add(pair):
                    ve.wait_ge(seg_done, i * 16 + 2 * pair + 2)
                    ve.wait_ge(seg_added, i * 8 + pair + 4)
                    place = AG[:, ds(at_block[pair], 1), :].rearrange("p a d -> p (a d)")
                    tt(place, place, B[pair % 4][:, 0:D], ALU.add).then_inc(seg_added, 1)
                for s in range(count):
                    j = i * 16 + s
                    if not (first and s < 2):
                        ve.wait_ge(seg_done, j - 1)
                    weigh(j + 2, s + 2)
                    if s % 2 == 0 and s:
                        add(s // 2 - 1)
                    if sort is not None:
                        for q in columns_at(s):
                            c = (i - PASS_AT[sort]) * SC2 + q
                            ve.wait_ge(perm_used, (i - PASS_AT[sort]) * SC2 + (sort * C2 + q + 1))
                            ts(lhs[q % 6], iota[:, 0:P], K0[:, ds(c, 1)], None, ALU.is_equal)
                            ts(rhs[q % 6], iota[:, 0:C2], K1[:, ds(c, 1)], VAL[:, ds(c, 1)],
                               ALU.is_equal, ALU.mult).then_inc(perm_ready, 1)
                add(count // 2 - 1)
            sort_places(0, (None, start_gathers))
            weigh(0, 0)
            weigh(1, 1)
            chunks(0, first=True)
            with ve.Fori(PASS_AT[0], PASS_AT[0] + PT) as i:
                chunks(i, sort=0)
            ve.wait_ge(perm_used, 6 + C2)
            sorted_values()
            ve.sem_inc(perm_read, 1)
            sort_places(1, (lambda: chunks(PT + 1), lambda: chunks(PT + 2)))
            with ve.Fori(PASS_AT[1], PASS_AT[1] + PT) as i:
                chunks(i, sort=1)
            ve.wait_ge(perm_used, 6 + 2 * C2)
            chunks(TURNS, count=8)
            ve.wait_ge(seg_added, 4 + CH // 2)

            sorted_values()
            ve.sem_inc(idx2_ready, 1)
            ve.sem_inc(sorted2_ready, 1)
            first_, goes_on = (FLG[:, i, :] for i in range(2))

            ve.sem_inc(bn_go, 1)
            ve.wait_ge(bn_done, 1)
            v(ts(stat[:, 0, :], B[4][:, 0:D], 1.0 / N, None, ALU.mult))
            wide = lambda r: r.unsqueeze(1).to_broadcast([P, PART, D])
            parts = [(n, AG[:, PART * n:PART * n + PART, :], X[:, PART * n:PART * n + PART, :]) for n in range(PARTS_N)]
            for n, ag, x1 in parts:
                tt(ag, ag, wide(stat[:, 0, :]), ALU.subtract).then_inc(bn_go, 1)
            ve.wait_ge(act_bn, PARTS_N + 1)
            v(ve.reciprocal(stat[:, 1, :], stat[:, 1, :]))
            v(tt(stat[:, 1, :], stat[:, 1, :], rowv[:, 2, :], ALU.mult))
            for n, ag, x1 in parts:
                v(tt(ag, ag, wide(stat[:, 1, :]), ALU.mult))
                tt(ag, ag, wide(rowv[:, 3, :]), ALU.add).then_inc(bn_go, 1)
            for n, ag, x1 in parts:
                ve.wait_ge(act_bn, PARTS_N + 1 + n + 1)
                v.go(tt(x1, x1, ag, ALU.add))
            v.join()

            statistics(X, mv, 4)
            reciprocal(4, rstd[:, :])

            def center3(t, b):
                ve.wait_ge(tp3_done, t + 1)
                ts(ring_n[b][:, 0:D], X[:, t, :], mv[:, t, 0:1], rstd[:, ds(t, 1)],
                   ALU.subtract, ALU.mult).then_inc(n3_ready, 1)

            def h_read(t, b):
                ve.wait_ge(h_done, 2 + t + 1)
                cp(HT[:, t, 2 * GH:ROW2], B[2 + b][:, 0:GH * NE]).then_inc(h_out, 1)
            tiles_two_ahead(ve, center3, h_read)
            ve.wait_ge(h_out, 2 + T)
            small_w = lambda i: attn_w[:, i, :].unsqueeze(1).to_broadcast([P, T, GH * NE])
            by_head = lambda a: a.rearrange("p t (h e) -> p t h e", e=NE)
            for i in range(2):
                v(tt(nodes2, HT[:, :, 2 * GH:ROW2], small_w(i), ALU.mult))
                v(red(HT[:, :, GH * i:GH * i + GH], by_head(nodes2), AX.X, ALU.add))
            ve.sem_inc(tab2_ready, 1)
            ve.wait_ge(edge_in, 16)
            v(tt(first_[:, 1:C2], DSTS[:, 1:C2], DSTS[:, 0:C2 - 1], ALU.not_equal))
            v(tt(first_[:, 0:1], DSTS[:, 0:1], dedge[:, 0:1], ALU.not_equal))
            v(ts(goes_on, first_, -1.0, 1.0, ALU.mult, ALU.add))
            v(ve.memset(goes_on[:, 0:1], 1.0))

            v(ts(DG[:, 0, :], ident[:, :], DSTS[:, 0:1], None, ALU.mult))
            ts(DG[:, 1, :], ident[:, :], DSTS[:, C2 - 1:C2], None, ALU.mult).then_inc(carry_go, 1)
            ve.wait_ge(carry_done, 1)
            v(stt(M2, B[6][:, 0:P], DSTS[:, C2 - 1:C2], tri[:, :], ALU.is_equal, ALU.mult))
            v(stt(MADD[0], B[6][:, P:2 * P], DSTS[:, 0:1], low[:, :], ALU.is_equal, ALU.mult))
            v(ts(MADD[0], MADD[0], BIG, BIG, ALU.mult, ALU.subtract))
            v(ts(MADD[1], M2, BIG, BIG, ALU.mult, ALU.subtract))

            bar = K2[:, 0:C2]
            bar_back = K1[:, 0:C2]
            held = K0[:, 0:C2]
            v(ts(bar, goes_on, BIG, BIG, ALU.mult, ALU.subtract))
            v(ve.memset(bar_back[:, C2 - 1:C2], 0.0))
            v(cp(bar_back[:, 0:C2 - 1], bar[:, 1:C2]))
            v(ts(held, first_, -1.0, 1.0, ALU.mult, ALU.add))
            v(scan(held, held, held, 1.0, ALU.mult, ALU.mult))

            with ve.Fori(0, C2 // 16) as i:
                for h in range(2):
                    for s in range(8):
                        ve.wait_ge(slot[8 * h + s], i * 16 + slot2[8 * h + s] + 16)
                    cp(G[:, ds(i * 16 + 8 * h, 8), :].rearrange("p c f -> p (c f)"), ROWS2[h]).then_inc(g_copied, 1)
            ve.wait_ge(g_copied, 2 * (C2 // 16))

            def largest(k, into, src, barrier):
                for h in range(GH):
                    v.go(scan(into(h), barrier, src(h), (-BIG if k is None else small[:, k + h:k + h + 1]), ALU.add, ALU.max))
                v.join()

            def edge_rows(diag, edge):
                for h in range(GH):
                    v.go(ts(diag[:, h, :], ident[:, :], edge[:, h:h + 1], None, ALU.mult))
                v.join()
                ve.sem_inc(carry_go, 1)

            def carried_in(n):
                v(tt(crows, B[6 + n][:, :].rearrange("p (h q) -> p h q", h=GH),
                     MADD[n].unsqueeze(1).to_broadcast([P, GH, P]), ALU.add))
                v(red(small[:, 16 + 4 * n:20 + 4 * n], crows, AX.X, ALU.max))

            v(tt(MB, G[:, :, GH:2 * GH], first_.unsqueeze(2).to_broadcast([P, C2, GH]), ALU.mult))
            for h in range(GH):
                v.go(scan(AD[:, :, h], goes_on, MB[:, :, h], 0.0, ALU.mult, ALU.add))
            v.join()
            v(cp(small[:, 0:GH], AD[:, C2 - 1, :]))
            fwd = (lambda h: MF[:, :, h], lambda h: G[:, :, h], bar)
            back = (lambda h: MB[:, ::-1, h], lambda h: G[:, ::-1, h], bar_back[:, ::-1])
            largest(None, *fwd)
            edge_rows(DG, MF[:, C2 - 1, :])
            largest(None, *back)
            edge_rows(DG2, MB[:, 0, :])
            ve.wait_ge(carry_done, 2)
            v(cp(small[:, 8:8 + GH], B[1][:, 0:GH]))
            for h in range(GH):
                v.go(stt(AD[:, :, h], held, small[:, 8 + h:9 + h], AD[:, :, h], ALU.mult, ALU.add))
            v.join()
            carried_in(0)
            largest(16, *fwd)
            ve.wait_ge(carry_done, 3)
            carried_in(1)
            largest(20, *back)
            v(tt(MF, MF, MB, ALU.max))
            v(tt(MF, MF, AD, ALU.add))
            v(stt(MB, MF, 0.2, MF, ALU.mult, ALU.max))
            v(tt(AD, AD, G[:, :, 0:GH], ALU.add))
            v(stt(MF, AD, 0.2, AD, ALU.mult, ALU.max))
            tt(MF, MF, MB, ALU.subtract).then_inc(esc_go, 1)
            ve.wait_ge(esc_done, 1)
            ee = G[:, :, GH:2 * GH]
            for h in range(GH):
                m = G[:, :, 2 * GH + NE * h:2 * GH + NE * h + NE]
                v.go(tt(m, m, ee[:, :, h:h + 1].to_broadcast([P, C2, NE]), ALU.mult))
            v.join()
            for f in range(SUMS):
                v.go(scan(G[:, :, GH + f], goes_on, G[:, :, GH + f], 0.0, ALU.mult, ALU.add))
            v.join()
            v(cp(small[:, 32:32 + SUMS], G[:, C2 - 1, GH:ROW2]))
            ve.sem_inc(carry_go, 1)
            ve.wait_ge(carry_done, 4)
            v(cp(small[:, 64:64 + SUMS], B[1][:, 32:32 + SUMS]))
            for f in range(SUMS):
                v.go(stt(G[:, :, GH + f], held, small[:, 64 + f:65 + f], G[:, :, GH + f], ALU.mult, ALU.add))
            v.join()
            ve.sem_inc(sums_ready, 1)

            ve.wait_ge(nodes_in, 16 * T)
            den, msg = nodes[:, :, GH:2 * GH], nodes[:, :, 2 * GH:ROW2]
            v(ts(den, den, 1e-16, None, ALU.add))
            v(cp(small[:, 0:T * GH].rearrange("p (t h) -> p t h", t=T), den))
            v(ve.reciprocal(small[:, 0:T * GH], small[:, 0:T * GH]))
            inv = small[:, 0:T * GH].rearrange("p (t h) -> p t h", t=T)
            v(tt(by_head(nodes2), by_head(msg), inv.unsqueeze(3).to_broadcast([P, T, GH, NE]), ALU.mult))
            v(tt(nodes2, nodes2, small_w(2), ALU.add))
            v(red(gstat[:, :, 0], nodes2, AX.X, ALU.add))
            v(ts(gstat[:, :, 0], gstat[:, :, 0], 1.0 / (GH * NE), None, ALU.mult))
            v(tt(nodes2, nodes2, gstat[:, :, 0:1].to_broadcast([P, T, GH * NE]), ALU.subtract))
            v(tt(nodes3, nodes2, nodes2, ALU.mult))
            v(red(gstat[:, :, 1], nodes3, AX.X, ALU.add))
            v(ts(gstat[:, :, 1], gstat[:, :, 1], 1.0 / (GH * NE), None, ALU.mult))
            ve.sem_inc(stats_ready, 1)
            ve.wait_ge(root_ready, 5)
            v(cp(small[:, 128:128 + T], gstat[:, :, 1]))
            v(ve.reciprocal(small[:, 128:128 + T], small[:, 128:128 + T]))
            v(tt(nodes2, nodes2, small[:, 128:128 + T].unsqueeze(2).to_broadcast([P, T, GH * NE]), ALU.mult))
            v(tt(nodes2, nodes2, small_w(3), ALU.mult))
            v(tt(nodes2, nodes2, small_w(4), ALU.add))
            v(red(gates[:, :, :], nodes2.rearrange("p t (h e) -> p t e h", e=NE), AX.X, ALU.add))
            v(ts(gates[:, :, :], gates[:, :, :], 1.0 / GH, None, ALU.mult))
            for e in range(NE):
                me = gates[:, :, e:e + 1]
                if e:
                    v(tt(nodes3[:, :, 0:e], gates[:, :, 0:e], me.to_broadcast([P, T, e]), ALU.is_ge))
                v(ve.memset(nodes3[:, :, e:e + 1], 0.0))
                if e + 1 < NE:
                    v(tt(nodes3[:, :, e + 1:NE], gates[:, :, e + 1:NE], me.to_broadcast([P, T, NE - 1 - e]), ALU.is_gt))
                v(red(nodes3[:, :, 4 + e], nodes3[:, :, 0:NE], AX.X, ALU.add))
            v(ts(nodes3[:, :, 4:8], nodes3[:, :, 4:8], 1.5, None, ALU.is_lt))
            v(red(gstat[:, :, 0], gates[:, :, :], AX.X, ALU.max))
            tt(gates[:, :, :], gates[:, :, :], gstat[:, :, 0:1].to_broadcast([P, T, NE]), ALU.subtract).then_inc(gate_go, 1)
            ve.wait_ge(gate_done, 1)
            v(tt(gates[:, :, :], rank[:, :, :], nodes3[:, :, 4:8], ALU.mult))
            v(red(gstat[:, :, 0], gates[:, :, :], AX.X, ALU.add))
            v(cp(small[:, 0:T], gstat[:, :, 0]))
            v(ve.reciprocal(small[:, 0:T], small[:, 0:T]))
            v(tt(gates[:, :, :], gates[:, :, :], small[:, 0:T].unsqueeze(2).to_broadcast([P, T, NE]), ALU.mult))

            ve.sem_inc(gates_ready, 1)

            for g in range(GROUPS + 1):
                ve.wait_ge(y_in[g], 16 * NE)
                for e in range(2):
                    for j in range(4 if g < GROUPS else 1):
                        t = 4 * g + j
                        v.go(stt(X[:, t, :], Y[g][:, e, j, :], gates[:, t, e:e + 1], X[:, t, :], ALU.mult, ALU.add))
                    v.join()
                ve.wait_ge(gb_done, g + 1)
                for k in range(2 if g < GROUPS else 1):
                    tiles = X[:, 4 * g + 2 * k:min(T, 4 * g + 2 * k + 2), :].rearrange("p t d -> p (t d)")
                    v.go(tt(tiles, tiles, B[2 + 2 * (g % 2) + k][:, 0:(2 * D if g < GROUPS else D)], ALU.add))
                v.join()
                ve.sem_inc(gb_added, 1)
                ve.sem_inc(combined, 1)


def kernel(**inputs):
    import numpy as np
    import concourse.bacc as bacc
    from concourse.bass_utils import run_bass_kernel_spmd

    nc = bacc.Bacc("TRN2", target_bir_lowering=False, num_devices=1)
    arrays, args = {}, {}
    for name in LOADS:
        a = np.ascontiguousarray(inputs[name])
        arrays[f"in_{name}"] = a
        args[name] = nc.dram_tensor(f"in_{name}", a.shape, mybir.dt.from_np(a.dtype), kind="ExternalInput").ap()
    out = nc.dram_tensor("out_0", (N, D), F32, kind="ExternalOutput").ap()
    build(nc, args, out)
    r = run_bass_kernel_spmd(nc, [arrays], core_ids=[0])
    return r.results[0]["out_0"]
```
